# Optimizing a Trainium2 kernel written in Bass

```python
import numpy as np
import jax
import jax.numpy as jnp

def _softmax(x, axis=-1):
    return jax.nn.softmax(x, axis=axis)

def _gelu(x):
    return jax.nn.gelu(x, approximate=True)

def _silu(x):
    return jax.nn.silu(x)

def _sigmoid(x):
    return jax.nn.sigmoid(x)

def _layernorm(x, axis=-1, eps=1e-05):
    m = jnp.mean(x, axis=axis, keepdims=True)
    v = jnp.var(x, axis=axis, keepdims=True)
    return (x - m) / jnp.sqrt(v + eps)

def _scatter_add(tgt, idx, src, axis=0):
    return tgt.at[idx].add(src)

def _segment_sum(src, seg, n):
    return jax.ops.segment_sum(src, seg, n)
kernel_name = 'mk_gps_d1_gnn_r8_2c2934'

def setup_inputs(seed: int=0):
    np.random.seed(seed)
    _w = jnp.asarray

    def _rec_inputs():
        import jax
        import jax.numpy as jnp
        _gk = jax.random.key(seed)
        x = -6.415e-05 + 1 * jax.random.normal(jax.random.fold_in(_gk, 1), (1250, 1024), jnp.float32)
        src = jax.random.randint(jax.random.fold_in(_gk, 2), (40000,), 0, 1250, jnp.int32)
        dst = jax.random.randint(jax.random.fold_in(_gk, 3), (40000,), 0, 1250, jnp.int32)
        _o = jnp.argsort(dst, stable=True)
        src = src[_o]
        dst = dst[_o]
        edge_type_8 = jax.random.randint(jax.random.fold_in(_gk, 12), (40000,), 0, 8, jnp.int32)
        return (x, src, dst, edge_type_8)
    x, src, dst, edge_type_8 = _rec_inputs()

    def _L0_gnn_setup():
        import jax, jax.numpy as jnp
        import numpy as np
        N, D, R, E = (1250, 1024, 8, 10000)

        def _rgcn(x, edge_index, edge_type, weight, root, bias):
            src, dst = (edge_index[0], edge_index[1])
            msgs = x[src]
            out = x @ root + bias
            n = x.shape[0]
            for r in range(weight.shape[0]):
                mask = (edge_type == r).astype(x.dtype)
                sums = jax.ops.segment_sum(msgs * mask[:, None], dst, num_segments=n)
                cnt = jax.ops.segment_sum(mask, dst, num_segments=n)
                mean = sums / jnp.maximum(cnt, 1.0)[:, None]
                out = out + mean @ weight[r]
            return out
        key = jax.random.key(seed)
        ks = jax.random.split(key, 8)
        s = 1.0 / np.sqrt(D)
        x = jax.random.normal(ks[0], (N, D), dtype=jnp.float32)
        edge_index = jax.random.randint(ks[1], (2, E), 0, N, dtype=jnp.int64)
        edge_type = jax.random.randint(ks[2], (E,), 0, R, dtype=jnp.int64)
        weight = jax.random.normal(ks[3], (R, D, D), dtype=jnp.float32) * s
        root = jax.random.normal(ks[4], (D, D), dtype=jnp.float32) * s
        bias = jnp.zeros((D,), dtype=jnp.float32)
        w_gate = jax.random.normal(ks[5], (2 * D, D), dtype=jnp.float32) * (1.0 / np.sqrt(2 * D))
        b_gate = jnp.zeros((D,), dtype=jnp.float32)
        return {'x': x, 'edge_index': edge_index, 'edge_type': edge_type, 'weight': weight, 'root': root, 'bias': bias, 'w_gate': w_gate, 'b_gate': b_gate}
    _L0_gnn_all = _L0_gnn_setup()
    _L0_gnn_in = {k: v for k, v in _L0_gnn_all.items() if k in ('weight', 'root', 'bias', 'w_gate', 'b_gate')}
    del _L0_gnn_all

    def _L0_mix_setup():
        import jax, jax.numpy as jnp
        import numpy as np
        DIM = 1024
        HEADS = 16
        DIM_HEAD = 64
        SCALE = DIM_HEAD ** (-0.5)

        def _split_heads(t):
            b, n, _ = t.shape
            return t.reshape(b, n, HEADS, DIM_HEAD).transpose(0, 2, 1, 3)
        key = jax.random.key(seed)
        ks = jax.random.split(key, 7)
        init = lambda k, shape: jax.random.normal(k, shape, dtype=jnp.float32) * shape[0] ** (-0.5)
        return {'x': jax.random.normal(ks[0], (4, 512, DIM), dtype=jnp.float32), 'Wq': init(ks[1], (DIM, HEADS * DIM_HEAD)), 'Wk': init(ks[2], (DIM, HEADS * DIM_HEAD)), 'Wv': init(ks[3], (DIM, HEADS * DIM_HEAD)), 'Wg': init(ks[4], (DIM, HEADS * DIM_HEAD)), 'bg': jnp.zeros((HEADS * DIM_HEAD,), dtype=jnp.float32), 'Wo': init(ks[5], (HEADS * DIM_HEAD, DIM))}
    _L0_mix_all = _L0_mix_setup()
    _L0_mix_in = {k: v for k, v in _L0_mix_all.items() if k in ('Wq', 'Wk', 'Wv', 'Wg', 'bg', 'Wo')}
    del _L0_mix_all

    def _L0_ffn_setup():
        import jax, jax.numpy as jnp
        import numpy as np
        SEQ, BATCH, D_IN, D_LAT = (512, 64, 1024, 1024)
        key = jax.random.key(seed)
        ks = jax.random.split(key, 5)
        scale = 0.02
        d_cat = D_IN + D_LAT
        return {'x': jax.random.normal(ks[0], (SEQ, BATCH, D_IN), dtype=jnp.float32), 'W_f': jax.random.normal(ks[1], (D_LAT, d_cat), dtype=jnp.float32) * scale, 'b_f': jnp.zeros((D_LAT,), dtype=jnp.float32), 'W_i': jax.random.normal(ks[2], (D_LAT, d_cat), dtype=jnp.float32) * scale, 'b_i': jnp.zeros((D_LAT,), dtype=jnp.float32), 'W_o': jax.random.normal(ks[3], (D_LAT, d_cat), dtype=jnp.float32) * scale, 'b_o': jnp.zeros((D_LAT,), dtype=jnp.float32), 'W_c': jax.random.normal(ks[4], (D_LAT, d_cat), dtype=jnp.float32) * scale, 'b_c': jnp.zeros((D_LAT,), dtype=jnp.float32)}
    _L0_ffn_all = _L0_ffn_setup()
    _L0_ffn_in = {k: v for k, v in _L0_ffn_all.items() if k in ('W_f', 'b_f', 'W_i', 'b_i', 'W_o', 'b_o', 'W_c', 'b_c')}
    del _L0_ffn_all
    return {'x': x, 'src': src, 'dst': dst, 'edge_type_8': edge_type_8, 'L0_gnn_weight': _L0_gnn_in['weight'], 'L0_gnn_root': _L0_gnn_in['root'], 'L0_gnn_bias': _L0_gnn_in['bias'], 'L0_gnn_w_gate': _L0_gnn_in['w_gate'], 'L0_gnn_b_gate': _L0_gnn_in['b_gate'], 'L0_mix_Wq': _L0_mix_in['Wq'], 'L0_mix_Wk': _L0_mix_in['Wk'], 'L0_mix_Wv': _L0_mix_in['Wv'], 'L0_mix_Wg': _L0_mix_in['Wg'], 'L0_mix_bg': _L0_mix_in['bg'], 'L0_mix_Wo': _L0_mix_in['Wo'], 'L0_ffn_W_f': _L0_ffn_in['W_f'], 'L0_ffn_b_f': _L0_ffn_in['b_f'], 'L0_ffn_W_i': _L0_ffn_in['W_i'], 'L0_ffn_b_i': _L0_ffn_in['b_i'], 'L0_ffn_W_o': _L0_ffn_in['W_o'], 'L0_ffn_b_o': _L0_ffn_in['b_o'], 'L0_ffn_W_c': _L0_ffn_in['W_c'], 'L0_ffn_b_c': _L0_ffn_in['b_c']}

def reference(x, src, dst, edge_type_8, L0_gnn_weight, L0_gnn_root, L0_gnn_bias, L0_gnn_w_gate, L0_gnn_b_gate, L0_mix_Wq, L0_mix_Wk, L0_mix_Wv, L0_mix_Wg, L0_mix_bg, L0_mix_Wo, L0_ffn_W_f, L0_ffn_b_f, L0_ffn_W_i, L0_ffn_b_i, L0_ffn_W_o, L0_ffn_b_o, L0_ffn_W_c, L0_ffn_b_c):
    import jax
    import jax.numpy as jnp

    def _L0_gnn_ref(x, edge_index, edge_type, weight, root, bias, w_gate, b_gate):
        import jax, jax.numpy as jnp
        import numpy as np
        N, D, R, E = (1250, 1024, 8, 10000)

        def _rgcn(x, edge_index, edge_type, weight, root, bias):
            src, dst = (edge_index[0], edge_index[1])
            msgs = x[src]
            out = x @ root + bias
            n = x.shape[0]
            for r in range(weight.shape[0]):
                mask = (edge_type == r).astype(x.dtype)
                sums = jax.ops.segment_sum(msgs * mask[:, None], dst, num_segments=n)
                cnt = jax.ops.segment_sum(mask, dst, num_segments=n)
                mean = sums / jnp.maximum(cnt, 1.0)[:, None]
                out = out + mean @ weight[r]
            return out
        u = _rgcn(x, edge_index, edge_type, weight, root, bias)
        z = jnp.concatenate([u, x], axis=1) @ w_gate + b_gate
        h = jnp.tanh(u) * z + x * (1.0 - z)
        return h

    def _L0_mix_ref(x, Wq, Wk, Wv, Wg, bg, Wo):
        import jax, jax.numpy as jnp
        import numpy as np
        DIM = 1024
        HEADS = 16
        DIM_HEAD = 64
        SCALE = DIM_HEAD ** (-0.5)

        def _split_heads(t):
            b, n, _ = t.shape
            return t.reshape(b, n, HEADS, DIM_HEAD).transpose(0, 2, 1, 3)
        q = _split_heads(x @ Wq)
        k = _split_heads(x @ Wk)
        v = _split_heads(x @ Wv)
        g = _split_heads(x @ Wg + bg)
        q = jax.nn.elu(q) + 1.0
        k = jax.nn.elu(k) + 1.0
        g = jax.nn.sigmoid(g)
        kv = jnp.einsum('bhnd,bhne->bhde', k, v)
        k_sum = k.sum(axis=-2)
        z = 1.0 / jnp.clip(jnp.einsum('bhnd,bhd->bhn', q, k_sum), 1e-06)
        out = jnp.einsum('bhnd,bhde->bhne', q * SCALE, kv)
        out = out * z[..., None] * g
        b, h, n, d = out.shape
        out = out.transpose(0, 2, 1, 3).reshape(b, n, h * d)
        return out @ Wo

    def _L0_ffn_ref(x, W_f, b_f, W_i, b_i, W_o, b_o, W_c, b_c):
        import jax, jax.numpy as jnp
        import numpy as np
        SEQ, BATCH, D_IN, D_LAT = (512, 64, 1024, 1024)
        d_lat = W_f.shape[0]
        W_all = jnp.concatenate([W_f, W_i, W_o, W_c], axis=0)
        b_all = jnp.concatenate([b_f, b_i, b_o, b_c], axis=0)
        batch = x.shape[1]
        h0 = jnp.zeros((batch, d_lat), dtype=x.dtype)
        c0 = jnp.zeros((batch, d_lat), dtype=x.dtype)

        def step(carry, x_t):
            h, c = carry
            z = jnp.concatenate([h, x_t], axis=-1)
            gates = z @ W_all.T + b_all
            f_t = jax.nn.sigmoid(gates[:, 0 * d_lat:1 * d_lat])
            i_t = jax.nn.sigmoid(gates[:, 1 * d_lat:2 * d_lat])
            o_t = jax.nn.sigmoid(gates[:, 2 * d_lat:3 * d_lat])
            g_t = jnp.tanh(gates[:, 3 * d_lat:4 * d_lat])
            c_t = f_t * c + i_t * g_t
            h_t = o_t * jnp.tanh(c_t)
            return ((h_t, c_t), h_t)
        _, hidden_states = jax.lax.scan(step, (h0, c0), x)
        return hidden_states
    edge_index = jnp.stack([src, dst])
    xn = _layernorm(x, axis=-1)
    x = x + _L0_gnn_ref(xn, edge_index, edge_type_8, L0_gnn_weight, L0_gnn_root, L0_gnn_bias, L0_gnn_w_gate, L0_gnn_b_gate) + _L0_mix_ref(xn[None], L0_mix_Wq, L0_mix_Wk, L0_mix_Wv, L0_mix_Wg, L0_mix_bg, L0_mix_Wo)[0]
    x = x + _L0_ffn_ref(_layernorm(x, axis=-1)[None], L0_ffn_W_f, L0_ffn_b_f, L0_ffn_W_i, L0_ffn_b_i, L0_ffn_W_o, L0_ffn_b_o, L0_ffn_W_c, L0_ffn_b_c)[0]
    return x

_drawn_inputs = setup_inputs


def setup_inputs(seed=0):
    import zlib

    import numpy as np

    out = dict(_drawn_inputs(seed))
    spreads = {'L0_gnn_bias': (0.0, 0.1),
     'L0_gnn_b_gate': (0.0, 0.1),
     'L0_mix_bg': (0.0, 2.0),
     'L0_ffn_b_f': (0.0, 0.1),
     'L0_ffn_b_i': (0.0, 2.0),
     'L0_ffn_b_o': (0.0, 2.0),
     'L0_ffn_b_c': (0.0, 0.8)}
    factors = {'L0_mix_Wq': 26.677,
     'L0_mix_Wk': 8.0,
     'L0_mix_Wv': 8.0,
     'L0_mix_Wg': 8.0,
     'L0_mix_Wo': 8.0,
     'L0_ffn_W_i': 4.693,
     'L0_ffn_W_o': 4.389}
    for name, (base, spread) in spreads.items():
        noise = np.random.default_rng([zlib.crc32(name.encode()), seed]).standard_normal(out[name].shape)
        drawn = base * np.exp(spread * noise) if base else spread * noise
        out[name] = jnp.asarray(drawn.astype(out[name].dtype))
    for name, factor in factors.items():
        out[name] = (out[name] * factor).astype(out[name].dtype)
    return out
```

```python
from contextlib import ExitStack

import concourse.bass as bass
from concourse import mybir

F32 = mybir.dt.float32
F32R = mybir.dt.float32r
BF16 = mybir.dt.bfloat16
I16 = mybir.dt.int16
I32 = mybir.dt.int32
ALU = mybir.AluOpType
ACT = mybir.ActivationFunctionType
AX = mybir.AxisListType

N = 1250
D = 1024
E = 40000
R = 8
T = 10
P = N // T
K = D // 128
H = 512
HEAD = 64
PAIRS = D // (2 * HEAD)
EC = E // P
B = R * T
CAP = 5
SLOTS = CAP * 128
MAX_ROUNDS = -(-E // SLOTS)
SORTED = E + (MAX_ROUNDS + 1) * SLOTS
KEY = 128
NO_ROW = 4096
LN_EPS = 1e-5
CB = 8
COUNTS = EC // CB

V_, G_, ROOT_, GATEX_, K_, Q_, O_ = range(7)
STAGES_A = 7
STORED = 4
INPUT_, CELL_, OUTPUT_ = range(3)
STAGES_E = 3
CONSTS = 3
KV_COPIES = 4


def up(size):
    return (size + 31) // 32 * 32


class Tally:

    def __init__(self, sem):
        self.sem, self.n = sem, 0

    def inc(self, instruction):
        self.n += 1
        instruction.then_inc(self.sem, 1)

    def dma(self, instruction):
        self.n += 16
        instruction.then_inc(self.sem, 16)

    def wait(self, engine):
        engine.wait_ge(self.sem, self.n)


def build(nc, x, src, dst, edge_type, weight, root, bias, w_gate, b_gate, Wq, Wk, Wv, Wg, bg, Wo,
          W_i, b_i, W_o, b_o, W_c, b_c, out):
    with ExitStack() as ctx:
        def sem(name):
            return ctx.enter_context(nc.semaphore(name))

        def dram(name, shape, dt=F32):
            return nc.dram_tensor(name, shape, dt).ap()

        xn_d = dram("xn_d", [N, D])
        v_d = dram("v_d", [N, D])
        g_d = dram("g_d", [N, D])
        ur_d = dram("ur_d", [N, D])
        zx_d = dram("zx_d", [N, D])
        acc_d = dram("acc_d", [N, D])
        x1_d = dram("x1_d", [N, D])
        gi_d = dram("gi_d", [N, D])
        tc_d = dram("tc_d", [N, D])
        sorted_d = dram("sorted_d", [SORTED, 2], I32)

        def rows(t):
            return slice(t * P, (t + 1) * P)

        top = [up(nc.sbuf_base)]

        def at(offset, name, shape, dt=F32):
            return nc.alloc_sbuf_tensor_at(name, shape, dt, offset=offset)

        def put(name, shape, dt=F32):
            size = {F32: 4, F32R: 4, I32: 4, BF16: 2}[dt]
            for n in shape[1:]:
                size *= n
            a = at(top[0], name, shape, dt)
            top[0] += up(size)
            return a

        ident = put("ident", [128, 128])
        iota = put("iota", [128, P])
        meta = put("meta", [128, B + 8], I32)
        inv = put("inv", [128, B])
        ksum = put("ksum", [128, PAIRS, 2])
        stats = put("stats", [128, 16])
        den = put("den", [128, 16])
        ones2 = put("ones2", [128, 2])
        bias_at = top[0]
        bias_sb = put("bias_sb", [128, D])
        pay_at = top[0]
        pay = put("pay", [128, EC, 2], I32)
        pos = put("pos", [128, EC], I32)
        Whi = put("Whi", [128, K, D], F32R)
        Wlo = put("Wlo", [128, K, D], F32R)
        Wraw = put("Wraw", [128, K, D])
        free = top[0]
        aThi = put("aThi", [128, T, K, P], F32R)
        aTlo = put("aTlo", [128, T, K, P], F32R)
        io_at = top[0]
        io = put("io", [128, 2, D])
        res = put("res", [128, 2, D])
        small_at = top[0]
        kv = at(small_at, "kv", [128, PAIRS, 128])
        qT = at(small_at + 4096, "qT", [128, K, P])
        raw_edges = at(free + (T - 1) * K * P * 4, "raw_edges", [128, 3, EC], I32)
        top[0] = small_at
        bucket = put("bucket", [128, EC])
        node = put("node", [128, EC])
        cum = put("cum", [128, B + 1])
        per = put("per", [128, B])
        off = put("off", [128, B])
        base = put("base", [128, B])
        step_at = top[0]
        onehot_b = put("onehot_b", [128, EC], BF16)
        scan = put("scan", [128, 2, EC])
        sel = at(pay_at + EC * 8, "sel", [128, EC])
        oh_node = at(step_at, "oh_node", [128, CB, P], BF16)
        oh_bucket = at(step_at + up(CB * P * 2), "oh_bucket", [128, CB, B], BF16)
        assert top[0] <= small_at + 8096 and step_at + up(CB * P * 2) + CB * B * 2 <= small_at + 8096
        top[0] = free
        U = put("U", [128, T, D])
        Graw = put("Graw", [128, CAP, D])
        Ghi = put("Ghi", [128, 2, D], F32R)
        Glo = put("Glo", [128, 2, D], F32R)
        mean = put("mean", [128, D])
        mThi = put("mThi", [128, 2, K, P], F32R)
        mTlo = put("mTlo", [128, 2, K, P], F32R)
        OH = put("OH", [128, 2, CAP, P], F32R)
        idx = put("idx", [128, 2, 8], I32)
        assert top[0] <= nc.sbuf_usable_end
        keybase = at(bias_at + B * CAP * 8, "keybase", [128, B])
        pay_all = at(bias_at, "pay_all", [128, B, CAP, 2], I32)
        idx_all = at(pay_at, "idx_all", [128, B + 1, CAP], I32)
        loc_all = at(pay_at + up((B + 1) * CAP * 4), "loc_all", [128, B + 1, CAP])
        assert 2 * up((B + 1) * CAP * 4) <= EC * 12
        c_at = free + T * D * 4
        uThi = at(c_at, "uThi", [128, 2, K, P], F32R)
        uTlo = at(c_at + up(8 * K * P), "uTlo", [128, 2, K, P], F32R)
        ld = at(c_at + 2 * up(8 * K * P), "ld", [128, 2, 3, D])
        th = at(c_at + 2 * up(8 * K * P) + 24 * D, "th", [128, 2, D])
        zb = at(c_at + 2 * up(8 * K * P) + 32 * D, "zb", [128, 2, D])
        x1s = at(small_at, "x1s", [128, 2, D])
        ones = at(io_at, "ones", [128, P])
        before = at(io_at + 512, "before", [128, P])
        place = at(io_at + 1024, "place", [128, 2, EC])
        nobody = at(io_at + 1024 + 8 * EC, "nobody", [128, 2 * (SORTED - E) // 128], I32)

        acc = ctx.enter_context(nc.psum_tensor("acc", [128, 2, 2, H], F32))
        tp = ctx.enter_context(nc.psum_tensor("tp", [128, 2, H], F32))
        aux = ctx.enter_context(nc.psum_tensor("aux", [128, 2, H], F32))
        tpv = tp[:, :, 0:4 * P]

        def as_blocks(a):
            return a.rearrange("p (h b) n -> p h (b n)", h=2)

        w_raw = [sem(f"w_raw{k}") for k in range(K)]
        w_hi, w_lo = sem("w_hi"), sem("w_lo")
        kstep = sem("kstep")
        x_in = [sem(f"x_in{i}") for i in range(2)]
        ln_done, xn_st = sem("ln_done"), [sem(f"xn_st{i}") for i in range(2)]
        turned, at_hi, at_lo = sem("turned"), sem("at_hi"), sem("at_lo")
        bias_in = sem("bias_in")
        evac = sem("evac")
        sig = sem("sig")
        res_st = [sem(f"res_st{i}") for i in range(2)]
        acc_st = [sem(f"acc_st{i}") for i in range(2)]
        neg, expd = sem("neg"), sem("expd")
        kv_done, kv_sb = sem("kv_done"), sem("kv_sb")
        q_turned, q_T, num_done, num_out, o_turned, ot_hi, ot_lo = (
            sem(n) for n in ("q_turned", "q_T", "num_done", "num_out", "o_turned", "ot_hi", "ot_lo"))
        const, edges_in, sent = sem("const"), sem("edges_in"), sem("sent")
        dve_step, pool_step = sem("dve_step"), sem("pool_step")
        passed_dve, passed_pool, passed_sp = sem("passed_dve"), sem("passed_pool"), sem("passed_sp")
        sort_cum, sort_sum, sort_off, pos_done, scattered = (
            sem(n) for n in ("sort_cum", "sort_sum", "sort_off", "pos_done", "scattered"))
        cnt_oh, cnt_mm, inv_done, meta_done = (
            sem(n) for n in ("cnt_oh", "cnt_mm", "inv_done", "meta_done"))
        pay_in, tables, tables_free = sem("pay_in"), sem("tables"), sem("tables_free")
        a_done, u_in = sem("a_done"), sem("u_in")
        idx_ready, oh_ready = sem("idx_ready"), sem("oh_ready")
        raw_in = [sem(f"raw_in{c}") for c in range(CAP)]
        g_zero, g_hi, g_lo, agg = sem("g_zero"), sem("g_hi"), sem("g_lo"), sem("agg")
        mean_out, m_turned, mt_hi, mt_lo, acc_free = (
            sem(n) for n in ("mean_out", "m_turned", "mt_hi", "mt_lo", "acc_free"))
        kv_zero, sort_const, keybase_done, table_step = (
            sem(n) for n in ("kv_zero", "sort_const", "keybase_done", "table_step"))
        b_out = sem("b_out")
        w2_raw = [sem(f"w2_raw{k}") for k in range(K)]
        w2_hi, w2_lo, w2_turned, kstep2 = (sem(n) for n in ("w2_hi", "w2_lo", "w2_turned", "kstep2"))
        u_turned, ut_hi, ut_lo, th_done, c_evac, x1_made = (
            sem(n) for n in ("u_turned", "ut_hi", "ut_lo", "th_done", "c_evac", "x1_made"))
        ld_in = [sem(f"ld_in{i}") for i in range(2)]
        x1_st = [sem(f"x1_st{i}") for i in range(2)]
        e_in = [sem(f"e_in{i}") for i in range(2)]
        e_st = [sem(f"e_st{i}") for i in range(2)]
        x1s_in = [sem(f"x1s_in{i}") for i in range(2)]
        ln2_done, x1_turned, et_hi, et_lo, e_evac, e_act, cell, cell_th, out_made, bias2_in = (
            sem(n) for n in ("ln2_done", "x1_turned", "et_hi", "et_lo", "e_evac", "e_act", "cell", "cell_th",
                             "out_made", "bias2_in"))

        A_TILES = STAGES_A * T
        weights_a = [Wv, Wg, root, w_gate[D:2 * D, :], Wk, Wq, Wo]
        biases_a = {G_: bg, ROOT_: bias, GATEX_: b_gate}
        scratch_a = {V_: v_d, G_: g_d, ROOT_: ur_d, GATEX_: zx_d}

        def io_count(s, t):
            return 16 * ({V_: 0, K_: 1, Q_: 2, O_: 3}[s] * (T // 2) + t // 2 + 1)

        LO_CREDIT, AGG_CREDIT, ACC_CREDIT = CAP, 2, 2

        block = ctx.enter_context(nc.Block())

        @block.sync
        def _(sp):
            def load_w(stage, source):
                for k in range(K):
                    if stage:
                        sp.wait_ge(w_lo, K * (stage - 1) + k + 1)
                    sp.dma_start(Wraw[:, k, :], source[k * 128:(k + 1) * 128, :]).then_inc(w_raw[k], 16)

            io_in = [Tally(x_in[0]), Tally(x_in[1])]
            res_out = [Tally(res_st[0]), Tally(res_st[1])]

            def load_io(t, source):
                io_in[t % 2].dma(sp.dma_start(io[0:P, t % 2, :], source[rows(t), :]))

            def load_bias(source):
                sp.dma_start(bias_sb[0:P, :], source.rearrange("(o n) -> o n", o=1)
                             .to_broadcast([P, D])).then_inc(bias_in, 16)

            def load_payloads(rnd):
                with sp.Fori(0, B) as b:
                    first = sp.value_load(meta[0:1, bass.ds(b, 1)], min_val=0, max_val=E) + rnd * SLOTS
                    sp.dma_start(pay_all[:, bass.ds(b, 1), :, :].rearrange("p o c e -> p (o c e)"),
                                 sorted_d[bass.ds(first, SLOTS), :].rearrange("(p c) e -> p (c e)", p=128)
                                 ).then_inc(pay_in, 16)

            load_io(0, x)
            for i, a in enumerate((src, dst, edge_type)):
                sp.dma_start(raw_edges[0:P, i, :], a.rearrange("(p c) -> p c", p=P)).then_inc(edges_in, 16)
            load_w(0, weights_a[0])
            load_io(1, x)
            for s in range(STAGES_A):
                if s + 1 < STAGES_A:
                    load_w(s + 1, weights_a[s + 1])
                if s in biases_a:
                    if s > G_:
                        sp.wait_ge(evac, s * T)
                    load_bias(biases_a[s])
                if s == K_:
                    for t in range(2):
                        load_io(t, v_d)
                if s == Q_:
                    for t in range(2):
                        sp.wait_ge(kv_done, T - 1 + t)
                        load_io(t, g_d)
                if s == O_:
                    for t in range(2):
                        sp.wait_ge(num_out, T - 1 + t)
                        load_io(t, x)
                    sp.wait_ge(scattered, 16 * EC)
                    sp.wait_ge(evac, STORED * T)
                    sp.wait_ge(meta_done, 2)
                    load_payloads(0)
                for t in range(T):
                    if s == V_:
                        sp.wait_ge(ln_done, t + 1)
                        sp.dma_start(xn_d[rows(t), :], io[0:P, t % 2, :]).then_inc(xn_st[t % 2], 16)
                        if t + 2 < T:
                            sp.wait_ge(xn_st[t % 2], 16 * (t // 2 + 1))
                            sp.wait_ge(turned, t + 1)
                            load_io(t + 2, x)
                    if s < STORED:
                        if s == G_:
                            sp.wait_ge(sig, t + 1)
                        else:
                            sp.wait_ge(evac, s * T + t + 1)
                        res_out[t % 2].dma(sp.dma_start(scratch_a[s][rows(t), :], res[0:P, t % 2, :]))
                    if s == K_ and t >= 1 and t + 1 < T:
                        sp.wait_ge(kv_done, t)
                        load_io(t + 1, v_d)
                    if s == Q_ and t >= 1 and t + 1 < T:
                        sp.wait_ge(num_out, t)
                        load_io(t + 1, g_d)
                    if s == O_ and t >= 1 and t + 1 < T:
                        sp.wait_ge(evac, s * T + t)
                        load_io(t + 1, x)
                if s == STORED - 1:
                    for i in range(2):
                        res_out[i].wait(sp)
                        sp.wait_ge(xn_st[i], 16 * (T // 2))
                    sp.wait_ge(pos_done, 1)
                    sp.wait_ge(sent, 16)

            for k in range(K):
                sp.wait_ge(w_lo, K * (STAGES_A - 1) + k + 1)
            rounds = sp.value_load(meta[0:1, B:B + 1], min_val=1, max_val=MAX_ROUNDS)
            all_w = weight.rearrange("r i o -> (r i) o")
            with sp.Fori(0, rounds) as rnd:
                with sp.Fori(0, R) as r:
                    w0 = (rnd * R + r + STAGES_A - 1) * K + 1
                    for k in range(K):
                        sp.wait_ge(w_lo, w0 + k)
                        sp.dma_start(Wraw[:, k, :], all_w[bass.ds(r * D + k * 128, 128), :]).then_inc(w_raw[k], 16)
                with sp.If(rnd + 1 < rounds):
                    sp.wait_ge(tables, rnd + 1)
                    sp.sem_inc(passed_sp, 1)
                    load_payloads(rnd + 1)

            def load_gate_tile(t):
                for i, a in enumerate((zx_d, xn_d, acc_d)):
                    sp.dma_start(ld[0:P, t % 2, i, :], a[rows(t), :]).then_inc(ld_in[t % 2], 16)

            def load_lstm_w(s, source):
                for m in range(K):
                    if s == 1:
                        sp.wait_ge(w2_lo, m + 1)
                    elif m == 0:
                        sp.wait_ge(w2_turned, K * (s - 1))
                    sp.dma_start(Wraw[:, m, :], source[m * 128:(m + 1) * 128, D:2 * D]).then_inc(w2_raw[m], 16)

            sp.wait_ge(w_lo, (rounds * R + STAGES_A) * K)
            for k in range(K):
                sp.dma_start(Wraw[:, k, :], w_gate[k * 128:(k + 1) * 128, :]).then_inc(w2_raw[k], 16)
            sp.wait_ge(b_out, 1)
            load_gate_tile(0)
            load_gate_tile(1)
            load_lstm_w(1, W_i)
            for t in range(T):
                sp.wait_ge(x1_made, t + 1)
                sp.dma_start(x1_d[rows(t), :], zb[0:P, t % 2, :]).then_inc(x1_st[t % 2], 16)
                if t + 2 < T:
                    load_gate_tile(t + 2)

            def load_e(t, source):
                sp.dma_start(io[0:P, t % 2, :], source[rows(t), :]).then_inc(e_in[t % 2], 16)

            biases_e = (b_i, b_c, b_o)
            sources_e = (x1_d, gi_d, tc_d)
            made_e = (e_act, cell_th, out_made)
            used_e = (x1_turned, cell, out_made)
            for s in range(STAGES_E):
                if s:
                    sp.wait_ge(e_evac, s * T)
                sp.dma_start(bias_sb[0:P, :], biases_e[s].rearrange("(o n) -> o n", o=1)
                             .to_broadcast([P, D])).then_inc(bias2_in, 16)
                for t in range(T):
                    if s == 0 and t == 0:
                        load_e_tiles = (0, 1)
                    elif t == 0:
                        load_e_tiles = (0, 1)
                    elif t + 1 < T and t >= 1:
                        load_e_tiles = (t + 1,)
                    else:
                        load_e_tiles = ()
                    for n in load_e_tiles:
                        if s == 0:
                            sp.wait_ge(x1_st[n % 2], 16 * (n // 2 + 1))
                        else:
                            sp.wait_ge(e_st[n % 2], 16 * ((s - 1) * (T // 2) + n // 2 + 1))
                        if n >= 2:
                            sp.wait_ge(used_e[s], n - 1)
                        elif s:
                            sp.wait_ge(used_e[s - 1], T - 1 + n)
                        load_e(n, sources_e[s])
                        if s == OUTPUT_:
                            sp.dma_start(x1s[0:P, n % 2, :], x1_d[rows(n), :]).then_inc(x1s_in[n % 2], 16)
                    if t == 0 and s + 1 < STAGES_E:
                        load_lstm_w(s + 2, (W_i, W_c, W_o)[s + 1])
                    sp.wait_ge(made_e[s], t + 1)
                    sp.dma_start((gi_d, tc_d, out)[s][rows(t), :], res[0:P, t % 2, :]).then_inc(e_st[t % 2], 16)
            for i in range(2):
                sp.wait_ge(e_st[i], 16 * STAGES_E * (T // 2))
                sp.wait_ge(xn_st[i], 16 * (T // 2))
                sp.wait_ge(x1_st[i], 16 * (T // 2))
                sp.wait_ge(acc_st[i], 16 * (T // 2))


        @block.tensor
        def _(pe):
            def split_product(slot, lhs_hi, lhs_lo, k, signal=kstep):
                first, last = k == 0, k == K - 1
                for a, w, start, stop in ((lhs_hi, Whi, first, False), (lhs_hi, Wlo, False, False),
                                          (lhs_lo, Whi, False, last)):
                    for h in range(2):
                        mm = nc.tensor.matmul(acc[0:P, slot, h, :], a, w[:, k, h * H:(h + 1) * H],
                                              start=start, stop=stop)
                mm.then_inc(signal, 1)

            def turn(source):
                for k in range(K):
                    tr = nc.tensor.transpose(tp[:, k // 4, (k % 4) * P:(k % 4 + 1) * P],
                                             source[:, k * 128:(k + 1) * 128], ident[0:P, 0:P])
                return tr

            def turn_x(t):
                pe.wait_ge(ln_done, t + 1)
                if t:
                    pe.wait_ge(at_lo, t)
                turn(io[0:P, t % 2, :]).then_inc(turned, 1)

            def kv_tile(t):
                pe.wait_ge(evac, K_ * T + t + 1)
                pe.wait_ge(x_in[t % 2], io_count(K_, t))
                if t == 0:
                    pe.wait_ge(inv_done, 2)
                for h in range(PAIRS):
                    cols = slice(h * 128, (h + 1) * 128)
                    nc.tensor.matmul(tp[:, h // 4, (h % 4) * 128:(h % 4 + 1) * 128], res[0:P, t % 2, cols],
                                     io[0:P, t % 2, cols], start=(t == 0 and h % 4 == 0), stop=(t == T - 1),
                                     skip_group_check=True)
                    mm = nc.tensor.matmul(aux[:, 0, 2 * h:2 * h + 2], res[0:P, t % 2, cols], ones2[0:P, :],
                                          start=(t == 0 and h == 0), stop=(t == T - 1), skip_group_check=True)
                mm.then_inc(kv_done, 1)

            def turn_q(t):
                pe.wait_ge(evac, Q_ * T + t + 1)
                if t == 0:
                    pe.wait_ge(kv_sb, KV_COPIES)
                else:
                    pe.wait_ge(ot_lo, t)
                turn(res[0:P, t % 2, :]).then_inc(q_turned, 1)

            def numerator(t):
                pe.wait_ge(q_T, t + 1)
                if t:
                    pe.wait_ge(num_out, t)
                for h in range(PAIRS):
                    nc.tensor.matmul(acc[0:P, t % 2, h // 4, (h % 4) * 128:(h % 4 + 1) * 128], qT[:, h, :],
                                     kv[:, h, :], start=True, stop=True)
                    mm = nc.tensor.matmul(aux[0:P, 1, 2 * h:2 * h + 2], qT[:, h, :], ksum[:, h, :],
                                          start=True, stop=True)
                mm.then_inc(num_done, 1)

            def turn_o(t):
                pe.wait_ge(num_out, t + 1)
                pe.wait_ge(q_T, t + 1)
                turn(res[0:P, t % 2, :]).then_inc(o_turned, 1)

            def sort_sums():
                pe.wait_ge(sort_cum, 1)
                pe.wait_ge(sort_const, 3)
                nc.tensor.matmul(aux[0:P, 1, 0:B], ones[0:P, :], per[0:P, :], start=True, stop=True)
                nc.tensor.matmul(aux[0:P, 1, 128:128 + B], before[0:P, :], per[0:P, :],
                                 start=True, stop=True).then_inc(sort_sum, 1)

            def count_step(n):
                pe.wait_ge(cnt_oh, 2 * (n + 1))
                for j in range(CB):
                    mm = nc.tensor.matmul(aux[0:P, 0, 0:B], oh_node[0:P, j, :], oh_bucket[0:P, j, :],
                                          start=(n == 0 and j == 0), stop=(n == COUNTS - 1 and j == CB - 1))
                mm.then_inc(cnt_mm, 1)

            def beside(s, t, k):
                if s == V_ and t + 1 < T and k == 4:
                    turn_x(t + 1)
                if s == ROOT_ and t == 0 and k == 0:
                    sort_sums()
                if s in (ROOT_, GATEX_) and k % 4 == 3:
                    count_step(((s - ROOT_) * T + t) * 2 + k // 4)
                if s == K_ and t >= 1 and k == 2:
                    kv_tile(t - 1)
                if s == Q_ and t == 0 and k == 2:
                    kv_tile(T - 1)
                n = (s - Q_) * T + t
                if s >= Q_ and 2 <= n < T + 2 and k == 1:
                    turn_o(n - 2)
                if s >= Q_ and 1 <= n < T + 1 and k == 3:
                    turn_q(n - 1)
                if s >= Q_ and 1 <= n < T + 1 and k == 6:
                    numerator(n - 1)

            def tile_a(s, t):
                q = s * T + t
                if s == O_ and t < 2:
                    pe.wait_ge(num_out, T - 1 + t)
                elif s == Q_ and t >= 2:
                    pe.wait_ge(num_out, t - 1)
                elif q >= 2:
                    pe.wait_ge(evac, q - 1)
                if s == V_:
                    pe.wait_ge(at_lo, t + 1)
                if s == O_:
                    pe.wait_ge(ot_lo, t + 1)
                for k in range(K):
                    beside(s, t, k)
                    if t == 0:
                        pe.wait_ge(w_lo, K * s + k + 1)
                    split_product(t % 2, aThi[:, t, k, :], aTlo[:, t, k, :], k)

            pe.wait_ge(const, CONSTS)
            turn_x(0)
            for s in range(STAGES_A):
                for t in range(T):
                    tile_a(s, t)

            def sums(i, rnd, slot):
                pe.wait_ge(oh_ready, i + rnd + 1)
                pe.wait_ge(mean_out, i)
                for c in range(CAP):
                    g = (slot * CAP + c) % 2
                    pe.wait_ge(g_lo, i * CAP + (c + 1 + LO_CREDIT))
                    for part, start, stop in ((Ghi, c == 0, False), (Glo, False, c == CAP - 1)):
                        for h in range(2):
                            mm = nc.tensor.matmul(aux[0:P, h, :], OH[:, slot, c, :],
                                                  part[:, g, h * H:(h + 1) * H], start=start, stop=stop)
                    mm.then_inc(agg, 1)

            def turn_mean(i):
                pe.wait_ge(mean_out, i + 1)
                pe.wait_ge(mt_lo, i)
                turn(mean[0:P, :]).then_inc(m_turned, 1)

            def relation_product(i, slot, k0, k1, weight_count=None):
                if k0 == 0:
                    pe.wait_ge(mt_lo, i + 1)
                    pe.wait_ge(acc_free, i + 1)
                for k in range(k0, k1):
                    pe.wait_ge(w_lo, weight_count + k)
                    split_product(slot, mThi[:, slot, k, :], mTlo[:, slot, k, :], k)

            def bucket_step(rnd, i, slot, weight_count, last=False):
                if not last:
                    sums(i + 1, rnd, 1 - slot)
                relation_product(i, slot, 0, 4, weight_count)
                if not last:
                    turn_mean(i + 1)
                relation_product(i, slot, 4, K, weight_count)

            pe.wait_ge(evac, A_TILES)
            pe.sem_inc(agg, AGG_CREDIT)
            pe.wait_ge(meta_done, 2)
            rounds = pe.value_load(meta[0:1, B:B + 1], min_val=1, max_val=MAX_ROUNDS)
            with pe.Fori(0, rounds) as rnd:
                i0 = rnd * B
                w0 = (rnd * R + STAGES_A) * K + 1
                sums(i0, rnd, 0)
                turn_mean(i0)
                with pe.Fori(0, R - 1) as r:
                    with pe.Fori(0, T // 2) as tt:
                        i = i0 + r * T + tt * 2
                        bucket_step(rnd, i, 0, w0 + r * K)
                        bucket_step(rnd, i + 1, 1, w0 + r * K)
                with pe.Fori(0, T // 2 - 1) as tt:
                    i = i0 + (R - 1) * T + tt * 2
                    bucket_step(rnd, i, 0, w0 + (R - 1) * K)
                    bucket_step(rnd, i + 1, 1, w0 + (R - 1) * K)
                bucket_step(rnd, i0 + B - 2, 0, w0 + (R - 1) * K)
                bucket_step(rnd, i0 + B - 1, 1, w0 + (R - 1) * K, last=True)

            def turn_u(t):
                if t == 0:
                    pe.wait_ge(b_out, 1)
                else:
                    pe.wait_ge(ut_lo, t)
                turn(U[0:P, t, :]).then_inc(u_turned, 1)

            def turn_weight(s, k):
                if k == 0:
                    for m in range(K):
                        pe.wait_ge(w2_raw[m], 16 * (s + 1))
                    if s == 1:
                        pe.wait_ge(ut_lo, T)
                if (s - 1) * K + k:
                    pe.wait_ge(w2_lo, K * s + k)
                for m in range(K):
                    tr = nc.tensor.transpose(aux[:, m // 4, (m % 4) * 128:(m % 4 + 1) * 128],
                                             Wraw[:, m, k * 128:(k + 1) * 128], ident[:, :])
                tr.then_inc(w2_turned, 1)

            turn_u(0)
            for t in range(T):
                pe.wait_ge(ut_lo, t + 1)
                if t >= 2:
                    pe.wait_ge(c_evac, t - 1)
                for k in range(K):
                    if t + 1 < T and k == 4:
                        turn_u(t + 1)
                    if t == 0:
                        pe.wait_ge(w2_lo, k + 1)
                    split_product(t % 2, uThi[:, t % 2, k, :], uTlo[:, t % 2, k, :], k, kstep2)
                    if t == T - 1:
                        turn_weight(1, k)

            def turn_x1(t):
                pe.wait_ge(ln2_done, t + 1)
                if t:
                    pe.wait_ge(et_lo, t)
                turn(io[0:P, t % 2, :]).then_inc(x1_turned, 1)

            turn_x1(0)
            for s in range(STAGES_E):
                for t in range(T):
                    q = s * T + t
                    if q >= 2:
                        pe.wait_ge(e_evac, q - 1)
                    else:
                        pe.wait_ge(c_evac, T - 1 + q)
                    if s == 0:
                        pe.wait_ge(et_lo, t + 1)
                    for k in range(K):
                        if s == 0 and t + 1 < T and k == 4:
                            turn_x1(t + 1)
                        if t == 0:
                            pe.wait_ge(w2_lo, K * (s + 1) + k + 1)
                        split_product(t % 2, aThi[:, t, k, :], aTlo[:, t, k, :], k, kstep2)
                        if t == T - 1 and s + 1 < STAGES_E:
                            turn_weight(s + 2, k)

        @block.scalar
        def _(act):
            def split_w(stage, k, raw_count, free_count, raw=w_raw, free=kstep, done=w_hi):
                act.wait_ge(raw[k], raw_count)
                if free_count is not None:
                    act.wait_ge(free, free_count)
                nc.scalar.copy(Whi[:, k, :], Wraw[:, k, :]).then_inc(done, 1)

            def split_w_a(s):
                for k in range(K):
                    split_w(s, k, 16 * (s + 1), s * T * K - K + k + 1 if s else None)

            def at_tile(t):
                act.wait_ge(turned, t + 1)
                nc.scalar.copy(as_blocks(aThi[:, t, :, :]), tpv).then_inc(at_hi, 1)

            def turned_q(t):
                act.wait_ge(q_turned, t + 1)
                if t:
                    act.wait_ge(num_done, t)
                else:
                    act.wait_ge(kv_sb, KV_COPIES)
                nc.scalar.copy(as_blocks(qT[:, :, :]), tpv).then_inc(q_T, 1)

            def turned_o(t):
                act.wait_ge(o_turned, t + 1)
                nc.scalar.copy(as_blocks(aThi[:, t, :, :]), tpv).then_inc(ot_hi, 1)

            at_tile(0)
            split_w_a(0)
            for s in range(STAGES_A):
                for t in range(T):
                    n = (s - Q_) * T + t
                    if s == V_ and t + 1 < T:
                        at_tile(t + 1)
                    if s >= Q_ and 2 <= n < T + 2:
                        turned_o(n - 2)
                    if s >= Q_ and 1 <= n < T + 1:
                        turned_q(n - 1)
                    if t == T - 1 and s + 1 < STAGES_A:
                        split_w_a(s + 1)
                    if s == G_:
                        act.wait_ge(evac, s * T + t + 1)
                        nc.scalar.activation(res[0:P, t % 2, :], res[0:P, t % 2, :], ACT.Sigmoid).then_inc(sig, 1)
                    if s in (K_, Q_):
                        act.wait_ge(neg, (s - K_) * T + t + 1)
                        nc.scalar.activation(res[0:P, t % 2, :], res[0:P, t % 2, :], ACT.Exp).then_inc(expd, 1)
                    if s == O_:
                        act.wait_ge(evac, s * T + t + 1)
                        act.dma_start(acc_d[rows(t), :], res[0:P, t % 2, :]).then_inc(acc_st[t % 2], 16)

            def hi_part(i, slot, c):
                act.wait_ge(raw_in[c], (i + 1) * 16)
                act.wait_ge(agg, i * CAP + (c + 1))
                nc.scalar.copy(Ghi[:, (slot * CAP + c) % 2, :], Graw[:, c, :]).then_inc(g_hi, 1)

            def means(i, slot, b):
                act.wait_ge(agg, i * CAP + (CAP + AGG_CREDIT))
                act.wait_ge(m_turned, i)
                nc.scalar.activation(mean[0:P, :], aux[0:P, :, :].rearrange("p h n -> p (h n)"), ACT.Copy,
                                     scale=inv[0:P, bass.ds(b, 1)]).then_inc(mean_out, 1)
                act.wait_ge(m_turned, i + 1)
                act.wait_ge(kstep, i * K + (A_TILES - 1) * K)
                nc.scalar.copy(as_blocks(mThi[:, slot, :, :]), tpv).then_inc(mt_hi, 1)

            act.wait_ge(a_done, 1)
            act.dma_start(U[0:P, :, :], ur_d.rearrange("(t p) n -> p t n", p=P)).then_inc(u_in, 16)
            act.wait_ge(inv_done, 2)
            act.wait_ge(meta_done, 2)
            rounds = act.value_load(meta[0:1, B:B + 1], min_val=1, max_val=MAX_ROUNDS)
            with act.Fori(0, rounds) as rnd:
                with act.Fori(0, R) as r:
                    i0 = rnd * B + r * T
                    b0 = r * T
                    stage = rnd * R + r + STAGES_A
                    for c in range(CAP):
                        hi_part(i0, 0, c)
                    means(i0, 0, b0)
                    hi_part(i0 + 1, 1, 0)
                    hi_part(i0 + 1, 1, 1)
                    for k in range(K):
                        split_w(stage, k, (stage + 1) * 16, stage * (T * K) + (k + 1 - K))
                    for c in range(2, CAP):
                        hi_part(i0 + 1, 1, c)
                    means(i0 + 1, 1, b0 + 1)
                    with act.Fori(1, T // 2) as tt:
                        for slot in range(2):
                            for c in range(CAP):
                                hi_part(i0 + tt * 2 + slot, slot, c)
                            means(i0 + tt * 2 + slot, slot, b0 + tt * 2 + slot)

            def u_tile(t):
                act.wait_ge(u_turned, t + 1)
                if t >= 2:
                    act.wait_ge(kstep2, K * (t - 1))
                nc.scalar.copy(as_blocks(uThi[:, t % 2, :, :]), tpv).then_inc(ut_hi, 1)
                if t >= 2:
                    act.wait_ge(x1_made, t - 1)
                nc.scalar.activation(th[0:P, t % 2, :], U[0:P, t, :], ACT.Tanh).then_inc(th_done, 1)

            def split_w_e(s):
                for k in range(K):
                    act.wait_ge(w2_turned, K * (s - 1) + k + 1)
                    act.wait_ge(kstep2, s * T * K - K + k + 1)
                    nc.scalar.copy(Whi[:, k, :], aux[:, :, :].rearrange("p h n -> p (h n)")).then_inc(w2_hi, 1)

            act.wait_ge(b_out, 1)
            u_tile(0)
            for k in range(K):
                split_w(0, k, 16, None, w2_raw, None, w2_hi)
            for t in range(1, T):
                u_tile(t)
            split_w_e(1)

            def x1_tile(t):
                act.wait_ge(x1_turned, t + 1)
                nc.scalar.copy(as_blocks(aThi[:, t, :, :]), tpv).then_inc(et_hi, 1)

            x1_tile(0)
            for s in range(STAGES_E):
                for t in range(T):
                    if s == 0 and t + 1 < T:
                        x1_tile(t + 1)
                    if t == T - 1 and s + 1 < STAGES_E:
                        split_w_e(s + 2)
                    act.wait_ge(e_evac, s * T + t + 1)
                    f = ACT.Tanh if s == CELL_ else ACT.Sigmoid
                    nc.scalar.activation(res[0:P, t % 2, :], res[0:P, t % 2, :], f).then_inc(e_act, 1)
                    if s == CELL_:
                        act.wait_ge(cell, t + 1)
                        nc.scalar.activation(res[0:P, t % 2, :], res[0:P, t % 2, :], ACT.Tanh).then_inc(cell_th, 1)

        @block.vector
        def _(dve):
            step = Tally(dve_step)

            def chain(instruction):
                step.inc(instruction)
                step.wait(dve)

            def split_w(k, count, hi=w_hi, done=w_lo):
                dve.wait_ge(hi, count)
                nc.vector.tensor_tensor(Wlo[:, k, :], Wraw[:, k, :], Whi[:, k, :].bitcast(F32),
                                        ALU.subtract).then_inc(done, 1)

            def inverse_sqrt(v, y, work):
                chain(nc.vector.tensor_scalar(v, v, LN_EPS, None, ALU.add))
                chain(nc.vector.tensor_scalar(y.bitcast(I32), v.bitcast(I32), 1, None, ALU.logical_shift_right))
                chain(nc.vector.tensor_scalar(y.bitcast(I32), y.bitcast(I32), -1.0, float(0x5F3759DF),
                                              ALU.mult, ALU.add))
                for _ in range(4):
                    chain(nc.vector.scalar_tensor_tensor(work, y, v, y, ALU.mult, ALU.mult))
                    chain(nc.vector.tensor_scalar(work, work, -0.5, 1.5, ALU.mult, ALU.add))
                    chain(nc.vector.tensor_tensor(y, y, work, ALU.mult))

            def layer_norm(a):
                for h in range(2):
                    step.inc(nc.vector.bn_stats(stats[0:P, 6 * h:6 * h + 6], a[:, h * H:(h + 1) * H]))
                step.wait(dve)
                chain(nc.vector.bn_aggr(stats[0:P, 12:14], stats[0:P, 0:12]))
                inverse_sqrt(stats[0:P, 13:14], stats[0:P, 14:15], stats[0:P, 0:1])
                return nc.vector.tensor_scalar(a, a, stats[0:P, 12:13], stats[0:P, 14:15],
                                               ALU.subtract, ALU.mult)

            def ln_x(t):
                dve.wait_ge(x_in[t % 2], io_count(V_, t))
                layer_norm(io[0:P, t % 2, :]).then_inc(ln_done, 1)

            def lo_of_turned(out_hi, out_lo, hi, count, done):
                dve.wait_ge(hi, count)
                nc.vector.tensor_tensor(as_blocks(out_lo), tpv, as_blocks(out_hi).bitcast(F32),
                                        ALU.subtract).then_inc(done, 1)

            def edges_prepare():
                dve.wait_ge(edges_in, 48)
                chain(nc.vector.tensor_copy(node[0:P, :], raw_edges[0:P, 1, :]))
                chain(nc.vector.tensor_scalar(bucket[0:P, :], node[0:P, :], float(P), None, ALU.is_ge))
                for k in range(2, T):
                    chain(nc.vector.scalar_tensor_tensor(bucket[0:P, :], node[0:P, :], float(P * k),
                                                         bucket[0:P, :], ALU.is_ge, ALU.add))
                chain(nc.vector.scalar_tensor_tensor(node[0:P, :], bucket[0:P, :], float(-P), node[0:P, :],
                                                     ALU.mult, ALU.add))
                chain(nc.vector.tensor_copy(scan[0:P, 0, :], raw_edges[0:P, 2, :]))
                chain(nc.vector.scalar_tensor_tensor(bucket[0:P, :], scan[0:P, 0, :], float(T), bucket[0:P, :],
                                                     ALU.mult, ALU.add))
                step.inc(nc.vector.tensor_copy(pay[0:P, :, 0], raw_edges[0:P, 0, :]))
                step.inc(nc.vector.scalar_tensor_tensor(pay[0:P, :, 1], bucket[0:P, :], float(KEY),
                                                        node[0:P, :], ALU.mult, ALU.add))
                chain(nc.vector.memset(cum[0:P, 0:1], 0.0))

            def sort_bucket(b):
                chain(nc.vector.tensor_scalar(onehot_b[0:P, :], bucket[0:P, :], float(b), None, ALU.is_equal))
                chain(nc.vector.tensor_tensor_scan(scan[0:P, b % 2, :], onehot_b[0:P, :], onehot_b[0:P, :],
                                                   cum[0:P, b:b + 1], ALU.add, ALU.bypass))
                step.inc(nc.vector.copy_predicated(sel[0:P, :], onehot_b[0:P, :].bitcast(I16), scan[0:P, b % 2, :]))
                chain(nc.vector.tensor_copy(cum[0:P, b + 1:b + 2], scan[0:P, b % 2, EC - 1:EC]))

            def sort_offsets():
                dve.wait_ge(sort_sum, 1)
                total, earlier = aux[0:P, 1, 0:B], aux[0:P, 1, 128:128 + B]
                chain(nc.vector.tensor_tensor_scan(base[0:P, :], total, per[0:P, :], 0.0, ALU.add, ALU.bypass))
                chain(nc.vector.tensor_tensor(base[0:P, :], base[0:P, :], total, ALU.subtract))
                chain(nc.vector.scalar_tensor_tensor(off[0:P, :], earlier, -1.0, base[0:P, :], ALU.add, ALU.add))
                nc.vector.tensor_tensor(off[0:P, :], off[0:P, :], cum[0:P, 0:B], ALU.subtract).then_inc(sort_off, 1)
                nc.vector.tensor_copy(meta[0:P, 0:B], base[0:P, :]).then_inc(meta_done, 1)
                chain(nc.vector.tensor_reduce(stats[0:P, 15:16], total, AX.X, ALU.max))
                chain(nc.vector.tensor_scalar(stats[0:P, 15:16], stats[0:P, 15:16], float(SLOTS - 1),
                                              1.0 / SLOTS, ALU.add, ALU.mult))
                nc.vector.tensor_scalar(meta[0:P, B:B + 1], stats[0:P, 15:16], -0.4995, None,
                                        ALU.add).then_inc(meta_done, 1)

            def count_step(n):
                if n:
                    dve.wait_ge(cnt_mm, n)
                for out_oh, value, width in ((oh_node, node, P), (oh_bucket, bucket, B)):
                    nc.vector.tensor_tensor(
                        out_oh[0:P, :, :], value[0:P, n * CB:(n + 1) * CB].unsqueeze(2).to_broadcast([P, CB, width]),
                        iota[0:P, 0:width].unsqueeze(1).to_broadcast([P, CB, width]), ALU.is_equal).then_inc(cnt_oh, 1)

            def in_degrees():
                dve.wait_ge(cnt_mm, COUNTS)
                nc.vector.tensor_scalar(inv[0:P, :], aux[0:P, 0, 0:B], 1.0, None, ALU.max).then_inc(inv_done, 1)
                dve.wait_ge(inv_done, 1)
                nc.vector.reciprocal(inv[0:P, :], inv[0:P, :]).then_inc(inv_done, 1)

            def product(slot):
                return acc[0:P, slot, :, :].rearrange("p h n -> p (h n)")

            def elu_plus_one(s, t):
                n = (s - K_) * T + t
                dve.wait_ge(kstep, K * (s * T + t + 1))
                nc.vector.tensor_scalar(res[0:P, t % 2, :], product(t % 2), 0.0, None, ALU.min).then_inc(neg, 1)
                dve.wait_ge(expd, n + 1)
                nc.vector.scalar_tensor_tensor(res[0:P, t % 2, :], product(t % 2), 0.0, res[0:P, t % 2, :],
                                               ALU.max, ALU.add).then_inc(evac, 1)

            def kv_to_sbuf():
                dve.wait_ge(kv_done, T)
                both = tp[:, :, :].rearrange("p h (b n) -> p (h b) n", n=128)
                for h in range(2):
                    part, cols = slice(h * HEAD, (h + 1) * HEAD), slice(h * HEAD, (h + 1) * HEAD)
                    nc.vector.tensor_copy(kv[part, :, cols], both[part, :, cols]).then_inc(kv_sb, 1)
                    nc.vector.tensor_copy(ksum[part, :, h], aux[part, 0, h:2 * PAIRS:2]).then_inc(kv_sb, 1)

            def attend(t):
                dve.wait_ge(num_done, t + 1)
                chain(nc.vector.tensor_scalar(den[0:P, :], aux[0:P, 1, 0:2 * PAIRS], 1e-6, None, ALU.max))
                chain(nc.vector.reciprocal(den[0:P, :], den[0:P, :]))
                heads = res[0:P, t % 2, :].rearrange("p (h e) -> p h e", e=HEAD)
                chain(nc.vector.scalar_tensor_tensor(
                    heads, product(t % 2).rearrange("p (h e) -> p h e", e=HEAD), float(HEAD) ** -0.5,
                    den[0:P, :].unsqueeze(2).to_broadcast([P, 2 * PAIRS, HEAD]), ALU.mult, ALU.mult))
                dve.wait_ge(x_in[t % 2], io_count(Q_, t))
                nc.vector.tensor_tensor(res[0:P, t % 2, :], res[0:P, t % 2, :], io[0:P, t % 2, :],
                                        ALU.mult).then_inc(num_out, 1)

            def free_res(s, t):
                q = s * T + t
                if s < STORED:
                    if q >= 2:
                        dve.wait_ge(res_st[t % 2], 16 * (q // 2))
                elif s == K_:
                    if t < 2:
                        dve.wait_ge(res_st[t % 2], 16 * STORED * T // 2)
                    else:
                        dve.wait_ge(kv_done, t - 1)
                elif s == Q_:
                    if t < 2:
                        dve.wait_ge(kv_done, T - 1 + t)
                    else:
                        dve.wait_ge(o_turned, t - 1)
                elif t < 2:
                    dve.wait_ge(o_turned, T - 1 + t)
                else:
                    dve.wait_ge(acc_st[t % 2], 16 * (t // 2))

            def finish_tile(s, t):
                free_res(s, t)
                if s in (K_, Q_):
                    elu_plus_one(s, t)
                    return
                dve.wait_ge(kstep, K * (s * T + t + 1))
                if s == V_:
                    nc.vector.tensor_copy(res[0:P, t % 2, :], product(t % 2)).then_inc(evac, 1)
                elif s == O_:
                    dve.wait_ge(x_in[t % 2], io_count(O_, t))
                    nc.vector.tensor_tensor(res[0:P, t % 2, :], product(t % 2), io[0:P, t % 2, :],
                                            ALU.add).then_inc(evac, 1)
                else:
                    dve.wait_ge(bias_in, 16 * s)
                    nc.vector.tensor_tensor(res[0:P, t % 2, :], product(t % 2), bias_sb[0:P, :],
                                            ALU.add).then_inc(evac, 1)

            ln_x(0)
            lo_of_turned(aThi[:, 0, :, :], aTlo[:, 0, :, :], at_hi, 1, at_lo)
            for k in range(K):
                split_w(k, k + 1)
            for s in range(STAGES_A):
                for t in range(T):
                    n = (s - Q_) * T + t
                    if s == V_ and t + 1 < T:
                        ln_x(t + 1)
                    if s == V_ and t == 0:
                        edges_prepare()
                    if s == V_ and t + 1 < T:
                        lo_of_turned(aThi[:, t + 1, :, :], aTlo[:, t + 1, :, :], at_hi, t + 2, at_lo)
                    if s == V_:
                        for b in range(3 * t, 3 * t + 3):
                            sort_bucket(b)
                    if s == G_:
                        for b in range(3 * T + 5 * t, 3 * T + 5 * t + 5):
                            sort_bucket(b)
                        if t == T - 1:
                            nc.vector.tensor_tensor(per[0:P, :], cum[0:P, 1:B + 1], cum[0:P, 0:B],
                                                    ALU.subtract).then_inc(sort_cum, 1)
                    if (s, t) == (ROOT_, 0):
                        sort_offsets()
                    if s in (ROOT_, GATEX_):
                        for n2 in range(2):
                            count_step(((s - ROOT_) * T + t) * 2 + n2)
                    if (s, t) == (K_, 0):
                        in_degrees()
                        dve.wait_ge(pos_done, 1)
                        nc.vector.memset(kv[:, :, :], 0.0).then_inc(kv_zero, 1)
                        nc.vector.memset(ksum[:, :, :], 0.0).then_inc(kv_zero, 1)
                        dve.wait_ge(kv_zero, 2)
                    if (s, t) == (Q_, 0):
                        kv_to_sbuf()
                    if s >= Q_ and 2 <= n < T + 2:
                        lo_of_turned(aThi[:, n - 2, :, :], aTlo[:, n - 2, :, :], ot_hi, n - 1, ot_lo)
                    if s >= Q_ and 1 <= n < T + 1:
                        attend(n - 1)
                    if t == T - 1 and s + 1 < STAGES_A:
                        for k in range(K):
                            split_w(k, K * (s + 1) + k + 1)
                    finish_tile(s, t)
            dve.wait_ge(acc_st[0], 16 * (T // 2))
            dve.wait_ge(acc_st[1], 16 * (T // 2))
            dve.wait_ge(evac, A_TILES)
            dve.sem_inc(a_done, 1)

            def tables_of_round(rnd):
                dve.wait_ge(pay_in, (rnd + 1) * (16 * B))
                nc.vector.tensor_tensor(
                    loc_all[:, 0:B, :], pay_all[:, :, :, 1], keybase[:, :].unsqueeze(2).to_broadcast([128, B, CAP]),
                    ALU.subtract).then_inc(table_step, 1)
                dve.wait_ge(table_step, rnd * 2 + 1)
                nc.vector.tensor_scalar(idx_all[:, 0:B, :].bitcast(F32), loc_all[:, 0:B, :], KEY - 0.5, float(NO_ROW),
                                        ALU.is_gt, ALU.mult).then_inc(table_step, 1)
                dve.wait_ge(table_step, rnd * 2 + 2)
                nc.vector.tensor_tensor(idx_all[:, 0:B, :], idx_all[:, 0:B, :].bitcast(F32), pay_all[:, :, :, 0],
                                        ALU.add).then_inc(tables, 1)
                dve.wait_ge(tables, rnd + 1)

            def next_bucket(i, rnd, slot, b, first=False):
                if not first:
                    dve.wait_ge(agg, (i - 1) * CAP + AGG_CREDIT)
                    dve.sem_inc(passed_dve, 1)
                nc.vector.tensor_copy(idx[:, slot, 0:CAP].unsqueeze(1),
                                      idx_all[:, bass.ds(b, 1), :]).then_inc(idx_ready, 1)
                nc.vector.tensor_tensor(
                    OH[:, slot, :, :], loc_all[:, bass.ds(b, 1), :].rearrange("p o c -> p (o c)")
                    .unsqueeze(2).to_broadcast([128, CAP, P]),
                    iota[:, :].unsqueeze(1).to_broadcast([128, CAP, P]), ALU.is_equal).then_inc(oh_ready, 1)

            def lo_part(i, slot, c):
                g = (slot * CAP + c) % 2
                dve.wait_ge(g_hi, i * CAP + (c + 1))
                nc.vector.tensor_tensor(Glo[:, g, :], Graw[:, c, :], Ghi[:, g, :].bitcast(F32),
                                        ALU.subtract).then_inc(g_lo, 1)

            def u_add(i, slot, t):
                dve.wait_ge(kstep, i * K + (A_TILES + 1) * K)
                dve.sem_inc(passed_dve, 1)
                dve.wait_ge(acc_free, ACC_CREDIT)
                u = U[0:P, bass.ds(t, 1), :].rearrange("p o n -> p (o n)")
                nc.vector.tensor_tensor(u, product(slot), u, ALU.add).then_inc(acc_free, 1)

            def bucket_work(i, rnd, slot, b, add_tile, weight_count=None):
                next_bucket(i + 1, rnd, 1 - slot, b + 1)
                lo_part(i, slot, 0)
                lo_part(i, slot, 1)
                if weight_count is not None:
                    for k in range(K):
                        split_w(k, weight_count + k)
                if add_tile is not None:
                    u_add(i - 2, slot, add_tile)
                for c in range(2, CAP):
                    lo_part(i, slot, c)
                dve.wait_ge(mt_hi, i + 1)
                nc.vector.tensor_tensor(as_blocks(mTlo[:, slot, :, :]), tpv,
                                        as_blocks(mThi[:, slot, :, :]).bitcast(F32), ALU.subtract).then_inc(mt_lo, 1)

            dve.wait_ge(keybase_done, 1)
            dve.wait_ge(pay_in, 16 * B)
            nc.vector.memset(Graw[:, :, :], 0.0).then_inc(g_zero, 1)
            nc.vector.memset(idx_all[:, B, :], NO_ROW).then_inc(g_zero, 1)
            nc.vector.memset(loc_all[:, B, :], -1.0).then_inc(g_zero, 1)
            tables_of_round(0)
            dve.wait_ge(g_zero, 3)
            dve.sem_inc(g_lo, LO_CREDIT)
            dve.wait_ge(u_in, 16)
            dve.sem_inc(acc_free, ACC_CREDIT)
            dve.wait_ge(meta_done, 2)
            rounds = dve.value_load(meta[0:1, B:B + 1], min_val=1, max_val=MAX_ROUNDS)
            with dve.Fori(0, rounds) as rnd:
                i0 = rnd * B
                w0 = (rnd * R + STAGES_A) * K + 1
                next_bucket(i0, rnd, 0, 0, first=True)
                bucket_work(i0, rnd, 0, 0, None)
                bucket_work(i0 + 1, rnd, 1, 1, None, w0)
                with dve.Fori(1, T // 2) as tt:
                    bucket_work(i0 + tt * 2, rnd, 0, tt * 2, tt * 2 - 2)
                    bucket_work(i0 + tt * 2 + 1, rnd, 1, tt * 2 + 1, tt * 2 - 1)
                with dve.Fori(1, R) as r:
                    bucket_work(i0 + r * T, rnd, 0, r * T, T - 2)
                    bucket_work(i0 + r * T + 1, rnd, 1, r * T + 1, T - 1, w0 + r * K)
                    with dve.Fori(1, T // 2) as tt:
                        bucket_work(i0 + r * T + tt * 2, rnd, 0, r * T + tt * 2, tt * 2 - 2)
                        bucket_work(i0 + r * T + tt * 2 + 1, rnd, 1, r * T + tt * 2 + 1, tt * 2 - 1)
                u_add(i0 + B - 2, 0, T - 2)
                u_add(i0 + B - 1, 1, T - 1)
                with dve.If(rnd + 1 < rounds):
                    tables_of_round(rnd + 1)
                    dve.sem_inc(passed_dve, 1)
            dve.wait_ge(acc_free, rounds * B + ACC_CREDIT)
            dve.sem_inc(b_out, 1)

            def u_lo(t):
                lo_of_turned(uThi[:, t % 2, :, :], uTlo[:, t % 2, :, :], ut_hi, t + 1, ut_lo)

            def gate(t):
                s = t % 2
                dve.wait_ge(kstep2, K * (t + 1))
                dve.wait_ge(ld_in[s], 48 * (t // 2 + 1))
                if t >= 2:
                    dve.wait_ge(x1_st[s], 16 * (t // 2))
                zx, xn, att = (ld[0:P, s, i, :] for i in range(3))
                nc.vector.tensor_tensor(zb[0:P, s, :], product(s), zx, ALU.add).then_inc(c_evac, 1)
                dve.wait_ge(th_done, t + 1)
                chain(nc.vector.tensor_tensor(th[0:P, s, :], th[0:P, s, :], xn, ALU.subtract))
                dve.wait_ge(c_evac, t + 1)
                chain(nc.vector.tensor_tensor(th[0:P, s, :], th[0:P, s, :], zb[0:P, s, :], ALU.mult))
                chain(nc.vector.tensor_tensor(th[0:P, s, :], th[0:P, s, :], xn, ALU.add))
                nc.vector.tensor_tensor(zb[0:P, s, :], th[0:P, s, :], att, ALU.add).then_inc(x1_made, 1)

            def split_w_e(s):
                for k in range(K):
                    dve.wait_ge(w2_hi, K * s + k + 1)
                    nc.vector.tensor_tensor(Wlo[:, k, :], aux[:, :, :].rearrange("p h n -> p (h n)"),
                                            Whi[:, k, :].bitcast(F32), ALU.subtract).then_inc(w2_lo, 1)

            u_lo(0)
            for k in range(K):
                split_w(k, k + 1, w2_hi, w2_lo)
            for t in range(T):
                if t + 1 < T:
                    u_lo(t + 1)
                else:
                    split_w_e(1)
                gate(t)

            def ln_x1(t):
                dve.wait_ge(e_in[t % 2], 16 * (t // 2 + 1))
                layer_norm(io[0:P, t % 2, :]).then_inc(ln2_done, 1)

            def x1_lo(t):
                lo_of_turned(aThi[:, t, :, :], aTlo[:, t, :, :], et_hi, t + 1, et_lo)

            def finish_gate(s, t):
                q, a = s * T + t, res[0:P, t % 2, :]
                if q < 2:
                    dve.wait_ge(x1_st[t], 16 * (T // 2))
                else:
                    dve.wait_ge(e_st[t % 2], 16 * (q // 2))
                dve.wait_ge(bias2_in, 16 * (s + 1))
                dve.wait_ge(kstep2, K * (T + q + 1))
                nc.vector.tensor_tensor(a, product(t % 2), bias_sb[0:P, :], ALU.add).then_inc(e_evac, 1)
                if s == INPUT_:
                    return
                dve.wait_ge(e_act, q + 1)
                dve.wait_ge(e_in[t % 2], 16 * (s * (T // 2) + t // 2 + 1))
                if s == CELL_:
                    nc.vector.tensor_tensor(a, a, io[0:P, t % 2, :], ALU.mult).then_inc(cell, 1)
                else:
                    chain(nc.vector.tensor_tensor(a, a, io[0:P, t % 2, :], ALU.mult))
                    dve.wait_ge(x1s_in[t % 2], 16 * (t // 2 + 1))
                    nc.vector.tensor_tensor(a, a, x1s[0:P, t % 2, :], ALU.add).then_inc(out_made, 1)

            ln_x1(0)
            x1_lo(0)
            for s in range(STAGES_E):
                for t in range(T):
                    if s == 0 and t + 1 < T:
                        ln_x1(t + 1)
                        x1_lo(t + 1)
                    if t == T - 1 and s + 1 < STAGES_E:
                        split_w_e(s + 2)
                    finish_gate(s, t)

        @block.gpsimd
        def _(pool):
            nc.gpsimd.memset(ident[:, :], 0.0).then_inc(pool_step, 1)
            nc.gpsimd.iota(iota[:, :], pattern=[[1, P]], base=0, channel_multiplier=0,
                           allow_small_or_imprecise_dtypes=True).then_inc(const, 1)
            nc.gpsimd.memset(ones2[:, :], 1.0).then_inc(const, 1)
            pool.wait_ge(pool_step, 1)
            nc.gpsimd.affine_select(out=ident[:, :], in_=ident[:, :], pattern=[[-1, 128]], base=0,
                                    channel_multiplier=1, compare_op=ALU.not_equal, fill=1.0).then_inc(const, 1)

            pool.wait_ge(turned, T)
            for i in range(2):
                pool.wait_ge(xn_st[i], 16 * (T // 2))
            nc.gpsimd.memset(ones[:, :], 1.0).then_inc(sort_const, 1)
            nc.gpsimd.memset(before[:, :], 1.0).then_inc(sort_const, 1)
            nc.gpsimd.memset(nobody[:, :], 1 << 20).then_inc(pool_step, 1)
            pool.wait_ge(sort_const, 2)
            nc.gpsimd.affine_select(out=before[:, :], in_=before[:, :], pattern=[[1, P]], base=0,
                                    channel_multiplier=-1, compare_op=ALU.is_gt, fill=0.0).then_inc(sort_const, 1)
            pool.wait_ge(pool_step, 2)
            pool.dma_start(sorted_d[E:SORTED, :].rearrange("(p n) c -> p (n c)", p=128),
                           nobody[:, :]).then_inc(sent, 16)

            pool.wait_ge(sort_off, 1)
            for b in range(B):
                nc.gpsimd.tensor_scalar(place[0:P, b % 2, :], bucket[0:P, :], float(b), off[0:P, b:b + 1],
                                        ALU.is_equal, ALU.mult).then_inc(pool_step, 1)
                pool.wait_ge(pool_step, 2 * b + 3)
                nc.gpsimd.tensor_tensor(sel[0:P, :], sel[0:P, :], place[0:P, b % 2, :],
                                        ALU.add).then_inc(pool_step, 1)
                pool.wait_ge(pool_step, 2 * b + 4)
            nc.gpsimd.tensor_copy(pos[0:P, :], sel[0:P, :]).then_inc(pos_done, 1)
            pool.wait_ge(pos_done, 1)
            for j in range(EC):
                pool.indirect_dma_start(sorted_d, bass.IndirectOffsetOnAxis(ap=pos[0:P, j:j + 1], axis=0),
                                        pay[0:P, j, :], None).then_inc(scattered, 16)
            pool.wait_ge(evac, STORED * T)
            nc.gpsimd.iota(keybase[:, :], pattern=[[KEY, B]], base=0, channel_multiplier=0,
                           allow_small_or_imprecise_dtypes=True).then_inc(keybase_done, 1)

            pool.wait_ge(g_zero, 1)
            pool.wait_ge(meta_done, 2)
            rounds = pool.value_load(meta[0:1, B:B + 1], min_val=1, max_val=MAX_ROUNDS)
            with pool.Fori(0, rounds) as rnd:
                with pool.Fori(0, B // 2) as m:
                    for slot in range(2):
                        i = rnd * B + m * 2 + slot
                        pool.wait_ge(idx_ready, i + rnd + 1)
                        for c in range(CAP):
                            pool.wait_ge(g_lo, i * CAP + (c + 1))
                            pool.sem_inc(passed_pool, 1)
                            pool.indirect_dma_start(
                                Graw[:, c, :], None, xn_d, bass.IndirectOffsetOnAxis(ap=idx[:, slot, c:c + 1], axis=0),
                                bounds_check=N - 1, oob_is_err=False).then_inc(raw_in[c], 16)


def kernel(**inputs):
    import numpy as np
    import concourse.bacc as bacc
    from concourse.bass_utils import run_bass_kernel_spmd

    names = ["x", "src", "dst", "edge_type_8", "L0_gnn_weight", "L0_gnn_root", "L0_gnn_bias", "L0_gnn_w_gate",
             "L0_gnn_b_gate", "L0_mix_Wq", "L0_mix_Wk", "L0_mix_Wv", "L0_mix_Wg", "L0_mix_bg", "L0_mix_Wo",
             "L0_ffn_W_i", "L0_ffn_b_i", "L0_ffn_W_o", "L0_ffn_b_o", "L0_ffn_W_c", "L0_ffn_b_c"]
    nc = bacc.Bacc("TRN2", target_bir_lowering=False, num_devices=1)
    arrays, args = {}, []
    for name in names:
        a = np.ascontiguousarray(inputs[name])
        arrays[f"in_{name}"] = a
        args.append(nc.dram_tensor(f"in_{name}", a.shape, mybir.dt.from_np(a.dtype), kind="ExternalInput").ap())
    args.append(nc.dram_tensor("out_x", [N, D], F32, kind="ExternalOutput").ap())
    build(nc, *args)
    result = run_bass_kernel_spmd(nc, [arrays], core_ids=[0])
    return result.results[0]["out_x"]
```

```python
from contextlib import ExitStack

import concourse.bass as bass
from concourse import mybir

F32 = mybir.dt.float32
F32R = mybir.dt.float32r
BF16 = mybir.dt.bfloat16
I16 = mybir.dt.int16
I32 = mybir.dt.int32
ALU = mybir.AluOpType
ACT = mybir.ActivationFunctionType
AX = mybir.AxisListType

N = 1250
D = 1024
E = 40000
R = 8
T = 10
P = N // T
K = D // 128
H = 512
HEAD = 64
PAIRS = D // (2 * HEAD)
EC = E // P
B = R * T
CAP = 5
SLOTS = CAP * 128
MAX_ROUNDS = -(-E // SLOTS)
SORTED = E + (MAX_ROUNDS + 1) * SLOTS
KEY = 128
NO_ROW = 4096
LN_EPS = 1e-5
CB = 8
COUNTS = EC // CB
PLACES = 10

V_, G_, ROOT_, GATEX_, K_, Q_, O_ = range(7)
STAGES_A = 7
STORED = 4
INPUT_, CELL_, OUTPUT_ = range(3)
STAGES_E = 3
CONSTS = 3
KV_COPIES = 4


def is_first(i):
    return isinstance(i, int) and i == 0


def up(size):
    return (size + 31) // 32 * 32


class Tally:

    def __init__(self, sem):
        self.sem, self.n = sem, 0

    def inc(self, instruction):
        self.n += 1
        instruction.then_inc(self.sem, 1)

    def dma(self, instruction):
        self.n += 16
        instruction.then_inc(self.sem, 16)

    def wait(self, engine):
        engine.wait_ge(self.sem, self.n)


def build(nc, x, src, dst, edge_type, weight, root, bias, w_gate, b_gate, Wq, Wk, Wv, Wg, bg, Wo,
          W_i, b_i, W_o, b_o, W_c, b_c, out):
    with ExitStack() as ctx:
        def sem(name):
            return ctx.enter_context(nc.semaphore(name))

        def dram(name, shape, dt=F32):
            return nc.dram_tensor(name, shape, dt).ap()

        xn_d = dram("xn_d", [N, D])
        v_d = dram("v_d", [N, D])
        g_d = dram("g_d", [N, D])
        ur_d = dram("ur_d", [N, D])
        zx_d = dram("zx_d", [N, D])
        acc_d = dram("acc_d", [N, D])
        x1_d = dram("x1_d", [N, D])
        gi_d = dram("gi_d", [N, D])
        tc_d = dram("tc_d", [N, D])
        sorted_d = dram("sorted_d", [SORTED, 2], I32)

        def rows(t):
            return slice(t * P, (t + 1) * P)

        top = [up(nc.sbuf_base)]

        def at(offset, name, shape, dt=F32):
            return nc.alloc_sbuf_tensor_at(name, shape, dt, offset=offset)

        def put(name, shape, dt=F32):
            size = {F32: 4, F32R: 4, I32: 4, BF16: 2}[dt]
            for n in shape[1:]:
                size *= n
            a = at(top[0], name, shape, dt)
            top[0] += up(size)
            return a

        ident = put("ident", [128, 128])
        iota = put("iota", [128, P])
        meta = put("meta", [128, B + 8], I32)
        inv = put("inv", [128, B])
        ksum = put("ksum", [128, PAIRS, 2])
        stats = put("stats", [128, 16])
        den = put("den", [128, 16])
        ones2 = put("ones2", [128, 2])
        idx = put("idx", [128, 2, 8], I32)
        bias_at = top[0]
        bias_sb = put("bias_sb", [128, D])
        pay_at = top[0]
        pay = put("pay", [128, EC, 2], I32)
        pos = put("pos", [128, EC], I32)
        Whi = put("Whi", [128, K, D], F32R)
        Wlo = put("Wlo", [128, K, D], F32R)
        Wraw = put("Wraw", [128, K, D])
        free = top[0]
        aThi = put("aThi", [128, T, K, P], F32R)
        aTlo = put("aTlo", [128, T, K, P], F32R)
        io_at = top[0]
        io = put("io", [128, 2, D])
        res = put("res", [128, 2, D])
        small_at = top[0]
        kv = at(small_at, "kv", [128, PAIRS, 128])
        qT = at(small_at + 4096, "qT", [128, K, P])
        raw_edges = at(free + (T - 1) * K * P * 4, "raw_edges", [128, 3, EC], I32)
        top[0] = small_at
        bucket = put("bucket", [128, EC])
        node = put("node", [128, EC])
        cum = put("cum", [128, B + 1])
        per = put("per", [128, B])
        off = put("off", [128, B])
        base = put("base", [128, B])
        step_at = top[0]
        onehot_b = put("onehot_b", [128, EC], BF16)
        scan = put("scan", [128, 2, EC])
        sel = at(pay_at + EC * 8, "sel", [128, EC])
        oh_node = at(step_at, "oh_node", [128, CB, P], BF16)
        oh_bucket = at(step_at + up(CB * P * 2), "oh_bucket", [128, CB, B], BF16)
        assert top[0] <= small_at + 8096 and step_at + up(CB * P * 2) + CB * B * 2 <= small_at + 8096
        top[0] = free
        Graw = put("Graw", [128, CAP, D])
        mTlo = put("mTlo", [128, 2, K, P], F32R)
        mean = put("mean", [128, D])
        mThi = put("mThi", [128, 2, K, P], F32R)
        OH = put("OH", [128, 2, CAP, P], F32R)
        Ghi = put("Ghi", [128, 2, D], F32R)
        Glo = put("Glo", [128, 2, D], F32R)
        U = put("U", [128, T, D])
        assert top[0] <= nc.sbuf_usable_end
        keybase = at(bias_at + B * CAP * 8, "keybase", [128, B])
        pay_all = at(bias_at, "pay_all", [128, B, CAP, 2], I32)
        idx_all = at(pay_at, "idx_all", [128, B, CAP], I32)
        loc_all = at(pay_at + up(B * CAP * 4), "loc_all", [128, B, CAP])
        assert 2 * up(B * CAP * 4) <= EC * 12
        c_at = free
        uThi = at(c_at, "uThi", [128, 2, K, P], F32R)
        uTlo = at(c_at + up(8 * K * P), "uTlo", [128, 2, K, P], F32R)
        ld = at(c_at + 2 * up(8 * K * P), "ld", [128, 2, 3, D])
        th = at(c_at + 2 * up(8 * K * P) + 24 * D, "th", [128, 2, D])
        zb = at(c_at + 2 * up(8 * K * P) + 32 * D, "zb", [128, 2, D])
        x1s = at(small_at, "x1s", [128, 2, D])
        ones = at(io_at, "ones", [128, P])
        before = at(io_at + 512, "before", [128, P])
        place = at(io_at + 1024, "place", [128, 2, EC])
        nobody = at(io_at + 1024 + 8 * EC, "nobody", [128, 2 * (SORTED - E) // 128], I32)

        acc = ctx.enter_context(nc.psum_tensor("acc", [128, 2, 2, H], F32))
        tp = ctx.enter_context(nc.psum_tensor("tp", [128, 2, H], F32))
        aux = ctx.enter_context(nc.psum_tensor("aux", [128, 2, H], F32))
        tpv = tp[:, :, 0:4 * P]

        degrees = aux[0:P, 1, 256:256 + B]

        def as_blocks(a):
            return a.rearrange("p (h b) n -> p h (b n)", h=2)

        w_raw = [sem(f"w_raw{k}") for k in range(K)]
        w_hi, w_lo = sem("w_hi"), sem("w_lo")
        kstep = sem("kstep")
        x_in = [sem(f"x_in{i}") for i in range(2)]
        ln_done, xn_st = sem("ln_done"), [sem(f"xn_st{i}") for i in range(2)]
        turned, at_hi, at_lo = sem("turned"), sem("at_hi"), sem("at_lo")
        bias_in = sem("bias_in")
        evac = sem("evac")
        sig = sem("sig")
        res_st = [sem(f"res_st{i}") for i in range(2)]
        acc_st = [sem(f"acc_st{i}") for i in range(2)]
        neg, expd = sem("neg"), sem("expd")
        kv_done, kv_sb = sem("kv_done"), sem("kv_sb")
        q_turned, q_T, num_done, num_out, o_turned, ot_hi, ot_lo = (
            sem(n) for n in ("q_turned", "q_T", "num_done", "num_out", "o_turned", "ot_hi", "ot_lo"))
        const, edges_in, sent = sem("const"), sem("edges_in"), sem("sent")
        dve_step, pool_step = sem("dve_step"), sem("pool_step")
        passed_dve, passed_pool = sem("passed_dve"), sem("passed_pool")
        sort_cum, sort_sum, sort_off, pos_done, scattered = (
            sem(n) for n in ("sort_cum", "sort_sum", "sort_off", "pos_done", "scattered"))
        cnt_oh, cnt_mm, inv_done, meta_done = (
            sem(n) for n in ("cnt_oh", "cnt_mm", "inv_done", "meta_done"))
        pay_in, tables, tables_free = sem("pay_in"), sem("tables"), sem("tables_free")
        a_done, u_in = sem("a_done"), sem("u_in")
        idx_ready, oh_ready = sem("idx_ready"), sem("oh_ready")
        raw_in = [sem(f"raw_in{c}") for c in range(CAP)]
        g_zero, g_hi, g_lo, agg = sem("g_zero"), sem("g_hi"), sem("g_lo"), sem("agg")
        mean_out, m_turned, mt_hi, mt_lo, acc_free = (
            sem(n) for n in ("mean_out", "m_turned", "mt_hi", "mt_lo", "acc_free"))
        kv_zero, sort_const, keybase_done, table_step = (
            sem(n) for n in ("kv_zero", "sort_const", "keybase_done", "table_step"))
        b_out = sem("b_out")
        w2_raw = [sem(f"w2_raw{k}") for k in range(K)]
        w2_hi, w2_lo, w2_turned, kstep2 = (sem(n) for n in ("w2_hi", "w2_lo", "w2_turned", "kstep2"))
        u_turned, ut_hi, ut_lo, th_done, c_evac, x1_made = (
            sem(n) for n in ("u_turned", "ut_hi", "ut_lo", "th_done", "c_evac", "x1_made"))
        ld_in = [sem(f"ld_in{i}") for i in range(2)]
        x1_st = [sem(f"x1_st{i}") for i in range(2)]
        e_in = [sem(f"e_in{i}") for i in range(2)]
        e_st = [sem(f"e_st{i}") for i in range(2)]
        x1s_in = [sem(f"x1s_in{i}") for i in range(2)]
        ln2_done, x1_turned, et_hi, et_lo, e_evac, e_act, cell, cell_th, out_made, bias2_in = (
            sem(n) for n in ("ln2_done", "x1_turned", "et_hi", "et_lo", "e_evac", "e_act", "cell", "cell_th",
                             "out_made", "bias2_in"))

        A_TILES = STAGES_A * T
        weights_a = [Wv, Wg, root, w_gate[D:2 * D, :], Wk, Wq, Wo]
        biases_a = {G_: bg, ROOT_: bias, GATEX_: b_gate}
        scratch_a = {V_: v_d, G_: g_d, ROOT_: ur_d, GATEX_: zx_d}

        def io_count(s, t):
            return 16 * ({V_: 0, K_: 1, Q_: 2, O_: 3}[s] * (T // 2) + t // 2 + 1)

        LO_CREDIT, AGG_CREDIT, ACC_CREDIT = CAP, 2, 2

        block = ctx.enter_context(nc.Block())

        @block.sync
        def _(sp):
            def load_w(stage, source):
                for k in range(K):
                    if stage:
                        sp.wait_ge(w_lo, K * (stage - 1) + k + 1)
                    sp.dma_start(Wraw[:, k, :], source[k * 128:(k + 1) * 128, :]).then_inc(w_raw[k], 16)

            io_in = [Tally(x_in[0]), Tally(x_in[1])]
            res_out = [Tally(res_st[0]), Tally(res_st[1])]

            def load_io(t, source):
                io_in[t % 2].dma(sp.dma_start(io[0:P, t % 2, :], source[rows(t), :]))

            def load_bias(source):
                sp.dma_start(bias_sb[0:P, :], source.rearrange("(o n) -> o n", o=1)
                             .to_broadcast([P, D])).then_inc(bias_in, 16)

            load_io(0, x)
            for i, a in enumerate((src, dst, edge_type)):
                sp.dma_start(raw_edges[0:P, i, :], a.rearrange("(p c) -> p c", p=P)).then_inc(edges_in, 16)
            load_w(0, weights_a[0])
            load_io(1, x)
            for s in range(STAGES_A):
                load_w(s + 1, weights_a[s + 1] if s + 1 < STAGES_A else weight[0])
                if s in biases_a:
                    if s > G_:
                        sp.wait_ge(evac, s * T)
                    load_bias(biases_a[s])
                if s == K_:
                    for t in range(2):
                        load_io(t, v_d)
                if s == Q_:
                    for t in range(2):
                        sp.wait_ge(kv_done, T - 1 + t)
                        load_io(t, g_d)
                if s == O_:
                    for t in range(2):
                        sp.wait_ge(num_out, T - 1 + t)
                        load_io(t, x)
                for t in range(T):
                    if s == V_:
                        sp.wait_ge(ln_done, t + 1)
                        sp.dma_start(xn_d[rows(t), :], io[0:P, t % 2, :]).then_inc(xn_st[t % 2], 16)
                        if t + 2 < T:
                            sp.wait_ge(xn_st[t % 2], 16 * (t // 2 + 1))
                            sp.wait_ge(turned, t + 1)
                            load_io(t + 2, x)
                    if s < STORED:
                        if s == G_:
                            sp.wait_ge(sig, t + 1)
                        else:
                            sp.wait_ge(evac, s * T + t + 1)
                        res_out[t % 2].dma(sp.dma_start(scratch_a[s][rows(t), :], res[0:P, t % 2, :]))
                    if s == K_ and t >= 1 and t + 1 < T:
                        sp.wait_ge(kv_done, t)
                        load_io(t + 1, v_d)
                    if s == Q_ and t >= 1 and t + 1 < T:
                        sp.wait_ge(num_out, t)
                        load_io(t + 1, g_d)
                    if s == O_ and t >= 1 and t + 1 < T:
                        sp.wait_ge(evac, s * T + t)
                        load_io(t + 1, x)
                if s == STORED - 1:
                    for i in range(2):
                        res_out[i].wait(sp)
                        sp.wait_ge(xn_st[i], 16 * (T // 2))
                    sp.wait_ge(pos_done, 1)
                    sp.wait_ge(sent, 16)

            sp.wait_ge(evac, A_TILES)
            sp.wait_ge(kstep, A_TILES * K)
            sp.wait_ge(acc_st[0], 16 * (T // 2))
            sp.wait_ge(acc_st[1], 16 * (T // 2))
            ur = ur_d.rearrange("(t p) n -> p t n", p=P)
            for p in (slice(0, P // 16 * 16), slice(P // 16 * 16, P)):
                sp.dma_start(U[p, :, :], ur[p, :, :]).then_inc(u_in, 16)
            sp.wait_ge(meta_done, 2)
            rounds = sp.value_load(meta[0:1, B:B + 1], min_val=1, max_val=MAX_ROUNDS)
            all_w = weight.rearrange("r i o -> (r i) o")

            def load_relation(r, w0):
                for k in range(K):
                    sp.wait_ge(w_lo, w0 + k)
                    sp.dma_start(Wraw[:, k, :], all_w[bass.ds(r * D + k * 128, 128), :]).then_inc(w_raw[k], 16)

            with sp.Fori(0, rounds) as rnd:
                w0 = (rnd * R + (STAGES_A - 1)) * K + 1
                with sp.Fori(1, R) as r:
                    load_relation(r, w0 + r * K)
                with sp.If(rnd + 1 < rounds):
                    load_relation(0, w0 + R * K)

            def load_gate_tile(t):
                for i, a in enumerate((zx_d, xn_d, acc_d)):
                    sp.dma_start(ld[0:P, t % 2, i, :], a[rows(t), :]).then_inc(ld_in[t % 2], 16)

            def load_lstm_w(s, source):
                for m in range(K):
                    if s == 1:
                        sp.wait_ge(w2_lo, m + 1)
                    elif m == 0:
                        sp.wait_ge(w2_turned, K * (s - 1))
                    sp.dma_start(Wraw[:, m, :], source[m * 128:(m + 1) * 128, D:2 * D]).then_inc(w2_raw[m], 16)

            sp.wait_ge(w_lo, (rounds * R + STAGES_A) * K)
            for k in range(K):
                sp.dma_start(Wraw[:, k, :], w_gate[k * 128:(k + 1) * 128, :]).then_inc(w2_raw[k], 16)
            sp.wait_ge(b_out, 1)
            load_gate_tile(0)
            load_gate_tile(1)
            load_lstm_w(1, W_i)
            for t in range(T):
                sp.wait_ge(x1_made, t + 1)
                sp.dma_start(x1_d[rows(t), :], zb[0:P, t % 2, :]).then_inc(x1_st[t % 2], 16)
                if t + 2 < T:
                    load_gate_tile(t + 2)

            def load_e(t, source):
                sp.dma_start(io[0:P, t % 2, :], source[rows(t), :]).then_inc(e_in[t % 2], 16)

            biases_e = (b_i, b_c, b_o)
            sources_e = (x1_d, gi_d, tc_d)
            made_e = (e_act, cell_th, out_made)
            used_e = (x1_turned, cell, out_made)
            for s in range(STAGES_E):
                if s:
                    sp.wait_ge(e_evac, s * T)
                sp.dma_start(bias_sb[0:P, :], biases_e[s].rearrange("(o n) -> o n", o=1)
                             .to_broadcast([P, D])).then_inc(bias2_in, 16)
                for t in range(T):
                    if s == 0 and t == 0:
                        load_e_tiles = (0, 1)
                    elif t == 0:
                        load_e_tiles = (0, 1)
                    elif t + 1 < T and t >= 1:
                        load_e_tiles = (t + 1,)
                    else:
                        load_e_tiles = ()
                    for n in load_e_tiles:
                        if s == 0:
                            sp.wait_ge(x1_st[n % 2], 16 * (n // 2 + 1))
                        else:
                            sp.wait_ge(e_st[n % 2], 16 * ((s - 1) * (T // 2) + n // 2 + 1))
                        if n >= 2:
                            sp.wait_ge(used_e[s], n - 1)
                        elif s:
                            sp.wait_ge(used_e[s - 1], T - 1 + n)
                        load_e(n, sources_e[s])
                        if s == OUTPUT_:
                            sp.dma_start(x1s[0:P, n % 2, :], x1_d[rows(n), :]).then_inc(x1s_in[n % 2], 16)
                    if t == 0 and s + 1 < STAGES_E:
                        load_lstm_w(s + 2, (W_i, W_c, W_o)[s + 1])
                    sp.wait_ge(made_e[s], t + 1)
                    sp.dma_start((gi_d, tc_d, out)[s][rows(t), :], res[0:P, t % 2, :]).then_inc(e_st[t % 2], 16)
            for i in range(2):
                sp.wait_ge(e_st[i], 16 * STAGES_E * (T // 2))
                sp.wait_ge(xn_st[i], 16 * (T // 2))
                sp.wait_ge(x1_st[i], 16 * (T // 2))
                sp.wait_ge(acc_st[i], 16 * (T // 2))


        @block.tensor
        def _(pe):
            def split_product(slot, lhs_hi, lhs_lo, k, signal=kstep):
                first, last = k == 0, k == K - 1
                for a, w, start, stop in ((lhs_hi, Whi, first, False), (lhs_hi, Wlo, False, False),
                                          (lhs_lo, Whi, False, last)):
                    for h in range(2):
                        mm = nc.tensor.matmul(acc[0:P, slot, h, :], a, w[:, k, h * H:(h + 1) * H],
                                              start=start, stop=stop)
                mm.then_inc(signal, 1)

            def turn(source):
                for k in range(K):
                    tr = nc.tensor.transpose(tp[:, k // 4, (k % 4) * P:(k % 4 + 1) * P],
                                             source[:, k * 128:(k + 1) * 128], ident[0:P, 0:P])
                return tr

            def turn_x(t):
                pe.wait_ge(ln_done, t + 1)
                if t:
                    pe.wait_ge(at_lo, t)
                turn(io[0:P, t % 2, :]).then_inc(turned, 1)

            def kv_tile(t):
                pe.wait_ge(evac, K_ * T + t + 1)
                pe.wait_ge(x_in[t % 2], io_count(K_, t))
                for h in range(PAIRS):
                    cols = slice(h * 128, (h + 1) * 128)
                    nc.tensor.matmul(tp[:, h // 4, (h % 4) * 128:(h % 4 + 1) * 128], res[0:P, t % 2, cols],
                                     io[0:P, t % 2, cols], start=(t == 0 and h % 4 == 0), stop=(t == T - 1),
                                     skip_group_check=True)
                    mm = nc.tensor.matmul(aux[:, 0, 2 * h:2 * h + 2], res[0:P, t % 2, cols], ones2[0:P, :],
                                          start=(t == 0 and h == 0), stop=(t == T - 1), skip_group_check=True)
                mm.then_inc(kv_done, 1)

            def turn_q(t):
                pe.wait_ge(evac, Q_ * T + t + 1)
                if t == 0:
                    pe.wait_ge(kv_sb, KV_COPIES)
                else:
                    pe.wait_ge(ot_lo, t)
                turn(res[0:P, t % 2, :]).then_inc(q_turned, 1)

            def numerator(t):
                pe.wait_ge(q_T, t + 1)
                if t:
                    pe.wait_ge(num_out, t)
                for h in range(PAIRS):
                    nc.tensor.matmul(acc[0:P, t % 2, h // 4, (h % 4) * 128:(h % 4 + 1) * 128], qT[:, h, :],
                                     kv[:, h, :], start=True, stop=True)
                    mm = nc.tensor.matmul(aux[0:P, 1, 2 * h:2 * h + 2], qT[:, h, :], ksum[:, h, :],
                                          start=True, stop=True)
                mm.then_inc(num_done, 1)

            def turn_o(t):
                pe.wait_ge(num_out, t + 1)
                pe.wait_ge(q_T, t + 1)
                turn(res[0:P, t % 2, :]).then_inc(o_turned, 1)

            def sort_sums():
                pe.wait_ge(sort_cum, 1)
                pe.wait_ge(sort_const, 3)
                nc.tensor.matmul(aux[0:P, 1, 0:B], ones[0:P, :], per[0:P, :], start=True, stop=True)
                nc.tensor.matmul(aux[0:P, 1, 128:128 + B], before[0:P, :], per[0:P, :],
                                 start=True, stop=True).then_inc(sort_sum, 1)

            def count_step(n):
                pe.wait_ge(cnt_oh, 2 * (n + 1))
                for j in range(CB):
                    mm = nc.tensor.matmul(degrees, oh_node[0:P, j, :], oh_bucket[0:P, j, :],
                                          start=(n == 0 and j == 0), stop=(n == COUNTS - 1 and j == CB - 1))
                mm.then_inc(cnt_mm, 1)

            def sums(i, slot, blocks):
                for c in blocks:
                    if c == 0:
                        pe.wait_ge(oh_ready, i + 1)
                        if is_first(i):
                            pe.wait_ge(inv_done, 2)
                        else:
                            pe.wait_ge(mean_out, i)
                    g = (slot * CAP + c) % 2
                    pe.wait_ge(g_lo, i * CAP + (c + 1 + LO_CREDIT))
                    for part, start, stop in ((Ghi, c == 0, False), (Glo, False, c == CAP - 1)):
                        for h in range(2):
                            mm = nc.tensor.matmul(aux[0:P, h, :], OH[:, slot, c, :],
                                                  part[:, g, h * H:(h + 1) * H], start=start, stop=stop)
                    mm.then_inc(agg, 1)

            def turn_mean(i):
                pe.wait_ge(mean_out, i + 1)
                if not is_first(i):
                    pe.wait_ge(mt_lo, i)
                turn(mean[0:P, :]).then_inc(m_turned, 1)

            def beside_product(i, slot, k):
                if k % 2 == 0:
                    if k < 6:
                        sums(i, slot, range(k, min(k + 2, CAP)))
                    else:
                        turn_mean(i)

            def beside(s, t, k):
                if s == V_ and t + 1 < T and k == 4:
                    turn_x(t + 1)
                if s == ROOT_ and t == 0 and k == 0:
                    sort_sums()
                if s in (GATEX_, K_) and k in (5, 7):
                    count_step(((s - GATEX_) * T + t) * 2 + (k - 5) // 2)
                if s == K_ and t >= 1 and k == 4:
                    kv_tile(t - 1)
                if s == Q_ and t == 0 and k == 4:
                    kv_tile(T - 1)
                n = (s - Q_) * T + t
                if s >= Q_ and 2 <= n < T + 2 and k == 1:
                    turn_o(n - 2)
                if s >= Q_ and 1 <= n < T + 1 and k == 3:
                    turn_q(n - 1)
                if s >= Q_ and 1 <= n < T + 1 and k == 6:
                    numerator(n - 1)
                if (s, t) == (O_, T - 1):
                    beside_product(0, 0, k)

            def tile_a(s, t):
                q = s * T + t
                if s == O_ and t < 2:
                    pe.wait_ge(num_out, T - 1 + t)
                elif s == Q_ and t >= 2:
                    pe.wait_ge(num_out, t - 1)
                elif q >= 2:
                    pe.wait_ge(evac, q - 1)
                if s == V_:
                    pe.wait_ge(at_lo, t + 1)
                if s == O_:
                    pe.wait_ge(ot_lo, t + 1)
                for k in range(K):
                    beside(s, t, k)
                    if t == 0:
                        pe.wait_ge(w_lo, K * s + k + 1)
                    split_product(t % 2, aThi[:, t, k, :], aTlo[:, t, k, :], k)

            pe.sem_inc(agg, AGG_CREDIT)
            pe.sem_inc(acc_free, ACC_CREDIT)
            pe.wait_ge(const, CONSTS)
            turn_x(0)
            for s in range(STAGES_A):
                for t in range(T):
                    tile_a(s, t)

            def bucket_step(i, slot, weight_count, last=False):
                for k in range(K):
                    if not last:
                        beside_product(i + 1, 1 - slot, k)
                    if k == 0:
                        pe.wait_ge(mt_lo, i + 1)
                        pe.wait_ge(acc_free, i + 1)
                    pe.wait_ge(w_lo, weight_count + k)
                    split_product(slot, mThi[:, slot, k, :], mTlo[:, slot, k, :], k)

            pe.wait_ge(evac, A_TILES)
            pe.wait_ge(meta_done, 2)
            rounds = pe.value_load(meta[0:1, B:B + 1], min_val=1, max_val=MAX_ROUNDS)
            with pe.Fori(0, rounds) as rnd:
                i0 = rnd * B
                w0 = (rnd * R + STAGES_A) * K + 1
                with pe.Fori(0, R - 1) as r:
                    with pe.Fori(0, T // 2) as tt:
                        i = i0 + r * T + tt * 2
                        bucket_step(i, 0, w0 + r * K)
                        bucket_step(i + 1, 1, w0 + r * K)
                with pe.Fori(0, T // 2 - 1) as tt:
                    i = i0 + (R - 1) * T + tt * 2
                    bucket_step(i, 0, w0 + (R - 1) * K)
                    bucket_step(i + 1, 1, w0 + (R - 1) * K)
                bucket_step(i0 + (B - 2), 0, w0 + (R - 1) * K)
                bucket_step(i0 + (B - 1), 1, w0 + (R - 1) * K, last=True)
                with pe.If(rnd + 1 < rounds):
                    sums(i0 + B, 0, range(CAP))
                    turn_mean(i0 + B)

            def turn_u(t):
                if t == 0:
                    pe.wait_ge(b_out, 1)
                else:
                    pe.wait_ge(ut_lo, t)
                turn(U[0:P, t, :]).then_inc(u_turned, 1)

            def turn_weight(s, k):
                if k == 0:
                    for m in range(K):
                        pe.wait_ge(w2_raw[m], 16 * (s + 1))
                    if s == 1:
                        pe.wait_ge(ut_lo, T)
                if (s - 1) * K + k:
                    pe.wait_ge(w2_lo, K * s + k)
                for m in range(K):
                    tr = nc.tensor.transpose(aux[:, m // 4, (m % 4) * 128:(m % 4 + 1) * 128],
                                             Wraw[:, m, k * 128:(k + 1) * 128], ident[:, :])
                tr.then_inc(w2_turned, 1)

            turn_u(0)
            for t in range(T):
                pe.wait_ge(ut_lo, t + 1)
                if t >= 2:
                    pe.wait_ge(c_evac, t - 1)
                for k in range(K):
                    if t + 1 < T and k == 4:
                        turn_u(t + 1)
                    if t == 0:
                        pe.wait_ge(w2_lo, k + 1)
                    split_product(t % 2, uThi[:, t % 2, k, :], uTlo[:, t % 2, k, :], k, kstep2)
                    if t == T - 1:
                        turn_weight(1, k)

            def turn_x1(t):
                pe.wait_ge(ln2_done, t + 1)
                if t:
                    pe.wait_ge(et_lo, t)
                turn(io[0:P, t % 2, :]).then_inc(x1_turned, 1)

            turn_x1(0)
            for s in range(STAGES_E):
                for t in range(T):
                    q = s * T + t
                    if q >= 2:
                        pe.wait_ge(e_evac, q - 1)
                    else:
                        pe.wait_ge(c_evac, T - 1 + q)
                    if s == 0:
                        pe.wait_ge(et_lo, t + 1)
                    for k in range(K):
                        if s == 0 and t + 1 < T and k == 4:
                            turn_x1(t + 1)
                        if t == 0:
                            pe.wait_ge(w2_lo, K * (s + 1) + k + 1)
                        split_product(t % 2, aThi[:, t, k, :], aTlo[:, t, k, :], k, kstep2)
                        if t == T - 1 and s + 1 < STAGES_E:
                            turn_weight(s + 2, k)

        @block.scalar
        def _(act):
            def split_w(stage, k, raw_count, free_count, raw=w_raw, free=kstep, done=w_hi):
                act.wait_ge(raw[k], raw_count)
                if free_count is not None:
                    act.wait_ge(free, free_count)
                nc.scalar.copy(Whi[:, k, :], Wraw[:, k, :]).then_inc(done, 1)

            def split_w_a(s):
                for k in range(K):
                    split_w(s, k, 16 * (s + 1), s * T * K - K + k + 1 if s else None)

            def at_tile(t):
                act.wait_ge(turned, t + 1)
                nc.scalar.copy(as_blocks(aThi[:, t, :, :]), tpv).then_inc(at_hi, 1)

            def turned_q(t):
                act.wait_ge(q_turned, t + 1)
                if t:
                    act.wait_ge(num_done, t)
                else:
                    act.wait_ge(kv_sb, KV_COPIES)
                nc.scalar.copy(as_blocks(qT[:, :, :]), tpv).then_inc(q_T, 1)

            def turned_o(t):
                act.wait_ge(o_turned, t + 1)
                nc.scalar.copy(as_blocks(aThi[:, t, :, :]), tpv).then_inc(ot_hi, 1)

            def hi_part(i, slot, c):
                act.wait_ge(raw_in[c], (i + 1) * 16)
                act.wait_ge(agg, i * CAP + (c + 1))
                nc.scalar.copy(Ghi[:, (slot * CAP + c) % 2, :], Graw[:, c, :]).then_inc(g_hi, 1)

            def means(i, b):
                act.wait_ge(agg, i * CAP + (CAP + AGG_CREDIT))
                if not is_first(i):
                    act.wait_ge(m_turned, i)
                nc.scalar.activation(mean[0:P, :], aux[0:P, :, :].rearrange("p h n -> p (h n)"), ACT.Copy,
                                     scale=inv[0:P, bass.ds(b, 1)]).then_inc(mean_out, 1)

            def turned_means(i, slot):
                act.wait_ge(m_turned, i + 1)
                act.wait_ge(kstep, A_TILES * K if is_first(i) else i * K + (A_TILES - 1) * K)
                nc.scalar.copy(as_blocks(mThi[:, slot, :, :]), tpv).then_inc(mt_hi, 1)

            def split_relation(stage, blocks):
                for k in blocks:
                    split_w(stage, k, (stage + 1) * 16, stage * (T * K) + (k + 1 - K))

            def round_start(i, stage):
                split_relation(stage, range(K))
                for c in range(CAP):
                    hi_part(i, 0, c)
                hi_part(i + 1, 1, 0)
                means(i, 0)
                hi_part(i + 1, 1, 1)
                turned_means(i, 0)

            def bucket_work(i, slot, b, early=None, late=None, left=2):
                if left >= 1:
                    hi_part(i + 1, 1 - slot, 2)
                    hi_part(i + 1, 1 - slot, 3)
                if early:
                    split_relation(early[0], early[1][0:2])
                if left >= 1:
                    hi_part(i + 1, 1 - slot, 4)
                if early:
                    split_relation(early[0], early[1][2:4])
                if left >= 2:
                    hi_part(i + 2, slot, 0)
                if left >= 1:
                    means(i + 1, b + 1)
                if left >= 2:
                    hi_part(i + 2, slot, 1)
                if left >= 1:
                    turned_means(i + 1, 1 - slot)
                if late:
                    split_relation(late[0], late[1])

            def relation_work(i, b, stage, first=False, last=False):
                bucket_work(i, 0, b, None if first else (stage, range(4, K)))
                bucket_work(i + 1, 1, b + 1)
                with act.Fori(1, T // 2 - 1) as tt:
                    bucket_work(i + tt * 2, 0, b + tt * 2)
                    bucket_work(i + tt * 2 + 1, 1, b + tt * 2 + 1)
                bucket_work(i + (T - 2), 0, b + (T - 2), left=1 if last else 2)
                if not last:
                    bucket_work(i + (T - 1), 1, b + (T - 1), late=(stage + 1, range(4)))

            at_tile(0)
            split_w_a(0)
            for s in range(STAGES_A):
                for t in range(T):
                    n = (s - Q_) * T + t
                    if s == V_ and t + 1 < T:
                        at_tile(t + 1)
                    if s >= Q_ and 2 <= n < T + 2:
                        turned_o(n - 2)
                    if s >= Q_ and 1 <= n < T + 1:
                        turned_q(n - 1)
                    if t == T - 1 and s + 1 < STAGES_A:
                        split_w_a(s + 1)
                    if (s, t) == (O_, T - 2):
                        act.wait_ge(kstep, (O_ * T + 6) * K)
                        hi_part(0, 0, 0)
                        hi_part(0, 0, 1)
                    if (s, t) == (O_, T - 1):
                        act.wait_ge(inv_done, 2)
                        hi_part(0, 0, 2)
                        hi_part(0, 0, 3)
                        split_relation(STAGES_A, range(0, 2))
                        hi_part(0, 0, 4)
                        split_relation(STAGES_A, range(2, 4))
                        hi_part(1, 1, 0)
                        means(0, 0)
                        hi_part(1, 1, 1)
                        split_relation(STAGES_A, range(4, 6))
                        turned_means(0, 0)
                        split_relation(STAGES_A, range(6, K))
                    if s == G_:
                        act.wait_ge(evac, s * T + t + 1)
                        nc.scalar.activation(res[0:P, t % 2, :], res[0:P, t % 2, :], ACT.Sigmoid).then_inc(sig, 1)
                    if s in (K_, Q_):
                        act.wait_ge(neg, (s - K_) * T + t + 1)
                        nc.scalar.activation(res[0:P, t % 2, :], res[0:P, t % 2, :], ACT.Exp).then_inc(expd, 1)
                    if s == O_:
                        act.wait_ge(evac, s * T + t + 1)
                        act.dma_start(acc_d[rows(t), :], res[0:P, t % 2, :]).then_inc(acc_st[t % 2], 16)

            act.wait_ge(meta_done, 2)
            rounds = act.value_load(meta[0:1, B:B + 1], min_val=1, max_val=MAX_ROUNDS)
            with act.Fori(0, rounds) as rnd:
                i0 = rnd * B
                stage0 = rnd * R + STAGES_A
                relation_work(i0, 0, stage0, first=True)
                with act.Fori(1, R - 1) as r:
                    relation_work(i0 + r * T, r * T, stage0 + r)
                relation_work(i0 + (R - 1) * T, (R - 1) * T, stage0 + (R - 1), last=True)
                with act.If(rnd + 1 < rounds):
                    round_start(i0 + B, stage0 + R)

            def u_tile(t):
                act.wait_ge(u_turned, t + 1)
                if t >= 2:
                    act.wait_ge(kstep2, K * (t - 1))
                nc.scalar.copy(as_blocks(uThi[:, t % 2, :, :]), tpv).then_inc(ut_hi, 1)
                if t >= 2:
                    act.wait_ge(x1_made, t - 1)
                nc.scalar.activation(th[0:P, t % 2, :], U[0:P, t, :], ACT.Tanh).then_inc(th_done, 1)

            def split_w_e(s):
                for k in range(K):
                    act.wait_ge(w2_turned, K * (s - 1) + k + 1)
                    act.wait_ge(kstep2, s * T * K - K + k + 1)
                    nc.scalar.copy(Whi[:, k, :], aux[:, :, :].rearrange("p h n -> p (h n)")).then_inc(w2_hi, 1)

            act.wait_ge(b_out, 1)
            u_tile(0)
            for k in range(K):
                split_w(0, k, 16, None, w2_raw, None, w2_hi)
            for t in range(1, T):
                u_tile(t)
            split_w_e(1)

            def x1_tile(t):
                act.wait_ge(x1_turned, t + 1)
                nc.scalar.copy(as_blocks(aThi[:, t, :, :]), tpv).then_inc(et_hi, 1)

            x1_tile(0)
            for s in range(STAGES_E):
                for t in range(T):
                    if s == 0 and t + 1 < T:
                        x1_tile(t + 1)
                    if t == T - 1 and s + 1 < STAGES_E:
                        split_w_e(s + 2)
                    act.wait_ge(e_evac, s * T + t + 1)
                    f = ACT.Tanh if s == CELL_ else ACT.Sigmoid
                    nc.scalar.activation(res[0:P, t % 2, :], res[0:P, t % 2, :], f).then_inc(e_act, 1)
                    if s == CELL_:
                        act.wait_ge(cell, t + 1)
                        nc.scalar.activation(res[0:P, t % 2, :], res[0:P, t % 2, :], ACT.Tanh).then_inc(cell_th, 1)

        @block.vector
        def _(dve):
            step = Tally(dve_step)

            def chain(instruction):
                step.inc(instruction)
                step.wait(dve)

            def split_w(k, count, hi=w_hi, done=w_lo):
                dve.wait_ge(hi, count)
                nc.vector.tensor_tensor(Wlo[:, k, :], Wraw[:, k, :], Whi[:, k, :].bitcast(F32),
                                        ALU.subtract).then_inc(done, 1)

            def inverse_sqrt(v, y, work):
                chain(nc.vector.tensor_scalar(v, v, LN_EPS, None, ALU.add))
                chain(nc.vector.tensor_scalar(y.bitcast(I32), v.bitcast(I32), 1, None, ALU.logical_shift_right))
                chain(nc.vector.tensor_scalar(y.bitcast(I32), y.bitcast(I32), -1.0, float(0x5F3759DF),
                                              ALU.mult, ALU.add))
                for _ in range(4):
                    chain(nc.vector.scalar_tensor_tensor(work, y, v, y, ALU.mult, ALU.mult))
                    chain(nc.vector.tensor_scalar(work, work, -0.5, 1.5, ALU.mult, ALU.add))
                    chain(nc.vector.tensor_tensor(y, y, work, ALU.mult))

            def layer_norm(a):
                for h in range(2):
                    step.inc(nc.vector.bn_stats(stats[0:P, 6 * h:6 * h + 6], a[:, h * H:(h + 1) * H]))
                step.wait(dve)
                chain(nc.vector.bn_aggr(stats[0:P, 12:14], stats[0:P, 0:12]))
                inverse_sqrt(stats[0:P, 13:14], stats[0:P, 14:15], stats[0:P, 0:1])
                return nc.vector.tensor_scalar(a, a, stats[0:P, 12:13], stats[0:P, 14:15],
                                               ALU.subtract, ALU.mult)

            def ln_x(t):
                dve.wait_ge(x_in[t % 2], io_count(V_, t))
                layer_norm(io[0:P, t % 2, :]).then_inc(ln_done, 1)

            def lo_of_turned(out_hi, out_lo, hi, count, done):
                dve.wait_ge(hi, count)
                nc.vector.tensor_tensor(as_blocks(out_lo), tpv, as_blocks(out_hi).bitcast(F32),
                                        ALU.subtract).then_inc(done, 1)

            def edges_prepare():
                dve.wait_ge(edges_in, 48)
                chain(nc.vector.tensor_copy(node[0:P, :], raw_edges[0:P, 1, :]))
                chain(nc.vector.tensor_scalar(bucket[0:P, :], node[0:P, :], float(P), None, ALU.is_ge))
                for k in range(2, T):
                    chain(nc.vector.scalar_tensor_tensor(bucket[0:P, :], node[0:P, :], float(P * k),
                                                         bucket[0:P, :], ALU.is_ge, ALU.add))
                chain(nc.vector.scalar_tensor_tensor(node[0:P, :], bucket[0:P, :], float(-P), node[0:P, :],
                                                     ALU.mult, ALU.add))
                chain(nc.vector.tensor_copy(scan[0:P, 0, :], raw_edges[0:P, 2, :]))
                chain(nc.vector.scalar_tensor_tensor(bucket[0:P, :], scan[0:P, 0, :], float(T), bucket[0:P, :],
                                                     ALU.mult, ALU.add))
                step.inc(nc.vector.tensor_copy(pay[0:P, :, 0], raw_edges[0:P, 0, :]))
                step.inc(nc.vector.scalar_tensor_tensor(pay[0:P, :, 1], bucket[0:P, :], float(KEY),
                                                        node[0:P, :], ALU.mult, ALU.add))
                chain(nc.vector.memset(cum[0:P, 0:1], 0.0))

            def sort_bucket(b):
                chain(nc.vector.tensor_scalar(onehot_b[0:P, :], bucket[0:P, :], float(b), None, ALU.is_equal))
                chain(nc.vector.tensor_tensor_scan(scan[0:P, b % 2, :], onehot_b[0:P, :], onehot_b[0:P, :],
                                                   cum[0:P, b:b + 1], ALU.add, ALU.bypass))
                step.inc(nc.vector.copy_predicated(sel[0:P, :], onehot_b[0:P, :].bitcast(I16), scan[0:P, b % 2, :]))
                chain(nc.vector.tensor_copy(cum[0:P, b + 1:b + 2], scan[0:P, b % 2, EC - 1:EC]))

            def sort_offsets():
                dve.wait_ge(sort_sum, 1)
                total, earlier = aux[0:P, 1, 0:B], aux[0:P, 1, 128:128 + B]
                chain(nc.vector.tensor_tensor_scan(base[0:P, :], total, per[0:P, :], 0.0, ALU.add, ALU.bypass))
                chain(nc.vector.tensor_tensor(base[0:P, :], base[0:P, :], total, ALU.subtract))
                chain(nc.vector.scalar_tensor_tensor(off[0:P, :], earlier, -1.0, base[0:P, :], ALU.add, ALU.add))
                nc.vector.tensor_tensor(off[0:P, :], off[0:P, :], cum[0:P, 0:B], ALU.subtract).then_inc(sort_off, 1)
                nc.vector.tensor_copy(meta[0:P, 0:B], base[0:P, :]).then_inc(meta_done, 1)
                chain(nc.vector.tensor_reduce(stats[0:P, 15:16], total, AX.X, ALU.max))
                chain(nc.vector.tensor_scalar(stats[0:P, 15:16], stats[0:P, 15:16], float(SLOTS - 1),
                                              1.0 / SLOTS, ALU.add, ALU.mult))
                nc.vector.tensor_scalar(meta[0:P, B:B + 1], stats[0:P, 15:16], -0.4995, None,
                                        ALU.add).then_inc(meta_done, 1)

            def place_buckets(first, count):
                def offsets(b):
                    return nc.vector.tensor_scalar(place[0:P, b % 2, :], bucket[0:P, :], float(b),
                                                   off[0:P, b:b + 1], ALU.is_equal, ALU.mult)
                chain(offsets(first))
                for b in range(first, first + count):
                    if b + 1 < first + count:
                        step.inc(offsets(b + 1))
                    chain(nc.vector.tensor_tensor(sel[0:P, :], sel[0:P, :], place[0:P, b % 2, :], ALU.add))
                if first + count == B:
                    nc.vector.tensor_copy(pos[0:P, :], sel[0:P, :]).then_inc(pos_done, 1)

            def count_step(n):
                if n:
                    dve.wait_ge(cnt_mm, n)
                for out_oh, value, width in ((oh_node, node, P), (oh_bucket, bucket, B)):
                    nc.vector.tensor_tensor(
                        out_oh[0:P, :, :], value[0:P, n * CB:(n + 1) * CB].unsqueeze(2).to_broadcast([P, CB, width]),
                        iota[0:P, 0:width].unsqueeze(1).to_broadcast([P, CB, width]), ALU.is_equal).then_inc(cnt_oh, 1)

            def in_degrees():
                dve.wait_ge(cnt_mm, COUNTS)
                nc.vector.tensor_scalar(inv[0:P, :], degrees, 1.0, None, ALU.max).then_inc(inv_done, 1)
                dve.wait_ge(inv_done, 1)
                nc.vector.reciprocal(inv[0:P, :], inv[0:P, :]).then_inc(inv_done, 1)

            def product(slot):
                return acc[0:P, slot, :, :].rearrange("p h n -> p (h n)")

            def elu_plus_one(s, t):
                n = (s - K_) * T + t
                dve.wait_ge(kstep, K * (s * T + t + 1))
                nc.vector.tensor_scalar(res[0:P, t % 2, :], product(t % 2), 0.0, None, ALU.min).then_inc(neg, 1)
                dve.wait_ge(expd, n + 1)
                nc.vector.scalar_tensor_tensor(res[0:P, t % 2, :], product(t % 2), 0.0, res[0:P, t % 2, :],
                                               ALU.max, ALU.add).then_inc(evac, 1)

            def kv_to_sbuf():
                dve.wait_ge(kv_done, T)
                both = tp[:, :, :].rearrange("p h (b n) -> p (h b) n", n=128)
                for h in range(2):
                    part, cols = slice(h * HEAD, (h + 1) * HEAD), slice(h * HEAD, (h + 1) * HEAD)
                    nc.vector.tensor_copy(kv[part, :, cols], both[part, :, cols]).then_inc(kv_sb, 1)
                    nc.vector.tensor_copy(ksum[part, :, h], aux[part, 0, h:2 * PAIRS:2]).then_inc(kv_sb, 1)

            def attend(t):
                dve.wait_ge(num_done, t + 1)
                chain(nc.vector.tensor_scalar(den[0:P, :], aux[0:P, 1, 0:2 * PAIRS], 1e-6, None, ALU.max))
                chain(nc.vector.reciprocal(den[0:P, :], den[0:P, :]))
                heads = res[0:P, t % 2, :].rearrange("p (h e) -> p h e", e=HEAD)
                chain(nc.vector.scalar_tensor_tensor(
                    heads, product(t % 2).rearrange("p (h e) -> p h e", e=HEAD), float(HEAD) ** -0.5,
                    den[0:P, :].unsqueeze(2).to_broadcast([P, 2 * PAIRS, HEAD]), ALU.mult, ALU.mult))
                dve.wait_ge(x_in[t % 2], io_count(Q_, t))
                nc.vector.tensor_tensor(res[0:P, t % 2, :], res[0:P, t % 2, :], io[0:P, t % 2, :],
                                        ALU.mult).then_inc(num_out, 1)

            def free_res(s, t):
                q = s * T + t
                if s < STORED:
                    if q >= 2:
                        dve.wait_ge(res_st[t % 2], 16 * (q // 2))
                elif s == K_:
                    if t < 2:
                        dve.wait_ge(res_st[t % 2], 16 * STORED * T // 2)
                    else:
                        dve.wait_ge(kv_done, t - 1)
                elif s == Q_:
                    if t < 2:
                        dve.wait_ge(kv_done, T - 1 + t)
                    else:
                        dve.wait_ge(o_turned, t - 1)
                elif t < 2:
                    dve.wait_ge(o_turned, T - 1 + t)
                else:
                    dve.wait_ge(acc_st[t % 2], 16 * (t // 2))

            def finish_tile(s, t):
                free_res(s, t)
                if s in (K_, Q_):
                    elu_plus_one(s, t)
                    return
                dve.wait_ge(kstep, K * (s * T + t + 1))
                if s == V_:
                    nc.vector.tensor_copy(res[0:P, t % 2, :], product(t % 2)).then_inc(evac, 1)
                elif s == O_:
                    dve.wait_ge(x_in[t % 2], io_count(O_, t))
                    nc.vector.tensor_tensor(res[0:P, t % 2, :], product(t % 2), io[0:P, t % 2, :],
                                            ALU.add).then_inc(evac, 1)
                else:
                    dve.wait_ge(bias_in, 16 * s)
                    nc.vector.tensor_tensor(res[0:P, t % 2, :], product(t % 2), bias_sb[0:P, :],
                                            ALU.add).then_inc(evac, 1)

            def tables_of_round(rnd):
                dve.wait_ge(pay_in, (rnd + 1) * (16 * B))
                nc.vector.tensor_tensor(
                    loc_all[:, :, :], pay_all[:, :, :, 1], keybase[:, :].unsqueeze(2).to_broadcast([128, B, CAP]),
                    ALU.subtract).then_inc(table_step, 1)
                dve.wait_ge(table_step, rnd * 2 + 1)
                nc.vector.tensor_scalar(idx_all[:, :, :].bitcast(F32), loc_all[:, :, :], KEY - 0.5, float(NO_ROW),
                                        ALU.is_gt, ALU.mult).then_inc(table_step, 1)
                dve.wait_ge(table_step, rnd * 2 + 2)
                nc.vector.tensor_tensor(idx_all[:, :, :], idx_all[:, :, :].bitcast(F32), pay_all[:, :, :, 0],
                                        ALU.add).then_inc(tables, 1)
                dve.wait_ge(tables, rnd + 1)

            def edges_of_bucket(i, slot, b, first=False):
                if not first:
                    dve.wait_ge(agg, (i - 1) * CAP + AGG_CREDIT)
                    dve.sem_inc(passed_dve, 1)
                nc.vector.tensor_copy(idx[:, slot, 0:CAP].unsqueeze(1),
                                      idx_all[:, bass.ds(b, 1), :]).then_inc(idx_ready, 1)
                nc.vector.tensor_tensor(
                    OH[:, slot, :, :], loc_all[:, bass.ds(b, 1), :].rearrange("p o c -> p (o c)")
                    .unsqueeze(2).to_broadcast([128, CAP, P]),
                    iota[:, :].unsqueeze(1).to_broadcast([128, CAP, P]), ALU.is_equal).then_inc(oh_ready, 1)

            def lo_part(i, slot, c):
                g = (slot * CAP + c) % 2
                dve.wait_ge(g_hi, i * CAP + (c + 1))
                nc.vector.tensor_tensor(Glo[:, g, :], Graw[:, c, :], Ghi[:, g, :].bitcast(F32),
                                        ALU.subtract).then_inc(g_lo, 1)

            def lo_of_means(i, slot):
                dve.wait_ge(mt_hi, i + 1)
                nc.vector.tensor_tensor(as_blocks(mTlo[:, slot, :, :]), tpv,
                                        as_blocks(mThi[:, slot, :, :]).bitcast(F32), ALU.subtract).then_inc(mt_lo, 1)

            def u_add(i, slot, t):
                dve.wait_ge(kstep, i * K + (A_TILES + 1) * K)
                dve.sem_inc(passed_dve, 1)
                u = U[0:P, bass.ds(t, 1), :].rearrange("p o n -> p (o n)")
                nc.vector.tensor_tensor(u, product(slot), u, ALU.add).then_inc(acc_free, 1)

            def split_relation(stage, blocks):
                for k in blocks:
                    split_w(k, stage * K + (k + 1))

            def round_start(i, stage):
                edges_of_bucket(i, 0, 0, first=True)
                edges_of_bucket(i + 1, 1, 1, first=True)
                split_relation(stage, range(K))
                for c in range(CAP):
                    lo_part(i, 0, c)
                lo_part(i + 1, 1, 0)
                lo_part(i + 1, 1, 1)
                lo_of_means(i, 0)

            def bucket_work(i, slot, b, t, early=None, late=None, left=2):
                if left >= 2:
                    edges_of_bucket(i + 2, slot, b + 2)
                if left >= 1:
                    lo_part(i + 1, 1 - slot, 2)
                    lo_part(i + 1, 1 - slot, 3)
                if early:
                    split_relation(early[0], early[1][0:2])
                if left >= 1:
                    lo_part(i + 1, 1 - slot, 4)
                if early:
                    split_relation(early[0], early[1][2:4])
                if t is not None:
                    u_add(i - 1, 1 - slot, t)
                if left >= 2:
                    lo_part(i + 2, slot, 0)
                    lo_part(i + 2, slot, 1)
                if left >= 1:
                    lo_of_means(i + 1, 1 - slot)
                if late:
                    split_relation(late[0], late[1])

            def relation_work(i, b, stage, first=False, last=False):
                bucket_work(i, 0, b, None if first else T - 1, None if first else (stage, range(4, K)))
                if first:
                    dve.wait_ge(u_in, 32)
                bucket_work(i + 1, 1, b + 1, 0)
                with dve.Fori(1, T // 2 - 1) as tt:
                    bucket_work(i + tt * 2, 0, b + tt * 2, tt * 2 - 1)
                    bucket_work(i + tt * 2 + 1, 1, b + tt * 2 + 1, tt * 2)
                bucket_work(i + (T - 2), 0, b + (T - 2), T - 3, left=1 if last else 2)
                if last:
                    bucket_work(i + (T - 1), 1, b + (T - 1), T - 2, left=0)
                else:
                    bucket_work(i + (T - 1), 1, b + (T - 1), T - 2, late=(stage + 1, range(4)))

            ln_x(0)
            lo_of_turned(aThi[:, 0, :, :], aTlo[:, 0, :, :], at_hi, 1, at_lo)
            for k in range(K):
                split_w(k, k + 1)
            for s in range(STAGES_A):
                for t in range(T):
                    n = (s - Q_) * T + t
                    if s == V_ and t + 1 < T:
                        ln_x(t + 1)
                    if s == V_ and t == 0:
                        edges_prepare()
                    if s == V_ and t + 1 < T:
                        lo_of_turned(aThi[:, t + 1, :, :], aTlo[:, t + 1, :, :], at_hi, t + 2, at_lo)
                    if s == V_:
                        for b in range(3 * t, 3 * t + 3):
                            sort_bucket(b)
                    if s == G_:
                        for b in range(3 * T + 5 * t, 3 * T + 5 * t + 5):
                            sort_bucket(b)
                        if t == T - 1:
                            nc.vector.tensor_tensor(per[0:P, :], cum[0:P, 1:B + 1], cum[0:P, 0:B],
                                                    ALU.subtract).then_inc(sort_cum, 1)
                    if (s, t) == (ROOT_, 0):
                        sort_offsets()
                    if s == ROOT_ and t < B // PLACES:
                        place_buckets(t * PLACES, PLACES)
                    if s in (GATEX_, K_):
                        for n2 in range(2):
                            count_step(((s - GATEX_) * T + t) * 2 + n2)
                    if (s, t) == (Q_, 0):
                        in_degrees()
                        nc.vector.memset(kv[:, :, :], 0.0).then_inc(kv_zero, 1)
                        nc.vector.memset(ksum[:, :, :], 0.0).then_inc(kv_zero, 1)
                        dve.wait_ge(kv_zero, 2)
                        kv_to_sbuf()
                    if (s, t) == (O_, 3):
                        dve.wait_ge(keybase_done, 1)
                        tables_of_round(0)
                    if (s, t) == (O_, T - 3):
                        dve.wait_ge(kstep, (O_ * T + 6) * K)
                        dve.sem_inc(g_lo, LO_CREDIT)
                        edges_of_bucket(0, 0, 0, first=True)
                        edges_of_bucket(1, 1, 1, first=True)
                    if (s, t) == (O_, T - 2):
                        lo_part(0, 0, 0)
                        lo_part(0, 0, 1)
                    if (s, t) == (O_, T - 1):
                        lo_part(0, 0, 2)
                        lo_part(0, 0, 3)
                        split_relation(STAGES_A, range(0, 2))
                        lo_part(0, 0, 4)
                        split_relation(STAGES_A, range(2, 4))
                        lo_part(1, 1, 0)
                        lo_part(1, 1, 1)
                        split_relation(STAGES_A, range(4, 6))
                        lo_of_means(0, 0)
                    if s >= Q_ and 2 <= n < T + 2:
                        lo_of_turned(aThi[:, n - 2, :, :], aTlo[:, n - 2, :, :], ot_hi, n - 1, ot_lo)
                    if s >= Q_ and 1 <= n < T + 1:
                        attend(n - 1)
                    if t == T - 1 and s + 1 < STAGES_A:
                        for k in range(K):
                            split_w(k, K * (s + 1) + k + 1)
                    finish_tile(s, t)
                    if (s, t) == (O_, T - 1):
                        split_relation(STAGES_A, range(6, K))

            dve.wait_ge(meta_done, 2)
            rounds = dve.value_load(meta[0:1, B:B + 1], min_val=1, max_val=MAX_ROUNDS)
            with dve.Fori(0, rounds) as rnd:
                i0 = rnd * B
                stage0 = rnd * R + STAGES_A
                relation_work(i0, 0, stage0, first=True)
                with dve.Fori(1, R - 1) as r:
                    relation_work(i0 + r * T, r * T, stage0 + r)
                relation_work(i0 + (R - 1) * T, (R - 1) * T, stage0 + (R - 1), last=True)
                u_add(i0 + (B - 1), 1, T - 1)
                with dve.If(rnd + 1 < rounds):
                    tables_of_round(rnd + 1)
                    round_start(i0 + B, stage0 + R)
                    dve.sem_inc(passed_dve, 1)
            dve.wait_ge(acc_free, rounds * B + ACC_CREDIT)
            dve.sem_inc(b_out, 1)

            def u_lo(t):
                lo_of_turned(uThi[:, t % 2, :, :], uTlo[:, t % 2, :, :], ut_hi, t + 1, ut_lo)

            def gate(t):
                s = t % 2
                dve.wait_ge(kstep2, K * (t + 1))
                dve.wait_ge(ld_in[s], 48 * (t // 2 + 1))
                if t >= 2:
                    dve.wait_ge(x1_st[s], 16 * (t // 2))
                zx, xn, att = (ld[0:P, s, i, :] for i in range(3))
                nc.vector.tensor_tensor(zb[0:P, s, :], product(s), zx, ALU.add).then_inc(c_evac, 1)
                dve.wait_ge(th_done, t + 1)
                chain(nc.vector.tensor_tensor(th[0:P, s, :], th[0:P, s, :], xn, ALU.subtract))
                dve.wait_ge(c_evac, t + 1)
                chain(nc.vector.tensor_tensor(th[0:P, s, :], th[0:P, s, :], zb[0:P, s, :], ALU.mult))
                chain(nc.vector.tensor_tensor(th[0:P, s, :], th[0:P, s, :], xn, ALU.add))
                nc.vector.tensor_tensor(zb[0:P, s, :], th[0:P, s, :], att, ALU.add).then_inc(x1_made, 1)

            def split_w_e(s):
                for k in range(K):
                    dve.wait_ge(w2_hi, K * s + k + 1)
                    nc.vector.tensor_tensor(Wlo[:, k, :], aux[:, :, :].rearrange("p h n -> p (h n)"),
                                            Whi[:, k, :].bitcast(F32), ALU.subtract).then_inc(w2_lo, 1)

            u_lo(0)
            for k in range(K):
                split_w(k, k + 1, w2_hi, w2_lo)
            for t in range(T):
                if t + 1 < T:
                    u_lo(t + 1)
                else:
                    split_w_e(1)
                gate(t)

            def ln_x1(t):
                dve.wait_ge(e_in[t % 2], 16 * (t // 2 + 1))
                layer_norm(io[0:P, t % 2, :]).then_inc(ln2_done, 1)

            def x1_lo(t):
                lo_of_turned(aThi[:, t, :, :], aTlo[:, t, :, :], et_hi, t + 1, et_lo)

            def finish_gate(s, t):
                q, a = s * T + t, res[0:P, t % 2, :]
                if q < 2:
                    dve.wait_ge(x1_st[t], 16 * (T // 2))
                else:
                    dve.wait_ge(e_st[t % 2], 16 * (q // 2))
                dve.wait_ge(bias2_in, 16 * (s + 1))
                dve.wait_ge(kstep2, K * (T + q + 1))
                nc.vector.tensor_tensor(a, product(t % 2), bias_sb[0:P, :], ALU.add).then_inc(e_evac, 1)
                if s == INPUT_:
                    return
                dve.wait_ge(e_act, q + 1)
                dve.wait_ge(e_in[t % 2], 16 * (s * (T // 2) + t // 2 + 1))
                if s == CELL_:
                    nc.vector.tensor_tensor(a, a, io[0:P, t % 2, :], ALU.mult).then_inc(cell, 1)
                else:
                    chain(nc.vector.tensor_tensor(a, a, io[0:P, t % 2, :], ALU.mult))
                    dve.wait_ge(x1s_in[t % 2], 16 * (t // 2 + 1))
                    nc.vector.tensor_tensor(a, a, x1s[0:P, t % 2, :], ALU.add).then_inc(out_made, 1)

            ln_x1(0)
            x1_lo(0)
            for s in range(STAGES_E):
                for t in range(T):
                    if s == 0 and t + 1 < T:
                        ln_x1(t + 1)
                        x1_lo(t + 1)
                    if t == T - 1 and s + 1 < STAGES_E:
                        split_w_e(s + 2)
                    finish_gate(s, t)

        @block.gpsimd
        def _(pool):
            nc.gpsimd.memset(ident[:, :], 0.0).then_inc(pool_step, 1)
            nc.gpsimd.iota(iota[:, :], pattern=[[1, P]], base=0, channel_multiplier=0,
                           allow_small_or_imprecise_dtypes=True).then_inc(const, 1)
            nc.gpsimd.memset(ones2[:, :], 1.0).then_inc(const, 1)
            pool.wait_ge(pool_step, 1)
            nc.gpsimd.affine_select(out=ident[:, :], in_=ident[:, :], pattern=[[-1, 128]], base=0,
                                    channel_multiplier=1, compare_op=ALU.not_equal, fill=1.0).then_inc(const, 1)

            pool.wait_ge(turned, T)
            for i in range(2):
                pool.wait_ge(xn_st[i], 16 * (T // 2))
            nc.gpsimd.memset(ones[:, :], 1.0).then_inc(sort_const, 1)
            nc.gpsimd.memset(before[:, :], 1.0).then_inc(sort_const, 1)
            nc.gpsimd.memset(nobody[:, :], 1 << 20).then_inc(pool_step, 1)
            pool.wait_ge(sort_const, 2)
            nc.gpsimd.affine_select(out=before[:, :], in_=before[:, :], pattern=[[1, P]], base=0,
                                    channel_multiplier=-1, compare_op=ALU.is_gt, fill=0.0).then_inc(sort_const, 1)
            pool.wait_ge(pool_step, 2)
            pool.dma_start(sorted_d[E:SORTED, :].rearrange("(p n) c -> p (n c)", p=128),
                           nobody[:, :]).then_inc(sent, 16)

            pool.wait_ge(pos_done, 1)
            for j in range(EC):
                pool.indirect_dma_start(sorted_d, bass.IndirectOffsetOnAxis(ap=pos[0:P, j:j + 1], axis=0),
                                        pay[0:P, j, :], None).then_inc(scattered, 16)
            pool.wait_ge(evac, STORED * T)
            nc.gpsimd.iota(keybase[:, :], pattern=[[KEY, B]], base=0, channel_multiplier=0,
                           allow_small_or_imprecise_dtypes=True).then_inc(keybase_done, 1)

            def load_payloads(rnd):
                with pool.Fori(0, B) as b:
                    first = pool.value_load(meta[0:1, bass.ds(b, 1)], min_val=0, max_val=E) + rnd * SLOTS
                    pool.dma_start(pay_all[:, bass.ds(b, 1), :, :].rearrange("p o c e -> p (o c e)"),
                                   sorted_d[bass.ds(first, SLOTS), :].rearrange("(p c) e -> p (c e)", p=128)
                                   ).then_inc(pay_in, 16)

            pool.wait_ge(scattered, 16 * EC)
            pool.wait_ge(sent, 16)
            pool.wait_ge(meta_done, 2)
            load_payloads(0)

            pool.wait_ge(kstep, (O_ * T + 6) * K)
            nc.gpsimd.memset(Graw[:, :, :], 0.0).then_inc(g_zero, 1)
            pool.wait_ge(g_zero, 1)
            rounds = pool.value_load(meta[0:1, B:B + 1], min_val=1, max_val=MAX_ROUNDS)
            with pool.Fori(0, rounds) as rnd:
                with pool.Fori(0, B // 2) as m:
                    for slot in range(2):
                        i = rnd * B + m * 2 + slot
                        pool.wait_ge(idx_ready, i + 1)
                        for c in range(CAP):
                            pool.wait_ge(g_lo, i * CAP + (c + 1))
                            pool.sem_inc(passed_pool, 1)
                            pool.indirect_dma_start(
                                Graw[:, c, :], None, xn_d, bass.IndirectOffsetOnAxis(ap=idx[:, slot, c:c + 1], axis=0),
                                bounds_check=N - 1, oob_is_err=False).then_inc(raw_in[c], 16)
                with pool.If(rnd + 1 < rounds):
                    pool.wait_ge(tables, rnd + 1)
                    pool.sem_inc(passed_pool, 1)
                    load_payloads(rnd + 1)


def kernel(**inputs):
    import numpy as np
    import concourse.bacc as bacc
    from concourse.bass_utils import run_bass_kernel_spmd

    names = ["x", "src", "dst", "edge_type_8", "L0_gnn_weight", "L0_gnn_root", "L0_gnn_bias", "L0_gnn_w_gate",
             "L0_gnn_b_gate", "L0_mix_Wq", "L0_mix_Wk", "L0_mix_Wv", "L0_mix_Wg", "L0_mix_bg", "L0_mix_Wo",
             "L0_ffn_W_i", "L0_ffn_b_i", "L0_ffn_W_o", "L0_ffn_b_o", "L0_ffn_W_c", "L0_ffn_b_c"]
    nc = bacc.Bacc("TRN2", target_bir_lowering=False, num_devices=1)
    arrays, args = {}, []
    for name in names:
        a = np.ascontiguousarray(inputs[name])
        arrays[f"in_{name}"] = a
        args.append(nc.dram_tensor(f"in_{name}", a.shape, mybir.dt.from_np(a.dtype), kind="ExternalInput").ap())
    args.append(nc.dram_tensor("out_x", [N, D], F32, kind="ExternalOutput").ap())
    build(nc, *args)
    result = run_bass_kernel_spmd(nc, [arrays], core_ids=[0])
    return result.results[0]["out_x"]
```

```python
from contextlib import ExitStack

import concourse.bass as bass
from concourse import mybir

F32 = mybir.dt.float32
F32R = mybir.dt.float32r
BF16 = mybir.dt.bfloat16
I16 = mybir.dt.int16
I32 = mybir.dt.int32
ALU = mybir.AluOpType
ACT = mybir.ActivationFunctionType
AX = mybir.AxisListType

N = 1250
D = 1024
E = 40000
R = 8
T = 10
P = N // T
K = D // 128
H = 512
HEAD = 64
PAIRS = D // (2 * HEAD)
EC = E // P
B = R * T
CAP = 5
SLOTS = CAP * 128
MAX_ROUNDS = -(-E // SLOTS)
SORTED = E + (MAX_ROUNDS + 1) * SLOTS
KEY = 128
NO_ROW = 4096
LN_EPS = 1e-5
CB = 8
COUNTS = EC // CB

V_, G_, ROOT_, GATEX_, K_, Q_, O_ = range(7)
STAGES_A = 7
STORED = 4
INPUT_, CELL_, OUTPUT_ = range(3)
STAGES_E = 3
CONSTS = 3
TILE_IN = 32
KV_COPIES = 4


def is_first(i):
    return isinstance(i, int) and i == 0


def up(size):
    return (size + 31) // 32 * 32


OFFSETS_AT = (ROOT_, 2)
PLACES = 12


def sorted_beside(s, t):
    if t == T - 1:
        return 0, 0
    if s == V_ and t >= 1:
        return 3 * t - 3, 3 * t
    if s == G_:
        return 24 + 5 * t, 29 + 5 * t
    if s == ROOT_ and t < 2:
        return 69 + 6 * t, min(75 + 6 * t, B)
    return 0, 0


def counted_beside(s, t):
    if t == T - 1:
        return 0, 0
    if s == GATEX_ and t >= 1:
        return 3 * t - 3, 3 * t
    if s == K_:
        return min(24 + 2 * t, COUNTS), min(26 + 2 * t, COUNTS)
    return 0, 0


class Tally:

    def __init__(self, sem):
        self.sem, self.n = sem, 0

    def inc(self, instruction):
        self.n += 1
        instruction.then_inc(self.sem, 1)

    def wait(self, engine):
        engine.wait_ge(self.sem, self.n)


def build(nc, x, src, dst, edge_type, weight, root, bias, w_gate, b_gate, Wq, Wk, Wv, Wg, bg, Wo,
          W_i, b_i, W_o, b_o, W_c, b_c, out):
    with ExitStack() as ctx:
        def sem(name):
            return ctx.enter_context(nc.semaphore(name))

        def dram(name, shape, dt=F32):
            return nc.dram_tensor(name, shape, dt).ap()

        xn_d = dram("xn_d", [N, D])
        v_d = dram("v_d", [N, D])
        g_d = dram("g_d", [N, D])
        ur_d = dram("ur_d", [N, D])
        zx_d = dram("zx_d", [N, D])
        acc_d = dram("acc_d", [N, D])
        x1_d = dram("x1_d", [N, D])
        gi_d = dram("gi_d", [N, D])
        tc_d = dram("tc_d", [N, D])
        sorted_d = dram("sorted_d", [SORTED, 2], I32)

        def rows(t):
            return slice(t * P, (t + 1) * P)

        top = [up(nc.sbuf_base)]

        def at(offset, name, shape, dt=F32):
            return nc.alloc_sbuf_tensor_at(name, shape, dt, offset=offset)

        def put(name, shape, dt=F32):
            size = {F32: 4, F32R: 4, I32: 4, BF16: 2}[dt]
            for n in shape[1:]:
                size *= n
            a = at(top[0], name, shape, dt)
            top[0] += up(size)
            return a

        ident = put("ident", [128, 128])
        iota = put("iota", [128, P])
        meta = put("meta", [128, B + 8], I32)
        inv = put("inv", [128, B])
        ksum = put("ksum", [128, PAIRS, 2])
        stats = put("stats", [128, 16])
        den = put("den", [128, 16])
        ones2 = put("ones2", [128, 2])
        idx = put("idx", [128, 2, 8], I32)
        bias_at = top[0]
        bias_sb = put("bias_sb", [128, D])
        k_total = at(bias_at, "k_total", [128, D])
        pay_at = top[0]
        pay = put("pay", [128, EC, 2], I32)
        pos = put("pos", [128, EC], I32)
        Whi = put("Whi", [128, K, D], F32R)
        Wlo = put("Wlo", [128, K, D], F32R)
        Wraw = put("Wraw", [128, K, D])
        free = top[0]
        aThi = put("aThi", [128, T, K, P], F32R)
        aTlo = put("aTlo", [128, T, K, P], F32R)
        io_at = top[0]
        io = put("io", [128, 2, D])
        res = put("res", [128, 2, D])
        small_at = top[0]
        kv = at(small_at, "kv", [128, PAIRS, 128])
        qT = at(small_at + 4096, "qT", [128, K, P])
        raw_edges = at(free + (T - 1) * K * P * 4, "raw_edges", [128, 3, EC], I32)
        top[0] = small_at
        bucket = put("bucket", [128, EC])
        node = put("node", [128, EC])
        cum = put("cum", [128, B + 1])
        per = put("per", [128, B])
        off = put("off", [128, B])
        base = put("base", [128, B])
        step_at = top[0]
        onehot_b = put("onehot_b", [128, EC], BF16)
        scan = put("scan", [128, 2, EC])
        sel = at(pay_at + EC * 8, "sel", [128, EC])
        oh_node = at(step_at, "oh_node", [128, CB, P], BF16)
        oh_bucket = at(step_at + up(CB * P * 2), "oh_bucket", [128, CB, B], BF16)
        assert top[0] <= small_at + 8096 and step_at + up(CB * P * 2) + CB * B * 2 <= small_at + 8096
        top[0] = free
        Graw = put("Graw", [128, CAP, D])
        mTlo = put("mTlo", [128, 2, K, P], F32R)
        mean = put("mean", [128, D])
        mThi = put("mThi", [128, 2, K, P], F32R)
        OH = put("OH", [128, 2, CAP, P], F32R)
        Ghi = put("Ghi", [128, 2, D], F32R)
        Glo = put("Glo", [128, 2, D], F32R)
        U = put("U", [128, T, D])
        assert top[0] <= nc.sbuf_usable_end
        keybase = at(bias_at + B * CAP * 8, "keybase", [128, B])
        pay_all = at(bias_at, "pay_all", [128, B, CAP, 2], I32)
        idx_all = at(pay_at, "idx_all", [128, B, CAP], I32)
        loc_all = at(pay_at + up(B * CAP * 4), "loc_all", [128, B, CAP])
        assert 2 * up(B * CAP * 4) <= EC * 12
        uThi = at(free, "uThi", [128, 2, K, P], F32R)
        uTlo = at(free + up(8 * K * P), "uTlo", [128, 2, K, P], F32R)
        th_at = free + 2 * up(8 * K * P)
        th = at(th_at, "th", [128, 2, D])
        tile_at = (th_at + 8 * D, free + up(4 * T * K * P) + up(4 * K * P))
        ld = [at(tile_at[i], f"ld{i}", [128, 3, D]) for i in range(2)]
        assert tile_at[0] + 12 * D <= free + up(4 * T * K * P) and tile_at[1] + 12 * D <= top[0] - 4 * T * D
        x1s = at(small_at, "x1s", [128, 2, D])
        ones = at(io_at, "ones", [128, P])
        before = at(io_at + 512, "before", [128, P])
        place = at(io_at + 1024, "place", [128, 2, EC])
        nobody = at(io_at + 1024 + 8 * EC, "nobody", [128, 2 * (SORTED - E) // 128], I32)

        acc = ctx.enter_context(nc.psum_tensor("acc", [128, 2, 2, H], F32))
        tp = ctx.enter_context(nc.psum_tensor("tp", [128, 2, H], F32))
        aux = ctx.enter_context(nc.psum_tensor("aux", [128, 2, H], F32))
        tpv = tp[:, :, 0:4 * P]

        turned_weight = (aux, tp)
        degrees = aux[0:P, 1, 256:256 + B]

        def as_blocks(a):
            return a.rearrange("p (h b) n -> p h (b n)", h=2)

        w_raw = [sem(f"w_raw{k}") for k in range(K)]
        w_hi, w_lo = sem("w_hi"), sem("w_lo")
        kstep = sem("kstep")
        x_in = [sem(f"x_in{i}") for i in range(2)]
        ln_done, xn_st = sem("ln_done"), [sem(f"xn_st{i}") for i in range(2)]
        turned, at_hi, at_lo = sem("turned"), sem("at_hi"), sem("at_lo")
        bias_in = sem("bias_in")
        evac = sem("evac")
        sig = sem("sig")
        res_st = [sem(f"res_st{i}") for i in range(2)]
        acc_st = [sem(f"acc_st{i}") for i in range(2)]
        neg, expd = sem("neg"), sem("expd")
        k_added = sem("k_added")
        kv_done, kv_sb = sem("kv_done"), sem("kv_sb")
        q_turned, q_T, num_done, num_out, o_turned, ot_hi, ot_lo = (
            sem(n) for n in ("q_turned", "q_T", "num_done", "num_out", "o_turned", "ot_hi", "ot_lo"))
        const, edges_in, sent = sem("const"), sem("edges_in"), sem("sent")
        edges_made = sem("edges_made")
        dve_step, pool_step = sem("dve_step"), sem("pool_step")
        passed_dve, passed_pool = sem("passed_dve"), sem("passed_pool")
        sort_cum, sort_sum, sort_off, pos_done, scattered = (
            sem(n) for n in ("sort_cum", "sort_sum", "sort_off", "pos_done", "scattered"))
        cnt_oh, cnt_mm, inv_done, meta_done = (
            sem(n) for n in ("cnt_oh", "cnt_mm", "inv_done", "meta_done"))
        pay_in, tables = sem("pay_in"), sem("tables")
        u_in = sem("u_in")
        idx_ready, oh_ready = sem("idx_ready"), sem("oh_ready")
        raw_in = [sem(f"raw_in{c}") for c in range(CAP)]
        g_zero, g_hi, g_lo, agg = sem("g_zero"), sem("g_hi"), sem("g_lo"), sem("agg")
        mean_out, m_turned, mt_hi, mt_lo, acc_free = (
            sem(n) for n in ("mean_out", "m_turned", "mt_hi", "mt_lo", "acc_free"))
        kv_zero, sort_const, keybase_done, table_step = (
            sem(n) for n in ("kv_zero", "sort_const", "keybase_done", "table_step"))
        less_xn = sem("less_xn")
        b_out = sem("b_out")
        w2_raw = [sem(f"w2_raw{k}") for k in range(K)]
        w2_hi, w2_lo, w2_turned, kstep2 = (sem(n) for n in ("w2_hi", "w2_lo", "w2_turned", "kstep2"))
        u_turned, ut_hi, ut_lo, th_done, c_evac, x1_made = (
            sem(n) for n in ("u_turned", "ut_hi", "ut_lo", "th_done", "c_evac", "x1_made"))
        ld_in = [sem(f"ld_in{i}") for i in range(2)]
        x1_st = [sem(f"x1_st{i}") for i in range(2)]
        e_in = [sem(f"e_in{i}") for i in range(2)]
        e_st = [sem(f"e_st{i}") for i in range(2)]
        x1s_in = [sem(f"x1s_in{i}") for i in range(2)]
        ln2_done, x1_turned, et_hi, et_lo, e_evac, e_act, cell, cell_th, out_made, bias2_in = (
            sem(n) for n in ("ln2_done", "x1_turned", "et_hi", "et_lo", "e_evac", "e_act", "cell", "cell_th",
                             "out_made", "bias2_in"))

        A_TILES = STAGES_A * T
        weights_a = [Wv, Wg, root, w_gate[D:2 * D, :], Wk, Wq, Wo]
        biases_a = {G_: bg, ROOT_: bias, GATEX_: b_gate}
        scratch_a = {V_: v_d, G_: g_d, ROOT_: ur_d, GATEX_: zx_d}

        def io_count(s, t):
            return TILE_IN * ({V_: 0, K_: 1, Q_: 2, O_: 3}[s] * (T // 2) + t // 2 + 1)

        LO_CREDIT, AGG_CREDIT, ACC_CREDIT = CAP, 2, 2

        block = ctx.enter_context(nc.Block())

        def move_tile(engine, to, source, signal):
            for part in (slice(0, P // 16 * 16), slice(P // 16 * 16, P)):
                engine.dma_start(to[part, :], source[part, :]).then_inc(signal, 16)

        @block.sync
        def _(sp):
            def load_w(stage, source):
                for k in range(K):
                    if stage:
                        sp.wait_ge(w_lo, K * (stage - 1) + k + 1)
                    sp.dma_start(Wraw[:, k, :], source[k * 128:(k + 1) * 128, :]).then_inc(w_raw[k], 16)


            def load_io(t, source):
                move_tile(sp, io[0:P, t % 2, :], source[rows(t), :], x_in[t % 2])

            def load_bias(source):
                sp.dma_start(bias_sb[0:P, :], source.rearrange("(o n) -> o n", o=1)
                             .to_broadcast([P, D])).then_inc(bias_in, 16)

            def store_tile(s, t):
                if s == G_:
                    sp.wait_ge(sig, t + 1)
                else:
                    sp.wait_ge(evac, s * T + t + 1)
                move_tile(sp, scratch_a[s][rows(t), :], res[0:P, t % 2, :], res_st[t % 2])

            load_io(0, x)
            load_w(0, weights_a[0])
            load_io(1, x)
            for i, a in enumerate((src, dst, edge_type)):
                sp.dma_start(raw_edges[0:P, i, :], a.rearrange("(p c) -> p c", p=P)).then_inc(edges_in, 16)
            for s in range(STAGES_A):
                if s in biases_a:
                    if s > G_:
                        sp.wait_ge(evac, s * T)
                    load_bias(biases_a[s])
                if s > V_:
                    load_w(s + 1, weights_a[s + 1] if s + 1 < STAGES_A else weight[0])
                if s == Q_:
                    for t in range(2):
                        sp.wait_ge(kv_done, T - 1 + t)
                        load_io(t, g_d)
                if s == O_:
                    for t in range(2):
                        sp.wait_ge(num_out, T - 1 + t)
                        load_io(t, x)
                for t in range(T):
                    if s == V_:
                        sp.wait_ge(ln_done, t + 1)
                        move_tile(sp, xn_d[rows(t), :], io[0:P, t % 2, :], xn_st[t % 2])
                        if t + 2 < T:
                            sp.wait_ge(xn_st[t % 2], TILE_IN * (t // 2 + 1))
                            sp.wait_ge(turned, t + 1)
                            load_io(t + 2, x)
                    if (s, t) == (V_, 2):
                        load_w(G_, weights_a[G_])
                    if s == V_ and t:
                        store_tile(s, t - 1)
                    if s == V_ and t == T - 1 or V_ < s < STORED:
                        store_tile(s, t)
                    if (s, t) == (GATEX_, T - 3):
                        for i in range(2):
                            sp.wait_ge(res_st[i], TILE_IN * (T // 2))
                        sp.wait_ge(pos_done, 1)
                        sp.wait_ge(sent, 16)
                        load_io(0, v_d)
                        load_io(1, v_d)
                    if s == K_ and t >= 1 and t + 1 < T:
                        sp.wait_ge(kv_done, t)
                        load_io(t + 1, v_d)
                    if s == Q_ and t >= 1 and t + 1 < T:
                        sp.wait_ge(num_out, t)
                        load_io(t + 1, g_d)
                    if s == O_ and t >= 1 and t + 1 < T:
                        sp.wait_ge(evac, s * T + t)
                        load_io(t + 1, x)
                if s == STORED - 1:
                    for i in range(2):
                        sp.wait_ge(res_st[i], TILE_IN * STORED * (T // 2))
                        sp.wait_ge(xn_st[i], TILE_IN * (T // 2))

            def load_sums(first, last):
                for t in range(first, last):
                    move_tile(sp, U[0:P, t, :], ur_d[rows(t), :], u_in)

            sp.wait_ge(kstep, (A_TILES - 1) * K)
            load_sums(0, 3)
            sp.wait_ge(evac, A_TILES)
            sp.wait_ge(kstep, A_TILES * K)
            sp.wait_ge(acc_st[0], TILE_IN * (T // 2))
            sp.wait_ge(acc_st[1], TILE_IN * (T // 2))
            load_sums(3, T)
            sp.wait_ge(meta_done, 2)
            rounds = sp.value_load(meta[0:1, B:B + 1], min_val=1, max_val=MAX_ROUNDS)
            all_w = weight.rearrange("r i o -> (r i) o")

            def load_relation(r, w0):
                for k in range(K):
                    sp.wait_ge(w_lo, w0 + k)
                    sp.dma_start(Wraw[:, k, :], all_w[bass.ds(r * D + k * 128, 128), :]).then_inc(w_raw[k], 16)

            sp.wait_ge(kstep, (A_TILES + 2) * K)
            with sp.Fori(0, rounds) as rnd:
                w0 = (rnd * R + (STAGES_A - 1)) * K + 1
                with sp.Fori(1, R) as r:
                    load_relation(r, w0 + r * K)
                with sp.If(rnd + 1 < rounds):
                    load_relation(0, w0 + R * K)

            def load_gate_tile(t):
                for i, a in enumerate((zx_d, xn_d, acc_d)):
                    move_tile(sp, ld[t % 2][0:P, i, :], a[rows(t), :], ld_in[t % 2])

            def load_lstm_w(s, source):
                for m in range(K):
                    if s == 1:
                        sp.wait_ge(w2_lo, m + 1)
                    elif m == 0:
                        sp.wait_ge(w2_turned, K * (s - 1))
                    sp.dma_start(Wraw[:, m, :], source[m * 128:(m + 1) * 128, D:2 * D]).then_inc(w2_raw[m], 16)

            sp.wait_ge(w_lo, (rounds * R + STAGES_A) * K)
            for k in range(K):
                sp.dma_start(Wraw[:, k, :], w_gate[k * 128:(k + 1) * 128, :]).then_inc(w2_raw[k], 16)
            def load_e(t, source):
                move_tile(sp, io[0:P, t % 2, :], source[rows(t), :], e_in[t % 2])

            sp.wait_ge(b_out, 1)
            load_gate_tile(0)
            load_gate_tile(1)
            load_lstm_w(1, W_i)
            for t in range(T):
                if t == T - 1:
                    sp.wait_ge(x1_turned, 1)
                    sp.wait_ge(x1_st[0], TILE_IN * 2)
                    load_e(2, x1_d)
                sp.wait_ge(x1_made, t + 1)
                move_tile(sp, x1_d[rows(t), :], ld[t % 2][0:P, 0, :], x1_st[t % 2])
                if t + 2 < T:
                    sp.wait_ge(x1_st[t % 2], TILE_IN * (t // 2 + 1))
                    load_gate_tile(t + 2)
                if t in (5, 6):
                    sp.wait_ge(th_done, t + 1)
                    sp.wait_ge(u_turned, t + 1)
                    load_e(t - 5, x1_d)

            biases_e = (b_i, b_c, b_o)
            sources_e = (x1_d, gi_d, tc_d)
            made_e = (e_act, cell_th, out_made)
            used_e = (x1_turned, cell, out_made)
            for s in range(STAGES_E):
                if s:
                    sp.wait_ge(e_evac, s * T)
                sp.dma_start(bias_sb[0:P, :], biases_e[s].rearrange("(o n) -> o n", o=1)
                             .to_broadcast([P, D])).then_inc(bias2_in, 16)
                for t in range(T):
                    if s == INPUT_:
                        ahead = [t + 3] if t + 3 < T else []
                    else:
                        ahead = [0, 1] if t == 0 else [t + 1] if t + 1 < T else []
                    for n in ahead:
                        if s == INPUT_:
                            sp.wait_ge(x1_st[n % 2], TILE_IN * (n // 2 + 1))
                        else:
                            sp.wait_ge(e_st[n % 2], TILE_IN * ((s - 1) * (T // 2) + n // 2 + 1))
                        if n >= 2:
                            sp.wait_ge(used_e[s], n - 1)
                        else:
                            sp.wait_ge(used_e[s - 1], T - 1 + n)
                        load_e(n, sources_e[s])
                        if s == OUTPUT_:
                            move_tile(sp, x1s[0:P, n % 2, :], x1_d[rows(n), :], x1s_in[n % 2])
                    if t == 0 and s + 1 < STAGES_E:
                        load_lstm_w(s + 2, (W_i, W_c, W_o)[s + 1])
                    sp.wait_ge(made_e[s], t + 1)
                    move_tile(sp, (gi_d, tc_d, out)[s][rows(t), :], res[0:P, t % 2, :], e_st[t % 2])
            for i in range(2):
                sp.wait_ge(e_st[i], TILE_IN * STAGES_E * (T // 2))
                sp.wait_ge(xn_st[i], TILE_IN * (T // 2))
                sp.wait_ge(x1_st[i], TILE_IN * (T // 2))
                sp.wait_ge(acc_st[i], TILE_IN * (T // 2))


        @block.tensor
        def _(pe):
            def split_product(slot, lhs_hi, lhs_lo, k, signal=kstep):
                first, last = k == 0, k == K - 1
                for a, w, start, stop in ((lhs_hi, Whi, first, False), (lhs_hi, Wlo, False, False),
                                          (lhs_lo, Whi, False, last)):
                    for h in range(2):
                        mm = nc.tensor.matmul(acc[0:P, slot, h, :], a, w[:, k, h * H:(h + 1) * H],
                                              start=start, stop=stop)
                mm.then_inc(signal, 1)

            def turn(source):
                for k in range(K):
                    tr = nc.tensor.transpose(tp[:, k // 4, (k % 4) * P:(k % 4 + 1) * P],
                                             source[:, k * 128:(k + 1) * 128], ident[0:P, 0:P])
                return tr

            def turn_x(t):
                pe.wait_ge(ln_done, t + 1)
                if t:
                    pe.wait_ge(at_lo, t)
                turn(io[0:P, t % 2, :]).then_inc(turned, 1)

            def kv_tile(t):
                pe.wait_ge(evac, K_ * T + t + 1)
                pe.wait_ge(x_in[t % 2], io_count(K_, t))
                for h in range(PAIRS):
                    cols = slice(h * 128, (h + 1) * 128)
                    mm = nc.tensor.matmul(tp[:, h // 4, (h % 4) * 128:(h % 4 + 1) * 128], res[0:P, t % 2, cols],
                                          io[0:P, t % 2, cols], start=(t == 0 and h % 4 == 0), stop=(t == T - 1),
                                          skip_group_check=True)
                if t == T - 1:
                    pe.wait_ge(k_added, T)
                    for h in range(PAIRS):
                        mm = nc.tensor.matmul(aux[:, 0, 2 * h:2 * h + 2], k_total[0:P, h * 128:(h + 1) * 128],
                                              ones2[0:P, :], start=True, stop=True)
                mm.then_inc(kv_done, 1)

            def turn_q(t):
                pe.wait_ge(evac, Q_ * T + t + 1)
                if t == 0:
                    pe.wait_ge(kv_sb, KV_COPIES)
                else:
                    pe.wait_ge(ot_lo, t)
                turn(res[0:P, t % 2, :]).then_inc(q_turned, 1)

            def numerator(t):
                pe.wait_ge(q_T, t + 1)
                if t:
                    pe.wait_ge(num_out, t)
                for h in range(PAIRS):
                    nc.tensor.matmul(acc[0:P, t % 2, h // 4, (h % 4) * 128:(h % 4 + 1) * 128], qT[:, h, :],
                                     kv[:, h, :], start=True, stop=True)
                    mm = nc.tensor.matmul(aux[0:P, 1, 2 * h:2 * h + 2], qT[:, h, :], ksum[:, h, :],
                                          start=True, stop=True)
                mm.then_inc(num_done, 1)

            def turn_o(t):
                pe.wait_ge(num_out, t + 1)
                pe.wait_ge(q_T, t + 1)
                turn(res[0:P, t % 2, :]).then_inc(o_turned, 1)

            def sort_sums():
                pe.wait_ge(sort_cum, 1)
                pe.wait_ge(sort_const, 3)
                nc.tensor.matmul(aux[0:P, 1, 0:B], ones[0:P, :], per[0:P, :], start=True, stop=True)
                nc.tensor.matmul(aux[0:P, 1, 128:128 + B], before[0:P, :], per[0:P, :],
                                 start=True, stop=True).then_inc(sort_sum, 1)

            def count_step(n):
                pe.wait_ge(cnt_oh, 2 * (n + 1))
                for j in range(CB):
                    mm = nc.tensor.matmul(degrees, oh_node[0:P, j, :], oh_bucket[0:P, j, :],
                                          start=(n == 0 and j == 0), stop=(n == COUNTS - 1 and j == CB - 1))
                mm.then_inc(cnt_mm, 1)

            def sums(i, slot, blocks):
                for c in blocks:
                    if c == 0:
                        pe.wait_ge(oh_ready, i + 1)
                        if is_first(i):
                            pe.wait_ge(inv_done, 2)
                        else:
                            pe.wait_ge(mean_out, i)
                    g = (slot * CAP + c) % 2
                    pe.wait_ge(g_lo, i * CAP + (c + 1 + LO_CREDIT))
                    for part, start, stop in ((Ghi, c == 0, False), (Glo, False, c == CAP - 1)):
                        for h in range(2):
                            mm = nc.tensor.matmul(aux[0:P, h, :], OH[:, slot, c, :],
                                                  part[:, g, h * H:(h + 1) * H], start=start, stop=stop)
                    mm.then_inc(agg, 1)

            def turn_mean(i):
                pe.wait_ge(mean_out, i + 1)
                if not is_first(i):
                    pe.wait_ge(mt_lo, i)
                turn(mean[0:P, :]).then_inc(m_turned, 1)

            def beside_product(i, slot, k):
                if k % 2 == 0:
                    if k < 6:
                        sums(i, slot, range(k, min(k + 2, CAP)))
                    else:
                        turn_mean(i)

            def beside(s, t, k):
                if s == V_ and t + 1 < T and k == 4:
                    turn_x(t + 1)
                if (s, t) == OFFSETS_AT and k == 5:
                    sort_sums()
                first, last = counted_beside(s, t)
                if k in (3, 5, 7) and first + (7 - k) // 2 < last:
                    count_step(last - 1 - (7 - k) // 2)
                if s == K_ and t >= 1 and k == 4:
                    kv_tile(t - 1)
                if s == Q_ and t == 0 and k == 4:
                    kv_tile(T - 1)
                n = (s - Q_) * T + t
                if s >= Q_ and 2 <= n < T + 2 and k == 1:
                    turn_o(n - 2)
                if s >= Q_ and 1 <= n < T + 1 and k == 3:
                    turn_q(n - 1)
                if s >= Q_ and 1 <= n < T + 1 and k == 6:
                    numerator(n - 1)
                if (s, t) == (O_, T - 1):
                    beside_product(0, 0, k)

            def tile_a(s, t):
                q = s * T + t
                if s == O_ and t < 2:
                    pe.wait_ge(num_out, T - 1 + t)
                elif s == Q_ and t >= 2:
                    pe.wait_ge(num_out, t - 1)
                elif q >= 2:
                    pe.wait_ge(evac, q - 1)
                if s == V_:
                    pe.wait_ge(at_lo, t + 1)
                if s == O_:
                    pe.wait_ge(ot_lo, t + 1)
                for k in range(K):
                    beside(s, t, k)
                    if t == 0:
                        pe.wait_ge(w_lo, K * s + k + 1)
                    split_product(t % 2, aThi[:, t, k, :], aTlo[:, t, k, :], k)

            pe.sem_inc(agg, AGG_CREDIT)
            pe.sem_inc(acc_free, ACC_CREDIT)
            pe.wait_ge(const, CONSTS)
            turn_x(0)
            for s in range(STAGES_A):
                for t in range(T):
                    if (s, t) == (O_, T - 1):
                        pe.wait_ge(meta_done, 2)
                        rounds = pe.value_load(meta[0:1, B:B + 1], min_val=1, max_val=MAX_ROUNDS)
                    tile_a(s, t)

            def bucket_step(i, slot, weight_count, last=False):
                for k in range(K):
                    if not last:
                        beside_product(i + 1, 1 - slot, k)
                    if k == 0:
                        pe.wait_ge(mt_lo, i + 1)
                        pe.wait_ge(acc_free, i + 1)
                    pe.wait_ge(w_lo, weight_count + k)
                    split_product(slot, mThi[:, slot, k, :], mTlo[:, slot, k, :], k)

            pe.wait_ge(evac, A_TILES)
            with pe.Fori(0, rounds) as rnd:
                i0 = rnd * B
                w0 = (rnd * R + STAGES_A) * K + 1
                with pe.Fori(0, R - 1) as r:
                    with pe.Fori(0, T // 2) as tt:
                        i = i0 + r * T + tt * 2
                        bucket_step(i, 0, w0 + r * K)
                        bucket_step(i + 1, 1, w0 + r * K)
                with pe.Fori(0, T // 2 - 1) as tt:
                    i = i0 + (R - 1) * T + tt * 2
                    bucket_step(i, 0, w0 + (R - 1) * K)
                    bucket_step(i + 1, 1, w0 + (R - 1) * K)
                bucket_step(i0 + (B - 2), 0, w0 + (R - 1) * K)
                bucket_step(i0 + (B - 1), 1, w0 + (R - 1) * K, last=True)
                with pe.If(rnd + 1 < rounds):
                    sums(i0 + B, 0, range(CAP))
                    turn_mean(i0 + B)

            def turn_u(t):
                if t == 0:
                    pe.wait_ge(b_out, 1)
                else:
                    pe.wait_ge(ut_lo, t)
                turn(U[0:P, t, :]).then_inc(u_turned, 1)

            def turn_weight(s, k):
                if k == 0:
                    for m in range(K):
                        pe.wait_ge(w2_raw[m], 16 * (s + 1))
                if k == 1:
                    pe.wait_ge(et_lo, 1 if s == 1 else T)
                if (s - 1) * K + k >= 2:
                    pe.wait_ge(w2_lo, K * s + k - 1)
                for m in range(K):
                    tr = nc.tensor.transpose(turned_weight[k % 2][:, m // 4, (m % 4) * 128:(m % 4 + 1) * 128],
                                             Wraw[:, m, k * 128:(k + 1) * 128], ident[:, :])
                tr.then_inc(w2_turned, 1)

            def turn_x1(t):
                pe.wait_ge(ln2_done, t + 1)
                if t == 0:
                    pe.wait_ge(ut_lo, T)
                else:
                    pe.wait_ge(et_lo, t)
                if t == 1:
                    pe.wait_ge(w2_lo, 2 * K)
                turn(io[0:P, t % 2, :]).then_inc(x1_turned, 1)

            turn_u(0)
            for t in range(T):
                if t == T - 1:
                    turn_x1(0)
                pe.wait_ge(ut_lo, t + 1)
                if t >= 2:
                    pe.wait_ge(c_evac, t - 1)
                for k in range(K):
                    if t + 1 < T and k == 4:
                        turn_u(t + 1)
                    if t == 0:
                        pe.wait_ge(w2_lo, k + 1)
                    split_product(t % 2, uThi[:, t % 2, k, :], uTlo[:, t % 2, k, :], k, kstep2)
                    if t == T - 1:
                        turn_weight(1, k)

            for s in range(STAGES_E):
                for t in range(T):
                    q = s * T + t
                    if q >= 2:
                        pe.wait_ge(e_evac, q - 1)
                    else:
                        pe.wait_ge(c_evac, T - 1 + q)
                    if s == 0:
                        pe.wait_ge(et_lo, t + 1)
                    for k in range(K):
                        if s == 0 and t + 1 < T and k == 4:
                            turn_x1(t + 1)
                        if t == 0:
                            pe.wait_ge(w2_lo, K * (s + 1) + k + 1)
                        split_product(t % 2, aThi[:, t, k, :], aTlo[:, t, k, :], k, kstep2)
                        if t == T - 1 and s + 1 < STAGES_E:
                            turn_weight(s + 2, k)

        @block.scalar
        def _(act):
            def split_w(stage, k, raw_count, free_count, raw=w_raw, free=kstep, done=w_hi):
                act.wait_ge(raw[k], raw_count)
                if free_count is not None:
                    act.wait_ge(free, free_count)
                nc.scalar.copy(Whi[:, k, :], Wraw[:, k, :]).then_inc(done, 1)

            def split_w_a(s, blocks=range(K)):
                for k in blocks:
                    split_w(s, k, 16 * (s + 1), s * T * K - K + k + 1 if s else None)

            def at_tile(t):
                act.wait_ge(turned, t + 1)
                nc.scalar.copy(as_blocks(aThi[:, t, :, :]), tpv).then_inc(at_hi, 1)

            def turned_q(t):
                act.wait_ge(q_turned, t + 1)
                if t:
                    act.wait_ge(num_done, t)
                else:
                    act.wait_ge(kv_sb, KV_COPIES)
                nc.scalar.copy(as_blocks(qT[:, :, :]), tpv).then_inc(q_T, 1)

            def turned_o(t):
                act.wait_ge(o_turned, t + 1)
                nc.scalar.copy(as_blocks(aThi[:, t, :, :]), tpv).then_inc(ot_hi, 1)

            def hi_part(i, slot, c):
                act.wait_ge(raw_in[c], (i + 1) * 16)
                act.wait_ge(agg, i * CAP + (c + 1))
                nc.scalar.copy(Ghi[:, (slot * CAP + c) % 2, :], Graw[:, c, :]).then_inc(g_hi, 1)

            def means(i, b):
                act.wait_ge(agg, i * CAP + (CAP + AGG_CREDIT))
                if not is_first(i):
                    act.wait_ge(m_turned, i)
                nc.scalar.activation(mean[0:P, :], aux[0:P, :, :].rearrange("p h n -> p (h n)"), ACT.Copy,
                                     scale=inv[0:P, bass.ds(b, 1)]).then_inc(mean_out, 1)

            def turned_means(i, slot):
                act.wait_ge(m_turned, i + 1)
                act.wait_ge(kstep, A_TILES * K if is_first(i) else i * K + (A_TILES - 1) * K)
                nc.scalar.copy(as_blocks(mThi[:, slot, :, :]), tpv).then_inc(mt_hi, 1)

            def split_relation(stage, blocks):
                for k in blocks:
                    split_w(stage, k, (stage + 1) * 16, stage * (T * K) + (k + 1 - K))

            def round_start(i, stage):
                split_relation(stage, range(K))
                for c in range(CAP):
                    hi_part(i, 0, c)
                hi_part(i + 1, 1, 0)
                means(i, 0)
                hi_part(i + 1, 1, 1)
                turned_means(i, 0)

            def bucket_work(i, slot, b, early=None, late=None, left=2):
                if left >= 1:
                    hi_part(i + 1, 1 - slot, 2)
                    hi_part(i + 1, 1 - slot, 3)
                if early:
                    split_relation(early[0], early[1][0:2])
                if left >= 1:
                    hi_part(i + 1, 1 - slot, 4)
                if early:
                    split_relation(early[0], early[1][2:4])
                if left >= 2:
                    hi_part(i + 2, slot, 0)
                if left >= 1:
                    means(i + 1, b + 1)
                if left >= 2:
                    hi_part(i + 2, slot, 1)
                if left >= 1:
                    turned_means(i + 1, 1 - slot)
                if late:
                    split_relation(late[0], late[1])

            def relation_work(i, b, stage, first=False, last=False):
                bucket_work(i, 0, b, None if first else (stage, range(4, K)))
                bucket_work(i + 1, 1, b + 1)
                with act.Fori(1, T // 2 - 1) as tt:
                    bucket_work(i + tt * 2, 0, b + tt * 2)
                    bucket_work(i + tt * 2 + 1, 1, b + tt * 2 + 1)
                bucket_work(i + (T - 2), 0, b + (T - 2), left=1 if last else 2)
                if not last:
                    bucket_work(i + (T - 1), 1, b + (T - 1), early=(stage + 1, range(0, 2)),
                                late=(stage + 1, range(2, 4)))

            split_w_a(0, range(0, 3))
            at_tile(0)
            split_w_a(0, range(3, K))
            for s in range(STAGES_A):
                for t in range(T):
                    n = (s - Q_) * T + t
                    if s == V_ and t + 1 < T:
                        at_tile(t + 1)
                    if s >= Q_ and 2 <= n < T + 2:
                        turned_o(n - 2)
                    if s >= Q_ and 1 <= n < T + 1:
                        turned_q(n - 1)
                    if t == T - 1 and s + 1 < STAGES_A:
                        split_w_a(s + 1)
                    if (s, t) == (O_, T - 2):
                        act.wait_ge(kstep, (O_ * T + 6) * K)
                        hi_part(0, 0, 0)
                        hi_part(0, 0, 1)
                    if (s, t) == (O_, T - 1):
                        act.wait_ge(inv_done, 2)
                        hi_part(0, 0, 2)
                        hi_part(0, 0, 3)
                        split_relation(STAGES_A, range(0, 2))
                        hi_part(0, 0, 4)
                        split_relation(STAGES_A, range(2, 4))
                        hi_part(1, 1, 0)
                        means(0, 0)
                        hi_part(1, 1, 1)
                        split_relation(STAGES_A, range(4, 6))
                        turned_means(0, 0)
                        split_relation(STAGES_A, range(6, K))
                    if s == V_:
                        act.wait_ge(kstep, K * (t + 1))
                        if t >= 2:
                            act.wait_ge(res_st[t % 2], TILE_IN * (t // 2))
                        nc.scalar.copy(res[0:P, t % 2, :], acc[0:P, t % 2, :, :].rearrange("p h n -> p (h n)")
                                       ).then_inc(evac, 1)
                    if s == G_:
                        act.wait_ge(evac, s * T + t + 1)
                        nc.scalar.activation(res[0:P, t % 2, :], res[0:P, t % 2, :], ACT.Sigmoid).then_inc(sig, 1)
                    if s in (K_, Q_):
                        act.wait_ge(neg, (s - K_) * T + t + 1)
                        nc.scalar.activation(res[0:P, t % 2, :], res[0:P, t % 2, :], ACT.Exp).then_inc(expd, 1)
                    if s == O_:
                        act.wait_ge(evac, s * T + t + 1)
                        move_tile(act, acc_d[rows(t), :], res[0:P, t % 2, :], acc_st[t % 2])

            act.wait_ge(meta_done, 2)
            rounds = act.value_load(meta[0:1, B:B + 1], min_val=1, max_val=MAX_ROUNDS)
            with act.Fori(0, rounds) as rnd:
                i0 = rnd * B
                stage0 = rnd * R + STAGES_A
                relation_work(i0, 0, stage0, first=True)
                with act.Fori(1, R - 1) as r:
                    relation_work(i0 + r * T, r * T, stage0 + r)
                relation_work(i0 + (R - 1) * T, (R - 1) * T, stage0 + (R - 1), last=True)
                with act.If(rnd + 1 < rounds):
                    round_start(i0 + B, stage0 + R)

            def u_tile(t):
                act.wait_ge(u_turned, t + 1)
                if t >= 2:
                    act.wait_ge(kstep2, K * (t - 1))
                nc.scalar.copy(as_blocks(uThi[:, t % 2, :, :]), tpv).then_inc(ut_hi, 1)
                if t >= 2:
                    act.wait_ge(x1_made, t - 1)
                nc.scalar.activation(th[0:P, t % 2, :], U[0:P, t, :], ACT.Tanh).then_inc(th_done, 1)

            def split_w_e(s):
                for k in range(K):
                    act.wait_ge(w2_turned, K * (s - 1) + k + 1)
                    act.wait_ge(kstep2, s * T * K - K + k + 1)
                    nc.scalar.copy(Whi[:, k, :], turned_weight[k % 2][:, :, :].rearrange("p h n -> p (h n)")
                                   ).then_inc(w2_hi, 1)

            for k in range(K // 2):
                split_w(0, k, 16, rounds * (B * K) + ((A_TILES - 1) * K + k + 1), w2_raw, kstep, w2_hi)
            act.wait_ge(b_out, 1)
            u_tile(0)
            for k in range(K // 2, K):
                split_w(0, k, 16, None, w2_raw, None, w2_hi)
            for t in range(1, T):
                u_tile(t)

            def x1_tile(t):
                act.wait_ge(x1_turned, t + 1)
                if t == 1:
                    for i in range(2):
                        act.wait_ge(x1_st[i], TILE_IN * (T // 2))
                nc.scalar.copy(as_blocks(aThi[:, t, :, :]), tpv).then_inc(et_hi, 1)

            x1_tile(0)
            split_w_e(1)
            for s in range(STAGES_E):
                for t in range(T):
                    if s == 0 and t + 1 < T:
                        x1_tile(t + 1)
                    if t == T - 1 and s + 1 < STAGES_E:
                        split_w_e(s + 2)
                    act.wait_ge(e_evac, s * T + t + 1)
                    f = ACT.Tanh if s == CELL_ else ACT.Sigmoid
                    nc.scalar.activation(res[0:P, t % 2, :], res[0:P, t % 2, :], f).then_inc(e_act, 1)
                    if s == CELL_:
                        act.wait_ge(cell, t + 1)
                        nc.scalar.activation(res[0:P, t % 2, :], res[0:P, t % 2, :], ACT.Tanh).then_inc(cell_th, 1)

        @block.vector
        def _(dve):
            step = Tally(dve_step)

            def chain(instruction):
                step.inc(instruction)
                step.wait(dve)

            def split_w(k, count, hi=w_hi, done=w_lo):
                dve.wait_ge(hi, count)
                nc.vector.tensor_tensor(Wlo[:, k, :], Wraw[:, k, :], Whi[:, k, :].bitcast(F32),
                                        ALU.subtract).then_inc(done, 1)

            def inverse_sqrt(v, y, work):
                chain(nc.vector.tensor_scalar(v, v, LN_EPS, None, ALU.add))
                chain(nc.vector.tensor_scalar(y.bitcast(I32), v.bitcast(I32), 1, None, ALU.logical_shift_right))
                chain(nc.vector.tensor_scalar(y.bitcast(I32), y.bitcast(I32), -1.0, float(0x5F3759DF),
                                              ALU.mult, ALU.add))
                for _ in range(3):
                    chain(nc.vector.scalar_tensor_tensor(work, y, v, y, ALU.mult, ALU.mult))
                    chain(nc.vector.tensor_scalar(work, work, -0.5, 1.5, ALU.mult, ALU.add))
                    chain(nc.vector.tensor_tensor(y, y, work, ALU.mult))

            def layer_norm(a):
                for h in range(2):
                    step.inc(nc.vector.bn_stats(stats[0:P, 6 * h:6 * h + 6], a[:, h * H:(h + 1) * H]))
                step.wait(dve)
                chain(nc.vector.bn_aggr(stats[0:P, 12:14], stats[0:P, 0:12]))
                inverse_sqrt(stats[0:P, 13:14], stats[0:P, 14:15], stats[0:P, 0:1])
                return nc.vector.tensor_scalar(a, a, stats[0:P, 12:13], stats[0:P, 14:15],
                                               ALU.subtract, ALU.mult)

            def ln_x(t):
                dve.wait_ge(x_in[t % 2], io_count(V_, t))
                layer_norm(io[0:P, t % 2, :]).then_inc(ln_done, 1)

            def lo_of_turned(out_hi, out_lo, hi, count, done):
                dve.wait_ge(hi, count)
                nc.vector.tensor_tensor(as_blocks(out_lo), tpv, as_blocks(out_hi).bitcast(F32),
                                        ALU.subtract).then_inc(done, 1)

            def sort_bucket(b):
                chain(nc.vector.tensor_scalar(onehot_b[0:P, :], bucket[0:P, :], float(b), None, ALU.is_equal))
                chain(nc.vector.tensor_tensor_scan(scan[0:P, b % 2, :], onehot_b[0:P, :], onehot_b[0:P, :],
                                                   cum[0:P, b:b + 1], ALU.add, ALU.bypass))
                step.inc(nc.vector.copy_predicated(sel[0:P, :], onehot_b[0:P, :].bitcast(I16), scan[0:P, b % 2, :]))
                chain(nc.vector.tensor_copy(cum[0:P, b + 1:b + 2], scan[0:P, b % 2, EC - 1:EC]))

            def sort_offsets():
                dve.wait_ge(sort_sum, 1)
                total, earlier = aux[0:P, 1, 0:B], aux[0:P, 1, 128:128 + B]
                chain(nc.vector.tensor_tensor_scan(base[0:P, :], total, per[0:P, :], 0.0, ALU.add, ALU.bypass))
                chain(nc.vector.tensor_tensor(base[0:P, :], base[0:P, :], total, ALU.subtract))
                chain(nc.vector.scalar_tensor_tensor(off[0:P, :], earlier, -1.0, base[0:P, :], ALU.add, ALU.add))
                nc.vector.tensor_tensor(off[0:P, :], off[0:P, :], cum[0:P, 0:B], ALU.subtract).then_inc(sort_off, 1)
                nc.vector.tensor_copy(meta[0:P, 0:B], base[0:P, :]).then_inc(meta_done, 1)
                chain(nc.vector.tensor_reduce(stats[0:P, 15:16], total, AX.X, ALU.max))
                chain(nc.vector.tensor_scalar(stats[0:P, 15:16], stats[0:P, 15:16], float(SLOTS - 1),
                                              1.0 / SLOTS, ALU.add, ALU.mult))
                nc.vector.tensor_scalar(meta[0:P, B:B + 1], stats[0:P, 15:16], -0.4995, None,
                                        ALU.add).then_inc(meta_done, 1)

            def place_buckets(first, count):
                def offsets(b):
                    return nc.vector.tensor_scalar(place[0:P, b % 2, :], bucket[0:P, :], float(b),
                                                   off[0:P, b:b + 1], ALU.is_equal, ALU.mult)
                chain(offsets(first))
                for b in range(first, first + count):
                    if b + 1 < first + count:
                        step.inc(offsets(b + 1))
                    chain(nc.vector.tensor_tensor(sel[0:P, :], sel[0:P, :], place[0:P, b % 2, :], ALU.add))
                if first + count == B:
                    nc.vector.tensor_copy(pos[0:P, :], sel[0:P, :]).then_inc(pos_done, 1)

            def count_step(n):
                if n:
                    dve.wait_ge(cnt_mm, n)
                for out_oh, value, width in ((oh_node, node, P), (oh_bucket, bucket, B)):
                    nc.vector.tensor_tensor(
                        out_oh[0:P, :, :], value[0:P, n * CB:(n + 1) * CB].unsqueeze(2).to_broadcast([P, CB, width]),
                        iota[0:P, 0:width].unsqueeze(1).to_broadcast([P, CB, width]), ALU.is_equal).then_inc(cnt_oh, 1)

            def in_degrees():
                dve.wait_ge(cnt_mm, COUNTS)
                nc.vector.tensor_scalar(inv[0:P, :], degrees, 1.0, None, ALU.max).then_inc(inv_done, 1)
                dve.wait_ge(inv_done, 1)
                nc.vector.reciprocal(inv[0:P, :], inv[0:P, :]).then_inc(inv_done, 1)

            def product(slot):
                return acc[0:P, slot, :, :].rearrange("p h n -> p (h n)")

            def elu_plus_one(s, t):
                n = (s - K_) * T + t
                dve.wait_ge(kstep, K * (s * T + t + 1))
                nc.vector.tensor_scalar(res[0:P, t % 2, :], product(t % 2), 0.0, None, ALU.min).then_inc(neg, 1)
                dve.wait_ge(expd, n + 1)
                nc.vector.scalar_tensor_tensor(res[0:P, t % 2, :], product(t % 2), 0.0, res[0:P, t % 2, :],
                                               ALU.max, ALU.add).then_inc(evac, 1)

            def add_up_k(t):
                dve.wait_ge(evac, K_ * T + t + 1)
                if t == 0:
                    nc.vector.tensor_copy(k_total[0:P, :], res[0:P, 0, :]).then_inc(k_added, 1)
                else:
                    dve.wait_ge(k_added, t)
                    nc.vector.tensor_tensor(k_total[0:P, :], k_total[0:P, :], res[0:P, t % 2, :],
                                            ALU.add).then_inc(k_added, 1)

            def kv_to_sbuf():
                dve.wait_ge(kv_done, T)
                both = tp[:, :, :].rearrange("p h (b n) -> p (h b) n", n=128)
                for h in range(2):
                    part, cols = slice(h * HEAD, (h + 1) * HEAD), slice(h * HEAD, (h + 1) * HEAD)
                    nc.vector.tensor_copy(kv[part, :, cols], both[part, :, cols]).then_inc(kv_sb, 1)
                    nc.vector.tensor_copy(ksum[part, :, h], aux[part, 0, h:2 * PAIRS:2]).then_inc(kv_sb, 1)

            def attend(t):
                dve.wait_ge(num_done, t + 1)
                chain(nc.vector.tensor_scalar(den[0:P, :], aux[0:P, 1, 0:2 * PAIRS], 1e-6, None, ALU.max))
                chain(nc.vector.reciprocal(den[0:P, :], den[0:P, :]))
                heads = res[0:P, t % 2, :].rearrange("p (h e) -> p h e", e=HEAD)
                chain(nc.vector.scalar_tensor_tensor(
                    heads, product(t % 2).rearrange("p (h e) -> p h e", e=HEAD), float(HEAD) ** -0.5,
                    den[0:P, :].unsqueeze(2).to_broadcast([P, 2 * PAIRS, HEAD]), ALU.mult, ALU.mult))
                dve.wait_ge(x_in[t % 2], io_count(Q_, t))
                nc.vector.tensor_tensor(res[0:P, t % 2, :], res[0:P, t % 2, :], io[0:P, t % 2, :],
                                        ALU.mult).then_inc(num_out, 1)

            def free_res(s, t):
                q = s * T + t
                if s < STORED:
                    if q >= 2:
                        dve.wait_ge(res_st[t % 2], TILE_IN * (q // 2))
                elif s == K_:
                    if t < 2:
                        dve.wait_ge(res_st[t % 2], TILE_IN * STORED * T // 2)
                    else:
                        dve.wait_ge(kv_done, t - 1)
                elif s == Q_:
                    if t < 2:
                        dve.wait_ge(kv_done, T - 1 + t)
                    else:
                        dve.wait_ge(o_turned, t - 1)
                elif t < 2:
                    dve.wait_ge(o_turned, T - 1 + t)
                else:
                    dve.wait_ge(acc_st[t % 2], TILE_IN * (t // 2))

            def finish_tile(s, t):
                free_res(s, t)
                if s in (K_, Q_):
                    elu_plus_one(s, t)
                    return
                dve.wait_ge(kstep, K * (s * T + t + 1))
                if s == O_:
                    dve.wait_ge(x_in[t % 2], io_count(O_, t))
                    nc.vector.tensor_tensor(res[0:P, t % 2, :], product(t % 2), io[0:P, t % 2, :],
                                            ALU.add).then_inc(evac, 1)
                else:
                    dve.wait_ge(bias_in, 16 * s)
                    nc.vector.tensor_tensor(res[0:P, t % 2, :], product(t % 2), bias_sb[0:P, :],
                                            ALU.add).then_inc(evac, 1)

            def tables_of_round(rnd):
                dve.wait_ge(pay_in, (rnd + 1) * (16 * B))
                nc.vector.tensor_tensor(
                    loc_all[:, :, :], pay_all[:, :, :, 1], keybase[:, :].unsqueeze(2).to_broadcast([128, B, CAP]),
                    ALU.subtract).then_inc(table_step, 1)
                dve.wait_ge(table_step, rnd * 2 + 1)
                nc.vector.tensor_scalar(idx_all[:, :, :].bitcast(F32), loc_all[:, :, :], KEY - 0.5, float(NO_ROW),
                                        ALU.is_gt, ALU.mult).then_inc(table_step, 1)
                dve.wait_ge(table_step, rnd * 2 + 2)
                nc.vector.tensor_tensor(idx_all[:, :, :], idx_all[:, :, :].bitcast(F32), pay_all[:, :, :, 0],
                                        ALU.add).then_inc(tables, 1)
                dve.wait_ge(tables, rnd + 1)

            def edges_of_bucket(i, slot, b, first=False):
                if not first:
                    dve.wait_ge(agg, (i - 1) * CAP + AGG_CREDIT)
                    dve.sem_inc(passed_dve, 1)
                nc.vector.tensor_copy(idx[:, slot, 0:CAP].unsqueeze(1),
                                      idx_all[:, bass.ds(b, 1), :]).then_inc(idx_ready, 1)
                nc.vector.tensor_tensor(
                    OH[:, slot, :, :], loc_all[:, bass.ds(b, 1), :].rearrange("p o c -> p (o c)")
                    .unsqueeze(2).to_broadcast([128, CAP, P]),
                    iota[:, :].unsqueeze(1).to_broadcast([128, CAP, P]), ALU.is_equal).then_inc(oh_ready, 1)

            def lo_part(i, slot, c):
                g = (slot * CAP + c) % 2
                dve.wait_ge(g_hi, i * CAP + (c + 1))
                nc.vector.tensor_tensor(Glo[:, g, :], Graw[:, c, :], Ghi[:, g, :].bitcast(F32),
                                        ALU.subtract).then_inc(g_lo, 1)

            def lo_of_means(i, slot):
                dve.wait_ge(mt_hi, i + 1)
                nc.vector.tensor_tensor(as_blocks(mTlo[:, slot, :, :]), tpv,
                                        as_blocks(mThi[:, slot, :, :]).bitcast(F32), ALU.subtract).then_inc(mt_lo, 1)

            def u_add(i, slot, t):
                dve.wait_ge(kstep, i * K + (A_TILES + 1) * K)
                dve.sem_inc(passed_dve, 1)
                u = U[0:P, bass.ds(t, 1), :].rearrange("p o n -> p (o n)")
                nc.vector.tensor_tensor(u, product(slot), u, ALU.add).then_inc(acc_free, 1)

            def split_relation(stage, blocks):
                for k in blocks:
                    split_w(k, stage * K + (k + 1))

            def round_start(i, stage):
                edges_of_bucket(i, 0, 0, first=True)
                edges_of_bucket(i + 1, 1, 1, first=True)
                split_relation(stage, range(K))
                for c in range(CAP):
                    lo_part(i, 0, c)
                lo_part(i + 1, 1, 0)
                lo_part(i + 1, 1, 1)
                lo_of_means(i, 0)

            def bucket_work(i, slot, b, t, early=None, late=None, left=2, first=False):
                if left >= 2:
                    edges_of_bucket(i + 2, slot, b + 2)
                if left >= 1:
                    lo_part(i + 1, 1 - slot, 2)
                    lo_part(i + 1, 1 - slot, 3)
                if early:
                    split_relation(early[0], early[1][0:2])
                if left >= 1:
                    lo_part(i + 1, 1 - slot, 4)
                if early:
                    split_relation(early[0], early[1][2:4])
                if first:
                    dve.wait_ge(u_in, TILE_IN * T)
                if t is not None:
                    u_add(i - 1, 1 - slot, t)
                if left >= 2:
                    lo_part(i + 2, slot, 0)
                    lo_part(i + 2, slot, 1)
                if left >= 1:
                    lo_of_means(i + 1, 1 - slot)
                if late:
                    split_relation(late[0], late[1])

            def relation_work(i, b, stage, first=False, last=False):
                bucket_work(i, 0, b, None if first else T - 1, None if first else (stage, range(4, K)))
                bucket_work(i + 1, 1, b + 1, 0, first=first)
                with dve.Fori(1, T // 2 - 1) as tt:
                    bucket_work(i + tt * 2, 0, b + tt * 2, tt * 2 - 1)
                    bucket_work(i + tt * 2 + 1, 1, b + tt * 2 + 1, tt * 2)
                bucket_work(i + (T - 2), 0, b + (T - 2), T - 3, left=1 if last else 2)
                if last:
                    bucket_work(i + (T - 1), 1, b + (T - 1), T - 2, left=0)
                else:
                    bucket_work(i + (T - 1), 1, b + (T - 1), T - 2, early=(stage + 1, range(0, 2)),
                                late=(stage + 1, range(2, 4)))

            def split_stage(s, blocks):
                for k in blocks:
                    split_w(k, K * s + k + 1)

            chain(nc.vector.memset(cum[0:P, 0:1], 0.0))
            ln_x(0)
            split_stage(0, range(0, 2))
            lo_of_turned(aThi[:, 0, :, :], aTlo[:, 0, :, :], at_hi, 1, at_lo)
            split_stage(0, range(2, K))
            ln_x(1)
            for s in range(STAGES_A):
                for t in range(T):
                    n = (s - Q_) * T + t
                    if s == V_ and t + 2 < T:
                        ln_x(t + 2)
                    if s == V_ and t + 1 < T:
                        lo_of_turned(aThi[:, t + 1, :, :], aTlo[:, t + 1, :, :], at_hi, t + 2, at_lo)
                    if (s, t) == (V_, 1):
                        dve.wait_ge(edges_made, 1)
                    for b in range(*sorted_beside(s, t)):
                        sort_bucket(b)
                    if (s, t) == (OFFSETS_AT[0], OFFSETS_AT[1] - 1):
                        nc.vector.tensor_tensor(per[0:P, :], cum[0:P, 1:B + 1], cum[0:P, 0:B],
                                                ALU.subtract).then_inc(sort_cum, 1)
                    if (s, t) == OFFSETS_AT:
                        sort_offsets()
                    if s == ROOT_ and OFFSETS_AT[1] <= t < T - 1:
                        first = (t - OFFSETS_AT[1]) * PLACES
                        place_buckets(first, min(PLACES, B - first))
                    for n2 in range(*counted_beside(s, t)):
                        count_step(n2)
                    if (s, t) == (Q_, 0):
                        in_degrees()
                        nc.vector.memset(kv[:, :, :], 0.0).then_inc(kv_zero, 1)
                        nc.vector.memset(ksum[:, :, :], 0.0).then_inc(kv_zero, 1)
                        dve.wait_ge(kv_zero, 2)
                        kv_to_sbuf()
                    if (s, t) == (O_, 3):
                        dve.wait_ge(keybase_done, 1)
                        tables_of_round(0)
                    if (s, t) == (O_, T - 3):
                        dve.wait_ge(kstep, (O_ * T + 6) * K)
                        dve.sem_inc(g_lo, LO_CREDIT)
                        edges_of_bucket(0, 0, 0, first=True)
                        edges_of_bucket(1, 1, 1, first=True)
                    if (s, t) == (O_, T - 2):
                        lo_part(0, 0, 0)
                        lo_part(0, 0, 1)
                    if (s, t) == (O_, T - 1):
                        lo_part(0, 0, 2)
                        lo_part(0, 0, 3)
                        split_relation(STAGES_A, range(0, 2))
                        lo_part(0, 0, 4)
                        split_relation(STAGES_A, range(2, 4))
                        lo_part(1, 1, 0)
                        lo_part(1, 1, 1)
                        split_relation(STAGES_A, range(4, 6))
                    if s >= Q_ and 2 <= n < T + 2:
                        lo_of_turned(aThi[:, n - 2, :, :], aTlo[:, n - 2, :, :], ot_hi, n - 1, ot_lo)
                    if t == T - 1 and s + 1 < STAGES_A:
                        split_stage(s + 1, range(0, 5))
                    if s >= Q_ and 1 <= n < T + 1:
                        attend(n - 1)
                    if t == T - 1 and s + 1 < STAGES_A:
                        split_stage(s + 1, range(5, 6))
                    if s != V_:
                        finish_tile(s, t)
                    if s == K_:
                        add_up_k(t)
                    if t == T - 1 and s + 1 < STAGES_A:
                        split_stage(s + 1, range(6, K))
                    if (s, t) == (O_, T - 1):
                        lo_of_means(0, 0)
                        split_relation(STAGES_A, range(6, K))

            dve.wait_ge(meta_done, 2)
            rounds = dve.value_load(meta[0:1, B:B + 1], min_val=1, max_val=MAX_ROUNDS)
            with dve.Fori(0, rounds) as rnd:
                i0 = rnd * B
                stage0 = rnd * R + STAGES_A
                relation_work(i0, 0, stage0, first=True)
                with dve.Fori(1, R - 1) as r:
                    relation_work(i0 + r * T, r * T, stage0 + r)
                relation_work(i0 + (R - 1) * T, (R - 1) * T, stage0 + (R - 1), last=True)
                u_add(i0 + (B - 1), 1, T - 1)
                with dve.If(rnd + 1 < rounds):
                    tables_of_round(rnd + 1)
                    round_start(i0 + B, stage0 + R)
                    dve.sem_inc(passed_dve, 1)
            dve.wait_ge(acc_free, rounds * B + ACC_CREDIT)
            dve.sem_inc(b_out, 1)

            def u_lo(t):
                lo_of_turned(uThi[:, t % 2, :, :], uTlo[:, t % 2, :, :], ut_hi, t + 1, ut_lo)

            def gate(t):
                s = t % 2
                dve.wait_ge(kstep2, K * (t + 1))
                dve.wait_ge(ld_in[s], 3 * TILE_IN * (t // 2 + 1))
                zx, att = ld[s][0:P, 0, :], ld[s][0:P, 2, :]
                nc.vector.tensor_tensor(zx, product(s), zx, ALU.add).then_inc(c_evac, 1)
                dve.wait_ge(less_xn, 2 * (t + 1))
                dve.wait_ge(c_evac, t + 1)
                chain(nc.vector.tensor_tensor(th[0:P, s, :], th[0:P, s, :], zx, ALU.mult))
                nc.vector.tensor_tensor(zx, th[0:P, s, :], att, ALU.add).then_inc(x1_made, 1)

            def ln_x1(t):
                dve.wait_ge(e_in[t % 2], TILE_IN * (t // 2 + 1))
                layer_norm(io[0:P, t % 2, :]).then_inc(ln2_done, 1)

            def x1_lo(t):
                lo_of_turned(aThi[:, t, :, :], aTlo[:, t, :, :], et_hi, t + 1, et_lo)

            def split_w_e(s, blocks=range(K)):
                for k in blocks:
                    dve.wait_ge(w2_hi, K * s + k + 1)
                    nc.vector.tensor_tensor(
                        Wlo[:, k, :], turned_weight[k % 2][:, :, :].rearrange("p h n -> p (h n)"),
                        Whi[:, k, :].bitcast(F32), ALU.subtract).then_inc(w2_lo, 1)

            for k in range(2):
                split_w(k, k + 1, w2_hi, w2_lo)
            u_lo(0)
            for k in range(2, K):
                split_w(k, k + 1, w2_hi, w2_lo)
            for t in range(T - 1):
                u_lo(t + 1)
                if t >= T - 3:
                    ln_x1(t - (T - 3))
                if t < T - 2:
                    gate(t)
            x1_lo(0)
            split_w_e(1, range(0, 4))
            gate(T - 2)
            split_w_e(1, range(4, K))
            gate(T - 1)

            def finish_gate(s, t):
                q, a = s * T + t, res[0:P, t % 2, :]
                if q < 2:
                    dve.wait_ge(x1_st[t], TILE_IN * (T // 2))
                else:
                    dve.wait_ge(e_st[t % 2], TILE_IN * (q // 2))
                dve.wait_ge(bias2_in, 16 * (s + 1))
                dve.wait_ge(kstep2, K * (T + q + 1))
                nc.vector.tensor_tensor(a, product(t % 2), bias_sb[0:P, :], ALU.add).then_inc(e_evac, 1)
                if s == INPUT_:
                    return
                dve.wait_ge(e_act, q + 1)
                dve.wait_ge(e_in[t % 2], TILE_IN * (s * (T // 2) + t // 2 + 1))
                if s == CELL_:
                    nc.vector.tensor_tensor(a, a, io[0:P, t % 2, :], ALU.mult).then_inc(cell, 1)
                else:
                    chain(nc.vector.tensor_tensor(a, a, io[0:P, t % 2, :], ALU.mult))
                    dve.wait_ge(x1s_in[t % 2], TILE_IN * (t // 2 + 1))
                    nc.vector.tensor_tensor(a, a, x1s[0:P, t % 2, :], ALU.add).then_inc(out_made, 1)

            for s in range(STAGES_E):
                for t in range(T):
                    if s == INPUT_ and t + 2 < T:
                        ln_x1(t + 2)
                    if s == INPUT_ and t + 1 < T:
                        x1_lo(t + 1)
                    if t == T - 1 and s + 1 < STAGES_E:
                        split_w_e(s + 2)
                    finish_gate(s, t)

        @block.gpsimd
        def _(pool):
            step = Tally(pool_step)

            def chain(instruction):
                step.inc(instruction)
                step.wait(pool)

            step.inc(nc.gpsimd.memset(ident[:, :], 0.0))
            nc.gpsimd.iota(iota[:, :], pattern=[[1, P]], base=0, channel_multiplier=0,
                           allow_small_or_imprecise_dtypes=True).then_inc(const, 1)
            nc.gpsimd.memset(ones2[:, :], 1.0).then_inc(const, 1)
            step.wait(pool)
            nc.gpsimd.affine_select(out=ident[:, :], in_=ident[:, :], pattern=[[-1, 128]], base=0,
                                    channel_multiplier=1, compare_op=ALU.not_equal, fill=1.0).then_inc(const, 1)

            part = [scan[0:P, i, :] for i in range(2)]
            pool.wait_ge(edges_in, 48)
            chain(nc.gpsimd.tensor_copy(node[0:P, :], raw_edges[0:P, 1, :]))
            step.inc(nc.gpsimd.tensor_scalar(bucket[0:P, :], node[0:P, :], float(P), None, ALU.is_ge))
            for k in range(2, T):
                chain(nc.gpsimd.tensor_scalar(part[k % 2], node[0:P, :], float(P * k), None, ALU.is_ge))
                step.inc(nc.gpsimd.tensor_tensor(bucket[0:P, :], bucket[0:P, :], part[k % 2], ALU.add))
            step.wait(pool)
            chain(nc.gpsimd.tensor_scalar(part[0], bucket[0:P, :], float(-P), None, ALU.mult))
            step.inc(nc.gpsimd.tensor_tensor(node[0:P, :], node[0:P, :], part[0], ALU.add))
            chain(nc.gpsimd.tensor_copy(part[1], raw_edges[0:P, 2, :]))
            chain(nc.gpsimd.tensor_scalar(part[1], part[1], float(T), None, ALU.mult))
            chain(nc.gpsimd.tensor_tensor(bucket[0:P, :], bucket[0:P, :], part[1], ALU.add))
            step.inc(nc.gpsimd.tensor_copy(pay[0:P, :, 0], raw_edges[0:P, 0, :]))
            chain(nc.gpsimd.tensor_scalar(part[0], bucket[0:P, :], float(KEY), None, ALU.mult))
            chain(nc.gpsimd.tensor_tensor(part[0], part[0], node[0:P, :], ALU.add))
            nc.gpsimd.tensor_copy(pay[0:P, :, 1], part[0]).then_inc(edges_made, 1)

            pool.wait_ge(turned, T)
            for i in range(2):
                pool.wait_ge(xn_st[i], TILE_IN * (T // 2))
            nc.gpsimd.memset(ones[:, :], 1.0).then_inc(sort_const, 1)
            nc.gpsimd.memset(before[:, :], 1.0).then_inc(sort_const, 1)
            step.inc(nc.gpsimd.memset(nobody[:, :], 1 << 20))
            pool.wait_ge(sort_const, 2)
            nc.gpsimd.affine_select(out=before[:, :], in_=before[:, :], pattern=[[1, P]], base=0,
                                    channel_multiplier=-1, compare_op=ALU.is_gt, fill=0.0).then_inc(sort_const, 1)
            step.wait(pool)
            pool.dma_start(sorted_d[E:SORTED, :].rearrange("(p n) c -> p (n c)", p=128),
                           nobody[:, :]).then_inc(sent, 16)

            pool.wait_ge(pos_done, 1)
            for j in range(EC):
                pool.indirect_dma_start(sorted_d, bass.IndirectOffsetOnAxis(ap=pos[0:P, j:j + 1], axis=0),
                                        pay[0:P, j, :], None).then_inc(scattered, 16)
            pool.wait_ge(kv_done, T)
            nc.gpsimd.iota(keybase[:, :], pattern=[[KEY, B]], base=0, channel_multiplier=0,
                           allow_small_or_imprecise_dtypes=True).then_inc(keybase_done, 1)

            def load_payloads(rnd):
                with pool.Fori(0, B) as b:
                    first = pool.value_load(meta[0:1, bass.ds(b, 1)], min_val=0, max_val=E) + rnd * SLOTS
                    pool.dma_start(pay_all[:, bass.ds(b, 1), :, :].rearrange("p o c e -> p (o c e)"),
                                   sorted_d[bass.ds(first, SLOTS), :].rearrange("(p c) e -> p (c e)", p=128)
                                   ).then_inc(pay_in, 16)

            pool.wait_ge(scattered, 16 * EC)
            pool.wait_ge(sent, 16)
            pool.wait_ge(meta_done, 2)
            load_payloads(0)

            pool.wait_ge(kstep, (O_ * T + 6) * K)
            nc.gpsimd.memset(Graw[:, :, :], 0.0).then_inc(g_zero, 1)
            pool.wait_ge(g_zero, 1)
            rounds = pool.value_load(meta[0:1, B:B + 1], min_val=1, max_val=MAX_ROUNDS)
            with pool.Fori(0, rounds) as rnd:
                with pool.Fori(0, B // 2) as m:
                    for slot in range(2):
                        i = rnd * B + m * 2 + slot
                        pool.wait_ge(idx_ready, i + 1)
                        for c in range(CAP):
                            pool.wait_ge(g_lo, i * CAP + (c + 1))
                            pool.sem_inc(passed_pool, 1)
                            pool.indirect_dma_start(
                                Graw[:, c, :], None, xn_d, bass.IndirectOffsetOnAxis(ap=idx[:, slot, c:c + 1], axis=0),
                                bounds_check=N - 1, oob_is_err=False).then_inc(raw_in[c], 16)
                with pool.If(rnd + 1 < rounds):
                    pool.wait_ge(tables, rnd + 1)
                    pool.sem_inc(passed_pool, 1)
                    load_payloads(rnd + 1)

            for t in range(T):
                s = t % 2
                xn, att = ld[s][0:P, 1, :], ld[s][0:P, 2, :]
                pool.wait_ge(ld_in[s], 3 * TILE_IN * (t // 2 + 1))
                nc.gpsimd.tensor_tensor(att, att, xn, ALU.add).then_inc(less_xn, 1)
                pool.wait_ge(th_done, t + 1)
                nc.gpsimd.tensor_tensor(th[0:P, s, :], th[0:P, s, :], xn, ALU.subtract).then_inc(less_xn, 1)


def kernel(**inputs):
    import numpy as np
    import concourse.bacc as bacc
    from concourse.bass_utils import run_bass_kernel_spmd

    names = ["x", "src", "dst", "edge_type_8", "L0_gnn_weight", "L0_gnn_root", "L0_gnn_bias", "L0_gnn_w_gate",
             "L0_gnn_b_gate", "L0_mix_Wq", "L0_mix_Wk", "L0_mix_Wv", "L0_mix_Wg", "L0_mix_bg", "L0_mix_Wo",
             "L0_ffn_W_i", "L0_ffn_b_i", "L0_ffn_W_o", "L0_ffn_b_o", "L0_ffn_W_c", "L0_ffn_b_c"]
    nc = bacc.Bacc("TRN2", target_bir_lowering=False, num_devices=1)
    arrays, args = {}, []
    for name in names:
        a = np.ascontiguousarray(inputs[name])
        arrays[f"in_{name}"] = a
        args.append(nc.dram_tensor(f"in_{name}", a.shape, mybir.dt.from_np(a.dtype), kind="ExternalInput").ap())
    args.append(nc.dram_tensor("out_x", [N, D], F32, kind="ExternalOutput").ap())
    build(nc, *args)
    result = run_bass_kernel_spmd(nc, [arrays], core_ids=[0])
    return result.results[0]["out_x"]
```
